# Optimizing a Trainium2 kernel written in Bass

```python
import numpy as np
import jax
import jax.numpy as jnp

def _softmax(x, axis=-1):
    return jax.nn.softmax(x, axis=axis)

def _gelu(x):
    return jax.nn.gelu(x, approximate=True)

def _silu(x):
    return jax.nn.silu(x)

def _sigmoid(x):
    return jax.nn.sigmoid(x)

def _layernorm(x, axis=-1, eps=1e-05):
    m = jnp.mean(x, axis=axis, keepdims=True)
    v = jnp.var(x, axis=axis, keepdims=True)
    return (x - m) / jnp.sqrt(v + eps)

def _scatter_add(tgt, idx, src, axis=0):
    return tgt.at[idx].add(src)

def _segment_sum(src, seg, n):
    return jax.ops.segment_sum(src, seg, n)
kernel_name = 'mk_hybrid_d2_jaxref_r8_0befdd'

def setup_inputs(seed: int=0):
    np.random.seed(seed)
    _w = jnp.asarray

    def _L0_attn_a_setup():
        import jax, jax.numpy as jnp
        import numpy as np
        D_MODEL = 128
        N_HEADS = 16
        LN_EPS = 1e-06

        def _layernorm(t, scale):
            mu = jnp.mean(t, axis=-1, keepdims=True)
            var = jnp.var(t, axis=-1, keepdims=True)
            return (t - mu) * jax.lax.rsqrt(var + LN_EPS) * scale
        key = jax.random.key(seed)
        k1, k2, k3 = jax.random.split(key, 3)
        B, S = (2, 256)
        x = jax.random.normal(k1, (B, S, D_MODEL), dtype=jnp.float32)
        W_qkv = jax.random.normal(k2, (D_MODEL, 3 * D_MODEL), dtype=jnp.float32) / np.sqrt(D_MODEL)
        W_out = jax.random.normal(k3, (D_MODEL, D_MODEL), dtype=jnp.float32) / np.sqrt(D_MODEL)
        q_scale = jnp.ones((D_MODEL,), dtype=jnp.float32)
        k_scale = jnp.ones((D_MODEL,), dtype=jnp.float32)
        return {'x': x, 'W_qkv': W_qkv, 'q_scale': q_scale, 'k_scale': k_scale, 'W_out': W_out}
    _L0_attn_a_in = _L0_attn_a_setup()

    def _L0_attn_b_setup():
        import jax, jax.numpy as jnp
        import numpy as np
        DIM = 128
        H = 16
        D = DIM // H
        HID = H * D
        N, T = (2, 128)
        key = jax.random.key(seed)
        ks = jax.random.split(key, 6)
        x = jax.random.normal(ks[0], (N, T, DIM), dtype=jnp.float32)
        key_w = jax.random.normal(ks[1], (HID, DIM), dtype=jnp.float32) * DIM ** (-0.5)
        key_b = jax.random.uniform(ks[2], (HID,), minval=-4.0, maxval=4.0, dtype=jnp.float32)
        vq_w = jax.random.normal(ks[3], (2 * HID, DIM), dtype=jnp.float32) * DIM ** (-0.5)
        out_w = jax.random.normal(ks[4], (DIM, HID), dtype=jnp.float32) * HID ** (-0.5)
        out_b = jax.random.normal(ks[5], (DIM,), dtype=jnp.float32) * 0.02
        return {'x': x, 'key_w': key_w, 'key_b': key_b, 'vq_w': vq_w, 'out_w': out_w, 'out_b': out_b}
    _L0_attn_b_in = _L0_attn_b_setup()

    def _L0_ffn_setup():
        import jax, jax.numpy as jnp
        import numpy as np
        DIM = 128

        def _reference_tuple_inner(x, W_r, W_k, W_v, mu_r, mu_k):
            B, T, C = x.shape
            x_prev = jnp.concatenate([jnp.zeros((B, 1, C), x.dtype), x[:, :-1, :]], axis=1)
            xr = mu_r * x + (1.0 - mu_r) * x_prev
            xk = mu_k * x + (1.0 - mu_k) * x_prev
            r = jax.nn.sigmoid(jnp.einsum('btc,dc->btd', xr, W_r))
            k = jnp.einsum('btc,dc->btd', xk, W_k)
            k_act = jnp.square(jax.nn.relu(k))
            out = r * jnp.einsum('btc,dc->btd', k_act, W_v)
            new_state = x[:, -1, :]
            return (out, new_state)
        key = jax.random.key(seed)
        ks = jax.random.split(key, 6)
        B, T, C = (8, 256, DIM)
        x = jax.random.normal(ks[0], (B, T, C), dtype=jnp.float32)
        s = 1.0 / np.sqrt(C)
        W_r = jax.random.uniform(ks[1], (C, C), jnp.float32, -s, s)
        W_k = jax.random.uniform(ks[2], (C, C), jnp.float32, -s, s)
        W_v = jax.random.uniform(ks[3], (C, C), jnp.float32, -s, s)
        mu_r = jax.random.uniform(ks[4], (C,), jnp.float32)
        mu_k = jax.random.uniform(ks[5], (C,), jnp.float32)
        return {'x': x, 'W_r': W_r, 'W_k': W_k, 'W_v': W_v, 'mu_r': mu_r, 'mu_k': mu_k}
    _L0_ffn_in = _L0_ffn_setup()

    def _L1_attn_a_setup():
        import jax, jax.numpy as jnp
        import numpy as np
        B, T, D_MODEL, N_HEADS = (2, 256, 128, 16)
        HEAD_DIM = D_MODEL // N_HEADS
        GN_EPS = 1e-05

        def decay_gammas(n_heads):
            h = jnp.arange(n_heads, dtype=jnp.float32)
            return 1.0 - jnp.power(2.0, -5.0 - h * (8.0 / n_heads))
        key = jax.random.key(seed)
        ks = jax.random.split(key, 7)
        w_scale = 0.02
        return {'x': jax.random.normal(ks[0], (B, T, D_MODEL), dtype=jnp.float32), 'Wq': jax.random.normal(ks[1], (D_MODEL, D_MODEL), dtype=jnp.float32) * w_scale, 'Wk': jax.random.normal(ks[2], (D_MODEL, D_MODEL), dtype=jnp.float32) * w_scale, 'Wv': jax.random.normal(ks[3], (D_MODEL, D_MODEL), dtype=jnp.float32) * w_scale, 'Wo': jax.random.normal(ks[4], (D_MODEL, D_MODEL), dtype=jnp.float32) * w_scale, 'gn_w': jnp.ones((D_MODEL,), dtype=jnp.float32), 'gn_b': jnp.zeros((D_MODEL,), dtype=jnp.float32)}
    _L1_attn_a_in = _L1_attn_a_setup()

    def _L1_attn_b_setup():
        import jax, jax.numpy as jnp
        import numpy as np
        E = 128
        H = 16
        D = E // H
        B = 2
        N = 1024
        CHUNK = 128
        LAYER_IDX = 0
        NUM_LAYERS = 12
        EPS = 1e-05

        def _build_slopes(n):

            def po2(m):
                start = 2.0 ** (-2.0 ** (-(np.log2(m) - 3)))
                return [start * start ** i for i in range(m)]
            if np.log2(n).is_integer():
                return po2(n)
            closest = 2 ** int(np.floor(np.log2(n)))
            return po2(closest) + _build_slopes(2 * closest)[0::2][:n - closest]

        def _slope_rate():
            s = np.array(_build_slopes(H), dtype=np.float32)
            s = s * (1.0 - LAYER_IDX / (NUM_LAYERS - 1) + 1e-05)
            return jnp.asarray(s)

        def lightning_attn(q, k, v, s):
            b, h, n, d = q.shape
            nc = n // CHUNK
            idx = jnp.arange(CHUNK, dtype=q.dtype)
            diff = idx[:, None] - idx[None, :]
            mask = jnp.where(diff >= 0, jnp.exp(-s[:, None, None] * diff), 0.0)
            lam_q = jnp.exp(-s[:, None] * (idx + 1.0))
            lam_k = jnp.exp(-s[:, None] * (CHUNK - 1.0 - idx))
            lam_c = jnp.exp(-s * CHUNK)

            def to_chunks(t):
                return t.reshape(b, h, nc, CHUNK, d).transpose(2, 0, 1, 3, 4)
            qc, kc, vc = (to_chunks(q), to_chunks(k), to_chunks(v))

            def step(kv, xs):
                qi, ki, vi = xs
                scores = jnp.einsum('bhid,bhjd->bhij', qi, ki) * mask
                o = jnp.einsum('bhij,bhjd->bhid', scores, vi)
                o = o + lam_q[:, :, None] * jnp.einsum('bhid,bhde->bhie', qi, kv)
                kv = lam_c[:, None, None] * kv + jnp.einsum('bhid,bhie->bhde', ki * lam_k[:, :, None], vi)
                return (kv, o)
            kv0 = jnp.zeros((b, h, d, d), q.dtype)
            _, o = jax.lax.scan(step, kv0, (qc, kc, vc))
            return o.transpose(1, 2, 0, 3, 4).reshape(b, h, n, d)
        key = jax.random.key(seed)
        ks = jax.random.split(key, 8)
        sc = 1.0 / np.sqrt(E)
        return {'x': jax.random.normal(ks[0], (B, N, E), jnp.float32), 'Wq': jax.random.normal(ks[1], (E, E), jnp.float32) * sc, 'Wk': jax.random.normal(ks[2], (E, E), jnp.float32) * sc, 'Wv': jax.random.normal(ks[3], (E, E), jnp.float32) * sc, 'Wo': jax.random.normal(ks[4], (E, E), jnp.float32) * sc, 'gamma': jnp.ones((E,), jnp.float32), 'beta': jnp.zeros((E,), jnp.float32), 'Wg1': jax.random.normal(ks[5], (E, D), jnp.float32) * sc, 'Wg2': jax.random.normal(ks[6], (D, E), jnp.float32) * (1.0 / np.sqrt(D))}
    _L1_attn_b_in = _L1_attn_b_setup()

    def _L1_ffn_setup():
        import jax, jax.numpy as jnp
        import numpy as np
        E = 8
        JITTER = 0.01

        def _sparse_mixer_routing(logits):
            top_vals, top_idx = jax.lax.top_k(logits, 2)
            eidx = jnp.arange(logits.shape[-1])

            def _multiplier(thr, base_logits, idx):
                factor = jnp.maximum(jnp.abs(logits), thr)
                mask = (thr - logits) / factor > 2.0 * JITTER
                probs = jax.nn.softmax(jnp.where(mask, -jnp.inf, base_logits), axis=-1)
                return jnp.take_along_axis(probs, idx, axis=-1)
            mult1 = _multiplier(top_vals[:, :1], logits, top_idx[:, :1])
            scat = jnp.where(eidx[None, :] == top_idx[:, :1], -jnp.inf, logits)
            mult2 = _multiplier(top_vals[:, 1:2], scat, top_idx[:, 1:2])
            return (jnp.concatenate([mult1, mult2], axis=-1), top_idx)
        key = jax.random.key(seed)
        ks = jax.random.split(key, 5)
        H, F = (128, 512)
        scale = 0.02
        return {'hidden_states': jax.random.normal(ks[0], (1, 256, H), jnp.float32), 'gate_w': jax.random.normal(ks[1], (H, E), jnp.float32) * scale, 'w1': jax.random.normal(ks[2], (E, H, F), jnp.float32) * scale, 'w2': jax.random.normal(ks[3], (E, F, H), jnp.float32) * scale, 'w3': jax.random.normal(ks[4], (E, H, F), jnp.float32) * scale}
    _L1_ffn_in = _L1_ffn_setup()
    _d = {'L0_attn_a_x': _L0_attn_a_in['x'], 'L0_attn_a_W_qkv': _L0_attn_a_in['W_qkv'], 'L0_attn_a_q_scale': _L0_attn_a_in['q_scale'], 'L0_attn_a_k_scale': _L0_attn_a_in['k_scale'], 'L0_attn_a_W_out': _L0_attn_a_in['W_out'], 'L0_attn_b_key_w': _L0_attn_b_in['key_w'], 'L0_attn_b_key_b': _L0_attn_b_in['key_b'], 'L0_attn_b_vq_w': _L0_attn_b_in['vq_w'], 'L0_attn_b_out_w': _L0_attn_b_in['out_w'], 'L0_attn_b_out_b': _L0_attn_b_in['out_b'], 'L0_ffn_W_r': _L0_ffn_in['W_r'], 'L0_ffn_W_k': _L0_ffn_in['W_k'], 'L0_ffn_W_v': _L0_ffn_in['W_v'], 'L0_ffn_mu_r': _L0_ffn_in['mu_r'], 'L0_ffn_mu_k': _L0_ffn_in['mu_k'], 'L1_attn_a_Wq': _L1_attn_a_in['Wq'], 'L1_attn_a_Wk': _L1_attn_a_in['Wk'], 'L1_attn_a_Wv': _L1_attn_a_in['Wv'], 'L1_attn_a_Wo': _L1_attn_a_in['Wo'], 'L1_attn_a_gn_w': _L1_attn_a_in['gn_w'], 'L1_attn_a_gn_b': _L1_attn_a_in['gn_b'], 'L1_attn_b_Wq': _L1_attn_b_in['Wq'], 'L1_attn_b_Wk': _L1_attn_b_in['Wk'], 'L1_attn_b_Wv': _L1_attn_b_in['Wv'], 'L1_attn_b_Wo': _L1_attn_b_in['Wo'], 'L1_attn_b_gamma': _L1_attn_b_in['gamma'], 'L1_attn_b_beta': _L1_attn_b_in['beta'], 'L1_attn_b_Wg1': _L1_attn_b_in['Wg1'], 'L1_attn_b_Wg2': _L1_attn_b_in['Wg2'], 'L1_ffn_gate_w': _L1_ffn_in['gate_w'], 'L1_ffn_w1': _L1_ffn_in['w1'], 'L1_ffn_w2': _L1_ffn_in['w2'], 'L1_ffn_w3': _L1_ffn_in['w3']}
    _x0 = _d['L0_attn_a_x']
    _d['L0_attn_a_x'] = jax.random.normal(jax.random.fold_in(jax.random.key(seed), 1), (1, 2048, 128), dtype=_x0.dtype)
    del _x0
    return _d

def reference(L0_attn_a_x, L0_attn_a_W_qkv, L0_attn_a_q_scale, L0_attn_a_k_scale, L0_attn_a_W_out, L0_attn_b_key_w, L0_attn_b_key_b, L0_attn_b_vq_w, L0_attn_b_out_w, L0_attn_b_out_b, L0_ffn_W_r, L0_ffn_W_k, L0_ffn_W_v, L0_ffn_mu_r, L0_ffn_mu_k, L1_attn_a_Wq, L1_attn_a_Wk, L1_attn_a_Wv, L1_attn_a_Wo, L1_attn_a_gn_w, L1_attn_a_gn_b, L1_attn_b_Wq, L1_attn_b_Wk, L1_attn_b_Wv, L1_attn_b_Wo, L1_attn_b_gamma, L1_attn_b_beta, L1_attn_b_Wg1, L1_attn_b_Wg2, L1_ffn_gate_w, L1_ffn_w1, L1_ffn_w2, L1_ffn_w3):

    def _L0_attn_a_ref(x, W_qkv, q_scale, k_scale, W_out):
        import jax, jax.numpy as jnp
        import numpy as np
        D_MODEL = 128
        N_HEADS = 16
        LN_EPS = 1e-06

        def _layernorm(t, scale):
            mu = jnp.mean(t, axis=-1, keepdims=True)
            var = jnp.var(t, axis=-1, keepdims=True)
            return (t - mu) * jax.lax.rsqrt(var + LN_EPS) * scale
        B, S, D = x.shape
        H = N_HEADS
        Hd = D // H
        qkv = jnp.einsum('bsd,de->bse', x, W_qkv)
        q, k, v = jnp.split(qkv, 3, axis=-1)
        q = _layernorm(q, q_scale)
        k = _layernorm(k, k_scale)
        q = q.reshape(B, S, H, Hd)
        k = k.reshape(B, S, H, Hd)
        v = v.reshape(B, S, H, Hd)
        scores = jnp.einsum('bshd,bthd->bhst', q / jnp.sqrt(Hd).astype(q.dtype), k)
        future = jnp.triu(jnp.ones((S, S), dtype=bool), 1)
        scores = jnp.where(future[None, None, :, :], jnp.finfo(scores.dtype).min, scores)
        attn = jax.nn.softmax(scores, axis=-1)
        ctx = jnp.einsum('bhst,bthd->bshd', attn, v)
        out = jnp.einsum('bsd,de->bse', ctx.reshape(B, S, D), W_out)
        return out

    def _L0_attn_b_ref(x, key_w, key_b, vq_w, out_w, out_b):
        import jax, jax.numpy as jnp
        import numpy as np
        DIM = 128
        H = 16
        D = DIM // H
        HID = H * D
        N, T = (2, 128)
        n, t, dim = x.shape
        vq = x @ vq_w.T
        v, q = jnp.split(vq, 2, axis=-1)
        k = jax.nn.sigmoid(x @ key_w.T + key_b)
        k = k.reshape(n, t, H, D)
        v = v.reshape(n, t, H, D)
        upd = (1.0 - k)[..., :, None] * v[..., None, :]
        decay = k[..., :, None]

        def combine(c1, c2):
            a1, b1 = c1
            a2, b2 = c2
            return (a1 * a2, b1 * a2 + b2)
        _, kv = jax.lax.associative_scan(combine, (decay, upd), axis=1)
        qh = q.reshape(n, t, H, D)
        h = jnp.einsum('nthd,nthde->nthe', qh, kv).reshape(n, t, HID)
        return h @ out_w.T + out_b

    def _L0_ffn_ref(x, W_r, W_k, W_v, mu_r, mu_k):
        import jax, jax.numpy as jnp
        import numpy as np
        DIM = 128

        def _reference_tuple_inner(x, W_r, W_k, W_v, mu_r, mu_k):
            B, T, C = x.shape
            x_prev = jnp.concatenate([jnp.zeros((B, 1, C), x.dtype), x[:, :-1, :]], axis=1)
            xr = mu_r * x + (1.0 - mu_r) * x_prev
            xk = mu_k * x + (1.0 - mu_k) * x_prev
            r = jax.nn.sigmoid(jnp.einsum('btc,dc->btd', xr, W_r))
            k = jnp.einsum('btc,dc->btd', xk, W_k)
            k_act = jnp.square(jax.nn.relu(k))
            out = r * jnp.einsum('btc,dc->btd', k_act, W_v)
            new_state = x[:, -1, :]
            return (out, new_state)
        return _reference_tuple_inner(x, W_r, W_k, W_v, mu_r, mu_k)[0]

    def _L1_attn_a_ref(x, Wq, Wk, Wv, Wo, gn_w, gn_b):
        import jax, jax.numpy as jnp
        import numpy as np
        B, T, D_MODEL, N_HEADS = (2, 256, 128, 16)
        HEAD_DIM = D_MODEL // N_HEADS
        GN_EPS = 1e-05

        def decay_gammas(n_heads):
            h = jnp.arange(n_heads, dtype=jnp.float32)
            return 1.0 - jnp.power(2.0, -5.0 - h * (8.0 / n_heads))
        Bx, Tx, C = x.shape
        H, D = (N_HEADS, C // N_HEADS)
        gammas = decay_gammas(H)

        def split_heads(y):
            return y.reshape(Bx, Tx, H, D).transpose(0, 2, 1, 3)
        Q = split_heads(x @ Wq.T)
        K = split_heads(x @ Wk.T)
        V = split_heads(x @ Wv.T)
        idx = jnp.arange(Tx, dtype=jnp.float32)
        diff = idx[:, None] - idx[None, :]
        mask = jnp.where(diff >= 0, gammas[:, None, None] ** jnp.maximum(diff, 0.0), 0.0)
        scores = jnp.einsum('bhtd,bhsd->bhts', Q, K) / jnp.sqrt(jnp.float32(D))
        scores = scores * mask[None]
        out = jnp.einsum('bhts,bhsd->bhtd', scores, V)
        y = out.transpose(0, 2, 1, 3).reshape(Bx, Tx, C)
        z = y.transpose(0, 2, 1).reshape(Bx, H, D, Tx)
        mu = z.mean(axis=(2, 3), keepdims=True)
        var = z.var(axis=(2, 3), keepdims=True)
        zn = (z - mu) * jax.lax.rsqrt(var + GN_EPS)
        zn = zn * gn_w.reshape(1, H, D, 1) + gn_b.reshape(1, H, D, 1)
        y = zn.reshape(Bx, C, Tx).transpose(0, 2, 1)
        return y @ Wo.T

    def _L1_attn_b_ref(x, Wq, Wk, Wv, Wo, gamma, beta, Wg1, Wg2):
        import jax, jax.numpy as jnp
        import numpy as np
        E = 128
        H = 16
        D = E // H
        B = 2
        N = 1024
        CHUNK = 128
        LAYER_IDX = 0
        NUM_LAYERS = 12
        EPS = 1e-05

        def _build_slopes(n):

            def po2(m):
                start = 2.0 ** (-2.0 ** (-(np.log2(m) - 3)))
                return [start * start ** i for i in range(m)]
            if np.log2(n).is_integer():
                return po2(n)
            closest = 2 ** int(np.floor(np.log2(n)))
            return po2(closest) + _build_slopes(2 * closest)[0::2][:n - closest]

        def _slope_rate():
            s = np.array(_build_slopes(H), dtype=np.float32)
            s = s * (1.0 - LAYER_IDX / (NUM_LAYERS - 1) + 1e-05)
            return jnp.asarray(s)

        def lightning_attn(q, k, v, s):
            b, h, n, d = q.shape
            nc = n // CHUNK
            idx = jnp.arange(CHUNK, dtype=q.dtype)
            diff = idx[:, None] - idx[None, :]
            mask = jnp.where(diff >= 0, jnp.exp(-s[:, None, None] * diff), 0.0)
            lam_q = jnp.exp(-s[:, None] * (idx + 1.0))
            lam_k = jnp.exp(-s[:, None] * (CHUNK - 1.0 - idx))
            lam_c = jnp.exp(-s * CHUNK)

            def to_chunks(t):
                return t.reshape(b, h, nc, CHUNK, d).transpose(2, 0, 1, 3, 4)
            qc, kc, vc = (to_chunks(q), to_chunks(k), to_chunks(v))

            def step(kv, xs):
                qi, ki, vi = xs
                scores = jnp.einsum('bhid,bhjd->bhij', qi, ki) * mask
                o = jnp.einsum('bhij,bhjd->bhid', scores, vi)
                o = o + lam_q[:, :, None] * jnp.einsum('bhid,bhde->bhie', qi, kv)
                kv = lam_c[:, None, None] * kv + jnp.einsum('bhid,bhie->bhde', ki * lam_k[:, :, None], vi)
                return (kv, o)
            kv0 = jnp.zeros((b, h, d, d), q.dtype)
            _, o = jax.lax.scan(step, kv0, (qc, kc, vc))
            return o.transpose(1, 2, 0, 3, 4).reshape(b, h, n, d)
        b, n, e = x.shape
        s = _slope_rate()
        silu = jax.nn.silu
        q = silu(x @ Wq)
        k = silu(x @ Wk)
        v = silu(x @ Wv)
        split = lambda t: t.reshape(b, n, H, D).transpose(0, 2, 1, 3)
        o = lightning_attn(split(q), split(k), split(v), s)
        o = o.transpose(0, 2, 1, 3).reshape(b, n, e)
        mu = jnp.mean(o, axis=-1, keepdims=True)
        var = jnp.var(o, axis=-1, keepdims=True)
        o = (o - mu) * jax.lax.rsqrt(var + EPS) * gamma + beta
        gate = jax.nn.sigmoid(x @ Wg1 @ Wg2)
        return o * gate @ Wo

    def _L1_ffn_ref(hidden_states, gate_w, w1, w2, w3):
        import jax, jax.numpy as jnp
        import numpy as np
        E = 8
        JITTER = 0.01

        def _sparse_mixer_routing(logits):
            top_vals, top_idx = jax.lax.top_k(logits, 2)
            eidx = jnp.arange(logits.shape[-1])

            def _multiplier(thr, base_logits, idx):
                factor = jnp.maximum(jnp.abs(logits), thr)
                mask = (thr - logits) / factor > 2.0 * JITTER
                probs = jax.nn.softmax(jnp.where(mask, -jnp.inf, base_logits), axis=-1)
                return jnp.take_along_axis(probs, idx, axis=-1)
            mult1 = _multiplier(top_vals[:, :1], logits, top_idx[:, :1])
            scat = jnp.where(eidx[None, :] == top_idx[:, :1], -jnp.inf, logits)
            mult2 = _multiplier(top_vals[:, 1:2], scat, top_idx[:, 1:2])
            return (jnp.concatenate([mult1, mult2], axis=-1), top_idx)
        B, S, H = hidden_states.shape
        x = hidden_states.reshape(-1, H)
        logits = x @ gate_w
        mult, sel = _sparse_mixer_routing(logits)
        w = jnp.sum(mult[:, :, None] * (sel[:, :, None] == jnp.arange(E)[None, None, :]), axis=1)
        h = jax.nn.silu(jnp.einsum('th,ehf->etf', x, w1)) * jnp.einsum('th,ehf->etf', x, w3)
        out = jnp.einsum('etf,efh,te->th', h, w2, w)
        return out.reshape(B, S, H)
    x = L0_attn_a_x
    x = x + _L0_attn_a_ref(_layernorm(x, axis=-1), L0_attn_a_W_qkv, L0_attn_a_q_scale, L0_attn_a_k_scale, L0_attn_a_W_out)
    x = x + _L0_ffn_ref(_layernorm(x, axis=-1), L0_ffn_W_r, L0_ffn_W_k, L0_ffn_W_v, L0_ffn_mu_r, L0_ffn_mu_k)
    x = x + _L0_attn_b_ref(_layernorm(x, axis=-1), L0_attn_b_key_w, L0_attn_b_key_b, L0_attn_b_vq_w, L0_attn_b_out_w, L0_attn_b_out_b)
    x = x + _L0_ffn_ref(_layernorm(x, axis=-1), L0_ffn_W_r, L0_ffn_W_k, L0_ffn_W_v, L0_ffn_mu_r, L0_ffn_mu_k)
    x = x + _L1_attn_a_ref(_layernorm(x, axis=-1), L1_attn_a_Wq, L1_attn_a_Wk, L1_attn_a_Wv, L1_attn_a_Wo, L1_attn_a_gn_w, L1_attn_a_gn_b)
    x = x + _L1_ffn_ref(_layernorm(x, axis=-1), L1_ffn_gate_w, L1_ffn_w1, L1_ffn_w2, L1_ffn_w3)
    x = x + _L1_attn_b_ref(_layernorm(x, axis=-1), L1_attn_b_Wq, L1_attn_b_Wk, L1_attn_b_Wv, L1_attn_b_Wo, L1_attn_b_gamma, L1_attn_b_beta, L1_attn_b_Wg1, L1_attn_b_Wg2)
    x = x + _L1_ffn_ref(_layernorm(x, axis=-1), L1_ffn_gate_w, L1_ffn_w1, L1_ffn_w2, L1_ffn_w3)
    return x

_drawn_inputs = setup_inputs


def setup_inputs(seed=0):
    import zlib

    import numpy as np

    out = dict(_drawn_inputs(seed))
    spreads = {'L0_attn_a_q_scale': (1.0, 0.2),
     'L0_attn_a_k_scale': (1.0, 0.2),
     'L1_attn_a_gn_w': (1.0, 0.6),
     'L1_attn_a_gn_b': (0.0, 0.564),
     'L1_attn_b_gamma': (1.0, 0.2),
     'L1_attn_b_beta': (0.0, 0.328)}
    factors = {'L0_attn_b_out_b': 4.091,
     'L0_ffn_mu_r': 4.107,
     'L1_ffn_gate_w': 4.679,
     'L1_ffn_w1': 4.072,
     'L1_ffn_w2': 4.032,
     'L1_ffn_w3': 4.04}
    for name, (base, spread) in spreads.items():
        noise = np.random.default_rng([zlib.crc32(name.encode()), seed]).standard_normal(out[name].shape)
        drawn = base * np.exp(spread * noise) if base else spread * noise
        out[name] = jnp.asarray(drawn.astype(out[name].dtype))
    for name, factor in factors.items():
        out[name] = (out[name] * factor).astype(out[name].dtype)
    return out
```

```python
import concourse.bass as bass
from concourse import mybir
from contextlib import ExitStack

FP32 = mybir.dt.float32
BF16 = mybir.dt.bfloat16
ACT = mybir.ActivationFunctionType
ALU = mybir.AluOpType
AX = mybir.AxisListType

T = 2048
D = 128
H = 16
HD = D // H
P = 128
NT = T // P
CH = 512
NC = T // CH
TPC = CH // P
E = 8
F = 512
NF = F // P
PARTS = 3
KROWS = PARTS * PARTS * HD
GH = 4
NG = H // GH
NEG = -1.0e30

C_IDENT = 0
C_PICK = C_IDENT + P
C_HEAD = C_PICK + HD * P
C_RET = C_HEAD + P
C_LT = C_RET + 1
C_RANK = C_LT + 1
C_QMASK = C_RANK + E
C_KMASK = C_QMASK + P
C_F32 = C_KMASK + P

WEIGHTS = [("qkv", 3 * D), ("wout", D), ("wr", D), ("wk", D), ("wv", D), ("hk", D), ("hv", D), ("hq", D), ("ho", D),
           ("rq", D), ("rk", D), ("rv", D), ("ro", D), ("lq", D), ("lk", D), ("lv", D), ("lo", D), ("lg1", HD),
           ("gate", E)]
VECTORS = ["q_scale", "k_scale", "key_b", "mu_r", "mu_k", "gn_w", "gn_b", "gamma", "beta"]
LOADS = 4 + len(WEIGHTS) + len(VECTORS)


def build(nc, io):
    ctx = ExitStack()
    with ctx:
        def sb(name, shape, dt=FP32):
            return ctx.enter_context(nc.sbuf_tensor(name, shape, dt))

        stage_sems = []

        def sem(name):
            stage_sems.append(nc.alloc_semaphore(name=name))
            return stage_sems[-1]

        def end_stage():
            with nc.Block() as block:
                @block.gpsimd
                def _(pool):
                    nc.clear_and_free_semaphores(stage_sems)
            stage_sems.clear()

        x = sb("x", [P, NT, D])
        xn = sb("xn", [P, NT, D])
        xt = sb("xt", [P, 1 + T])
        xT = xt[:, 1:1 + T]
        cst = sb("cst", [P, C_F32])
        cstb = sb("cstb", [P, 3 * P], BF16)
        w = {}
        for name, width in WEIGHTS:
            w[name] = sb("w_" + name, [P, width])
        w["lg2"] = sb("w_lg2", [HD, D])
        vec = sb("vec", [P, len(VECTORS)])
        col = {name: vec[:, i:i + 1] for i, name in enumerate(VECTORS)}
        out_bias = sb("out_bias", [P, D])
        w1 = sb("w1", [P, E, F])
        w3 = sb("w3", [P, E, F])
        w2 = sb("w2", [P, E, NF, D])
        stats = sb("stats", [P, 2 * NT, 6])
        small = sb("small", [P, 10, 2 * NT])
        neghalf = sb("neghalf", [P, NT])
        arena = sb("arena", [P, 24 * 1024 + 8])
        ps = ctx.enter_context(nc.psum_tensor("ps", [P, 8, CH], FP32))

        ident = cst[:, C_IDENT:C_IDENT + P]
        pick = cst[:, C_PICK:C_PICK + HD * P].rearrange("p (e m) -> p e m", e=HD)
        head_mean = cst[:, C_HEAD:C_HEAD + P]
        rank = cst[:, C_RANK:C_RANK + E]
        identb, qmask, kmask = (cstb[:, i * P:(i + 1) * P] for i in range(3))

        q_parts = nc.dram_tensor("q_parts", [H, PARTS, HD, T], BF16, kind="Internal").ap()
        k_parts = nc.dram_tensor("k_parts", [H, 2 * PARTS - 1, HD, T], BF16, kind="Internal").ap()

        loaded = ctx.enter_context(nc.semaphore("loaded"))
        moe_loaded = ctx.enter_context(nc.semaphore("moe_loaded"))

        class Chain:

            def __init__(self, eng, s):
                self.eng, self.s, self.n = eng, s, 0

            def __call__(self, ins):
                self.n += 1
                ins.then_inc(self.s, 1)
                self.eng.wait_ge(self.s, self.n)

        class Norm:

            def __init__(self, name, src, dst, n, eps, banks=(0, 1)):
                self.src, self.dst, self.n, self.eps, self.banks = src, dst, n, eps, banks
                self.chain = sem(name + "_chain")
                self.var_ready = sem(name + "_var_ready")
                self.rstd_ready = sem(name + "_rstd_ready")
                self.normed = sem(name + "_normed")
                self.turned = sem(name + "_turned")
                self.out = sem(name + "_out")

            def vector(self, dve):
                n = self.n
                link = Chain(dve, self.chain)
                st = stats[:, 0:n, :]
                for t in range(n):
                    ins = nc.vector.bn_stats(st[:, t, :], self.src[:, t, :])
                link(ins)
                me, se, mo, so = st[:, :, 1], st[:, :, 2], st[:, :, 4], st[:, :, 5]
                mean, diff, m2, sq, var = (small[:, i, 0:n] for i in range(5))
                link(nc.vector.tensor_tensor(mean, me, mo, ALU.add))
                link(nc.vector.tensor_tensor(diff, me, mo, ALU.subtract))
                link(nc.vector.tensor_tensor(m2, se, so, ALU.add))
                link(nc.vector.tensor_tensor(sq, diff, diff, ALU.mult))
                link(nc.vector.tensor_scalar(mean, mean, 0.5, None, ALU.mult))
                link(nc.vector.tensor_scalar(m2, m2, 1.0 / D, self.eps, ALU.mult, ALU.add))
                nc.vector.scalar_tensor_tensor(out=var, in0=sq, scalar=0.25, in1=m2, op0=ALU.mult,
                                               op1=ALU.add).then_inc(self.var_ready, 1)
                for g in range(n // 4):
                    dve.wait_ge(self.rstd_ready, g + 1)
                    for t in range(4 * g, 4 * g + 4):
                        ins = nc.vector.tensor_scalar(self.dst[:, t, :], self.src[:, t, :], small[:, 0, t:t + 1],
                                                      small[:, 5, t:t + 1], ALU.subtract, ALU.mult)
                    ins.then_inc(self.normed, 1)

            def gpsimd(self, pool):
                pool.wait_ge(self.var_ready, 1)
                for g in range(self.n // 4):
                    nc.gpsimd.tensor_tensor(small[:, 5, 4 * g:4 * g + 4], small[:, 4, 4 * g:4 * g + 4],
                                            neghalf[:, 0:4], ALU.pow).then_inc(self.rstd_ready, 1)

            def tensor(self, pe):
                for g in range(self.n // 4):
                    pe.wait_ge(self.normed, g + 1)
                    if g >= 2:
                        pe.wait_ge(self.out, g - 1)
                    for i in range(4):
                        ins = nc.tensor.transpose(ps[:, self.banks[g % 2], i * P:(i + 1) * P],
                                                  self.dst[:, 4 * g + i, :], ident)
                    ins.then_inc(self.turned, 1)

            def scalar(self, act):
                for g in range(self.n // 4):
                    act.wait_ge(self.turned, g + 1)
                    nc.scalar.copy(xT[:, g * CH:(g + 1) * CH], ps[:, self.banks[g % 2], :]).then_inc(self.out, 1)

        with nc.Block() as block:
            @block.sync
            def _(sp):
                sp.dma_start(x[:], io["x"].rearrange("a (t p) d -> p (a t) d", p=P)).then_inc(loaded, 16)
                sp.dma_start(cst[:], io["cst"]).then_inc(loaded, 16)
                for name, _ in WEIGHTS:
                    sp.dma_start(w[name][:], io[name]).then_inc(loaded, 16)
                sp.dma_start(w["lg2"][:], io["lg2"]).then_inc(loaded, 16)
                sp.dma_start(out_bias[:], io["out_b"].rearrange("(a n) -> a n", a=1).to_broadcast([P, D])).then_inc(loaded, 16)
                for i, name in enumerate(VECTORS):
                    sp.dma_start(vec[:, i:i + 1], io[name].rearrange("(n a) -> n a", a=1)).then_inc(loaded, 16)
                sp.wait_ge(loaded, 16 * LOADS)

            @block.vector
            def _(dve):
                nc.vector.memset(xt[:, 0:1], 0.0)
                nc.vector.memset(neghalf[:], -0.5)
                dve.wait_ge(loaded, 16 * LOADS)
                nc.vector.tensor_copy(identb, ident)
                nc.vector.tensor_copy(cstb[:, P:3 * P], cst[:, C_QMASK:C_QMASK + 2 * P])

        def load_experts():
            with nc.Block() as block:
                @block.sync
                def _(sp):
                    sp.dma_start(w1[:], io["w1"].rearrange("e h f -> h e f")).then_inc(moe_loaded, 16)
                    sp.dma_start(w3[:], io["w3"].rearrange("e h f -> h e f")).then_inc(moe_loaded, 16)
                    sp.dma_start(w2[:], io["w2"].rearrange("e (t f) h -> f e t h", f=P)).then_inc(moe_loaded, 16)


        def softmax_attention():
            QK = GH * T // 2
            Qs = [arena[:, 2 * b * QK:(2 * b + 1) * QK].bitcast(BF16).rearrange("p (j t) -> p j t", j=GH) for b in (0, 1)]
            Ks = [arena[:, (2 * b + 1) * QK:(2 * b + 2) * QK].bitcast(BF16).rearrange("p (j t) -> p j t", j=GH) for b in (0, 1)]
            at = 4 * QK
            probs = arena[:, at:at + 2 * GH * CH].rearrange("p (b j q) -> p b j q", b=2, j=GH)
            at += 2 * GH * CH
            qk = arena[:, 0:2 * NT * D].rearrange("p (n d) -> p n d", d=D)
            qkn = arena[:, 2 * NT * D:4 * NT * D].rearrange("p (n d) -> p n d", d=D)
            feat = arena[:, 4 * NT * D:6 * NT * D].rearrange("p (s t) -> p s t", s=2)
            parts = arena[:, 6 * NT * D:9 * NT * D].bitcast(BF16).rearrange("p (s r t) -> p s r t", s=2, r=PARTS)
            rest = arena[:, 9 * NT * D:9 * NT * D + 2 * T].rearrange("p (s t) -> p s t", s=2)
            ctxt = xn
            with ExitStack() as mem:
                def own(name, shape, dt=FP32):
                    return mem.enter_context(nc.sbuf_tensor(name, shape, dt))

                spare = w1[:].rearrange("p e f -> p (e f)")
                nv = NT * H * (HD + 1)
                vaug = spare[:, 0:nv].rearrange("p (t h d) -> p t h d", t=NT, h=H)
                osb = spare[:, nv:nv + 2 * CH].rearrange("p (b q) -> p b q", b=2)
                vg = w3[:].rearrange("p e f -> p (e f)").rearrange("p (b t j m) -> p b t j m", b=2, t=NT, j=GH)
                qscaled = own("qscaled", [P, 1])
                rec = own("rec", [P, 2, TPC, GH])
                mpart = own("mpart", [P, GH, TPC, NC])
                negmax = own("negmax", [P, 2, GH, TPC])
                mwide = own("mwide", [P, GH, P // GH], BF16)
                mparts = mwide[:, :, 0:PARTS * TPC].rearrange("p j (r t) -> p j r t", r=PARTS)
                ones = own("ones", [PARTS, T], BF16)
                mrow = own("mrow", [P, P], BF16)

                norm = Norm("a0", x, xn, NT, 1e-5)
                qkn_norm = Norm("a1", qk, qkn, 2 * NT, 1e-6, banks=(6, 7))
                projected = sem("a_projected")
                split_out = sem("a_split_out")
                v_out = sem("a_v_out")
                scaled = sem("a_scaled")
                with nc.Block() as block:
                    @block.vector
                    def _(dve):
                        dve.wait_ge(loaded, 16 * LOADS)
                        nc.vector.tensor_scalar(qscaled[:], col["q_scale"], float(HD) ** -0.5, None, ALU.mult).then_inc(scaled, 1)
                        norm.vector(dve)
                        for t in range(NT):
                            dve.wait_ge(projected, t + 1)
                            dve.wait_ge(split_out, t + 1)
                            nc.vector.tensor_copy(vaug[:, t, :, 0:HD],
                                                  ps[:, 2 + t % 4, 2 * D:3 * D].rearrange("p (h d) -> p h d", h=H)).then_inc(v_out, 1)

                    @block.gpsimd
                    def _(pool):
                        nc.gpsimd.memset(vaug[:, :, :, HD:HD + 1], 1.0)
                        norm.gpsimd(pool)

                    @block.tensor
                    def _(pe):
                        pe.wait_ge(loaded, 16 * LOADS)
                        norm.tensor(pe)
                        for t in range(NT):
                            pe.wait_ge(norm.out, t // TPC + 1)
                            if t >= 4:
                                pe.wait_ge(v_out, t - 3)
                            nc.tensor.matmul(ps[:, 2 + t % 4, 0:3 * D], xT[:, t * P:(t + 1) * P], w["qkv"][:],
                                             start=True, stop=True).then_inc(projected, 1)

                    @block.scalar
                    def _(act):
                        norm.scalar(act)
                        for t in range(NT):
                            act.wait_ge(projected, t + 1)
                            nc.scalar.copy(qk.rearrange("p (s t) d -> p s t d", s=2)[:, :, t, :],
                                           ps[:, 2 + t % 4, 0:2 * D].rearrange("p (s d) -> p s d", s=2)).then_inc(split_out, 1)

                high = sem("a_high")
                mid = sem("a_mid")
                rest_ready = sem("a_rest_ready")
                low = sem("a_low")
                stored = sem("a_stored")
                with nc.Block() as block:
                    @block.vector
                    def _(dve):
                        qkn_norm.vector(dve)
                        link = Chain(dve, sem("a_split_chain"))
                        for s in range(2):
                            for c in range(NC):
                                g = s * NC + c
                                o = slice(c * CH, (c + 1) * CH)
                                dve.wait_ge(high, g + 1)
                                nc.vector.tensor_tensor(rest[:, s, o], feat[:, s, o], parts[:, s, 0, o],
                                                        ALU.subtract).then_inc(rest_ready, 1)
                                dve.wait_ge(mid, g + 1)
                                nc.vector.tensor_tensor(parts[:, s, 2, o], rest[:, s, o], parts[:, s, 1, o],
                                                        ALU.subtract).then_inc(low, 1)

                    @block.gpsimd
                    def _(pool):
                        qkn_norm.gpsimd(pool)

                    @block.tensor
                    def _(pe):
                        qkn_norm.tensor(pe)

                    @block.scalar
                    def _(act):
                        act.wait_ge(scaled, 1)
                        for g in range(2 * NC):
                            s, c = g // NC, g % NC
                            o = slice(c * CH, (c + 1) * CH)
                            act.wait_ge(qkn_norm.turned, g + 1)
                            nc.scalar.mul(feat[:, s, o], ps[:, 6 + g % 2, :],
                                          qscaled[:, 0:1] if s == 0 else col["k_scale"]).then_inc(qkn_norm.out, 1)
                            act.wait_ge(qkn_norm.out, g + 1)
                            nc.scalar.copy(parts[:, s, 0, o], feat[:, s, o]).then_inc(high, 1)
                            act.wait_ge(rest_ready, g + 1)
                            nc.scalar.copy(parts[:, s, 1, o], rest[:, s, o]).then_inc(mid, 1)

                    @block.sync
                    def _(sp):
                        for s, dst, n in ((0, q_parts, PARTS), (1, k_parts, 2 * PARTS - 1)):
                            sp.wait_ge(low, NC * (s + 1))
                            for r in range(n):
                                sp.dma_start(dst[:, r],
                                             parts[:, s, r % PARTS, :]).then_inc(stored, 16)
                        sp.wait_ge(stored, 16 * (3 * PARTS - 1))

                STEPS = [(0, 0), (0, 1), (0, 2), (0, 3), (1, 3), (1, 2), (1, 1), (1, 0)]
                UNITS = [TPC * (c + 1) for _, c in STEPS]
                CHUNKS = [GH * TPC * (c + 1) for _, c in STEPS]
                NU, NM, NS = sum(UNITS), sum(CHUNKS), len(STEPS)
                u0 = [sum(UNITS[:k]) for k in range(NS + 1)]
                m0 = [sum(CHUNKS[:k]) for k in range(NS + 1)]
                stack_loaded = [sem("a_stack_a"), sem("a_stack_b")]
                ones_set = sem("a_ones_set")
                ones_loaded = sem("a_ones_loaded")
                vg_ready = sem("a_vg_ready")
                vg_zero = sem("a_vg_zero")
                s_ready = sem("a_s_ready")
                s_read = sem("a_s_read")
                max_split = sem("a_max_split")
                max_turned = sem("a_max_turned")
                max_row = sem("a_max_row")
                max_set = sem("a_max_set")
                st_ready = sem("a_st_ready")
                exp_done = sem("a_exp_done")
                pv_done = sem("a_pv_done")
                o_out = sem("a_o_out")
                o_turned = sem("a_o_turned")
                o_kept = sem("a_o_kept")
                link_sem = sem("a_link")
                ST, S, O, TR = 0, 4, 6, 7

                with nc.Block() as block:
                    @block.sync
                    def _(sp):
                        sp.wait_ge(ones_set, 1)
                        for b in (0, 1):
                            for j in range(GH):
                                sp.dma_start(Ks[b][KROWS:KROWS + PARTS, j, :], ones[:]).then_inc(ones_loaded, 16)

                        def load(g):
                            b = g % 2
                            for j in range(GH):
                                h = g * GH + j
                                sp.dma_start(Qs[b][0:KROWS, j, :], bass.AP(
                                    tensor=q_parts.tensor, offset=h * PARTS * HD * T,
                                    ap=[[0, PARTS], [T, PARTS * HD], [1, T]])).then_inc(stack_loaded[b], 16)
                                sp.dma_start(Ks[b][0:KROWS, j, :], bass.AP(
                                    tensor=k_parts.tensor, offset=h * (2 * PARTS - 1) * HD * T,
                                    ap=[[HD * T, PARTS], [T, PARTS * HD], [1, T]])).then_inc(stack_loaded[b], 16)

                        def set_maxima(i, k):
                            b, c = STEPS[k]
                            n = i * NS + k + 1
                            sp.wait_ge(max_row, n)
                            for j in range(GH):
                                sp.dma_start(Qs[b][KROWS:KROWS + PARTS, j, c * CH:(c + 1) * CH],
                                             mrow[j * P // GH:j * P // GH + PARTS * TPC, :]).then_inc(max_set, 16)
                            sp.wait_ge(max_set, 16 * GH * n)

                        load(0)
                        load(1)
                        for i in range(2):
                            for k in range(NS):
                                set_maxima(i, k)
                                if i == 0 and k == 4:
                                    sp.wait_ge(pv_done, u0[4])
                                    load(2)
                            if i == 0:
                                sp.wait_ge(pv_done, NU)
                                load(3)

                    @block.gpsimd
                    def _(pool):
                        nc.gpsimd.memset(ones[:], 1.0).then_inc(ones_set, 1)
                        nc.gpsimd.memset(vg, 0.0).then_inc(vg_zero, 1)
                        pool.wait_ge(vg_zero, 1)
                        for g in range(NG):
                            if g >= 2:
                                pool.wait_ge(pv_done, u0[4] if g == 2 else NU)
                            nc.gpsimd.tensor_copy(vg[:, g % 2, :, :, 0:HD + 1],
                                                  vaug[:, :, g * GH:(g + 1) * GH, :]).then_inc(vg_ready, 1)

                    def keep_values(dve, i, k):
                        b, c = STEPS[k]
                        dve.wait_ge(o_turned, i * NS + k + 1)
                        o = ps[:, TR, :].rearrange("p (t j m) -> p t j m", t=TPC, j=GH)
                        nc.vector.reciprocal(rec[:, k % 2], o[:, :, :, HD]).then_inc(link_sem, 1)
                        dve.wait_ge(link_sem, i * (5 * NS) + (5 * (k + 2) - 1 if k < NS - 1 else 5 * NS))
                        for t in range(TPC):
                            ins = nc.vector.tensor_tensor(
                                ctxt[:, c * TPC + t, bass.ds(i * (2 * GH * HD) + b * GH * HD, GH * HD)].rearrange("p (j d) -> p j d", j=GH),
                                o[:, t, :, 0:HD],
                                rec[:, k % 2, t].rearrange("p (j a) -> p j a", a=1).to_broadcast([P, GH, HD]), ALU.mult)
                        ins.then_inc(o_kept, 1)

                    @block.vector
                    def _(dve):
                        nc.vector.memset(mwide[:], 0.0)
                        with dve.Fori(0, 2) as i:
                            for k, (b, c) in enumerate(STEPS):
                                n = m0[k]
                                for t in range(TPC):
                                    for j in range(GH):
                                        for kc in range(c + 1):
                                            width = CH if kc < c else (t + 1) * P
                                            dve.wait_ge(s_ready, i * NM + n + 1)
                                            nc.vector.tensor_reduce(out=mpart[:, j, t, kc:kc + 1], in_=ps[:, S + n % 2, 0:width],
                                                                    axis=AX.X, op=ALU.max).then_inc(s_read, 1)
                                            n += 1
                                dve.wait_ge(s_read, i * NM + n)
                                base = i * (5 * NS) + max(0, 5 * k - 1)
                                m, r1 = negmax[:, 0], negmax[:, 1]
                                nc.vector.tensor_reduce(out=m, in_=mpart[:, :, :, 0:c + 1],
                                                        axis=AX.X, op=ALU.max, negate=True).then_inc(link_sem, 1)
                                dve.wait_ge(link_sem, base + 1)
                                if k >= 1:
                                    dve.wait_ge(max_turned, i * NS + k)
                                nc.vector.tensor_copy(mparts[:, :, 0, :], m).then_inc(link_sem, 1)
                                dve.wait_ge(link_sem, base + 2)
                                nc.vector.tensor_tensor(r1, m, mparts[:, :, 0, :], ALU.subtract).then_inc(link_sem, 1)
                                dve.wait_ge(link_sem, base + 3)
                                nc.vector.tensor_copy(mparts[:, :, 1, :], r1).then_inc(link_sem, 1)
                                dve.wait_ge(link_sem, base + 4)
                                nc.vector.tensor_tensor(mparts[:, :, 2, :], r1, mparts[:, :, 1, :], ALU.subtract).then_inc(max_split, 1)
                                if k >= 1:
                                    keep_values(dve, i, k - 1)
                            keep_values(dve, i, NS - 1)
                            dve.wait_ge(max_set, i * (16 * GH * NS) + 16 * GH * NS)

                    def rows_of_maxima(act, i, k):
                        act.wait_ge(max_turned, i * NS + k + 1)
                        if k >= 1:
                            act.wait_ge(max_set, i * (16 * GH * NS) + 16 * GH * k)
                        nc.scalar.copy(mrow[:], ps[:, TR, 0:P // 2].bitcast(BF16)).then_inc(max_row, 1)

                    @block.tensor
                    def _(pe):
                        def scores_for_max(i, k):
                            b, c = STEPS[k]
                            n = m0[k]
                            for t in range(TPC):
                                for j in range(GH):
                                    q = Qs[b][0:KROWS, j, (c * TPC + t) * P:(c * TPC + t + 1) * P]
                                    for kc in range(c + 1):
                                        diagonal = kc == c
                                        width = (t + 1) * P if diagonal else CH
                                        if n >= 2:
                                            pe.wait_ge(s_read, i * NM + n - 1)
                                        out = ps[:, S + n % 2, 0:width]
                                        ins = nc.tensor.matmul(out, q, Ks[b][0:KROWS, j, kc * CH:kc * CH + width],
                                                               start=True, stop=not diagonal)
                                        if diagonal:
                                            ins = nc.tensor.matmul(out[:, width - P:width], identb, qmask, start=False, stop=True)
                                        ins.then_inc(s_ready, 1)
                                        n += 1
                                        yield

                        def turn_maxima(i, k):
                            pe.wait_ge(max_split, i * NS + k + 1)
                            if k >= 1:
                                pe.wait_ge(o_kept, i * NS + k - 1)
                            nc.tensor.transpose(ps[:, TR, 0:P // 2].bitcast(BF16), mwide[:].rearrange("p j m -> p (j m)"),
                                                identb).then_inc(max_turned, 1)

                        def values(i, k, kt):
                            b, c = STEPS[k]
                            n = u0[k] + kt
                            off = max(0, (kt - c * TPC) * P)
                            pe.wait_ge(exp_done, i * (2 * NU) + 2 * n + 2)
                            if kt == 0 and k >= 1:
                                pe.wait_ge(o_out, i * NS + k)
                            for j in range(GH):
                                ins = nc.tensor.matmul(ps[32 * j:32 * j + 32, O, off:CH], vg[:, b, kt, j, :],
                                                       probs[:, n % 2, j, off:CH], start=kt == 0, stop=kt == UNITS[k] - 1)
                            ins.then_inc(pv_done, 1)

                        def turn_values(i, k):
                            pe.wait_ge(o_out, i * NS + k + 1)
                            if k >= 1:
                                pe.wait_ge(o_kept, i * NS + k)
                            if k + 1 < NS:
                                pe.wait_ge(max_row, i * NS + k + 2)
                            for t in range(TPC):
                                ins = nc.tensor.transpose(ps[:, TR, t * P:(t + 1) * P], osb[:, k % 2, t * P:(t + 1) * P], ident)
                            ins.then_inc(o_turned, 1)

                        pe.wait_ge(ones_loaded, 16 * 2 * GH)
                        pe.wait_ge(stack_loaded[0], 16 * 2 * GH)
                        with pe.Fori(0, 2) as i:
                            pe.wait_ge(stack_loaded[0], i * (16 * 2 * GH) + 16 * 2 * GH)
                            for _ in scores_for_max(i, 0):
                                pass
                            turn_maxima(i, 0)
                            for k, (b, c) in enumerate(STEPS):
                                if k == 3:
                                    pe.wait_ge(stack_loaded[1], i * (16 * 2 * GH) + 16 * 2 * GH)
                                pe.wait_ge(max_set, i * (16 * GH * NS) + 16 * GH * (k + 1))
                                pe.wait_ge(vg_ready, i * 2 + b + 1)
                                ahead = scores_for_max(i, k + 1) if k + 1 < NS else iter(())
                                todo = CHUNKS[k + 1] if k + 1 < NS else 0
                                given = 0
                                for kt in range(UNITS[k]):
                                    n = u0[k] + kt
                                    off = max(0, (kt - c * TPC) * P)
                                    diagonal = kt >= c * TPC
                                    for pair in range(2):
                                        if n >= 1:
                                            pe.wait_ge(exp_done, i * (2 * NU) + 2 * n - 1 + pair)
                                        for j in (2 * pair, 2 * pair + 1):
                                            ins = nc.tensor.matmul(ps[:, ST + j, off:CH],
                                                                   Ks[b][0:KROWS + PARTS, j, kt * P:(kt + 1) * P],
                                                                   Qs[b][0:KROWS + PARTS, j, c * CH + off:(c + 1) * CH],
                                                                   start=True, stop=not diagonal)
                                            if diagonal:
                                                ins = nc.tensor.matmul(ps[:, ST + j, off:off + P], identb, kmask, start=False, stop=True)
                                        ins.then_inc(st_ready, 1)
                                    if kt >= 1:
                                        values(i, k, kt - 1)
                                    while given * UNITS[k] < todo * (kt + 1):
                                        next(ahead)
                                        given += 1
                                if k + 1 < NS:
                                    for _ in ahead:
                                        pass
                                values(i, k, UNITS[k] - 1)
                                if k + 1 < NS:
                                    turn_maxima(i, k + 1)
                                turn_values(i, k)
                            pe.wait_ge(s_read, i * NM + NM)
                            pe.wait_ge(exp_done, i * (2 * NU) + 2 * NU)
                            pe.wait_ge(o_kept, i * NS + NS)

                    @block.scalar
                    def _(act):
                        with act.Fori(0, 2) as i:
                            for k, (b, c) in enumerate(STEPS):
                                if k == 0:
                                    rows_of_maxima(act, i, 0)
                                for kt in range(UNITS[k]):
                                    n = u0[k] + kt
                                    off = max(0, (kt - c * TPC) * P)
                                    if n >= 2:
                                        act.wait_ge(pv_done, i * NU + n - 1)
                                    for pair in range(2):
                                        act.wait_ge(st_ready, i * (2 * NU) + 2 * n + pair + 1)
                                        nc.scalar.activation(probs[:, n % 2, 2 * pair:2 * pair + 2, off:CH],
                                                             ps[:, ST + 2 * pair:ST + 2 * pair + 2, off:CH], ACT.Exp).then_inc(exp_done, 1)
                                act.wait_ge(pv_done, i * NU + u0[k + 1])
                                nc.scalar.copy(osb[:, k % 2, :], ps[:, O, :]).then_inc(o_out, 1)
                                if k + 1 < NS:
                                    rows_of_maxima(act, i, k + 1)
                            act.wait_ge(o_kept, i * NS + NS)
                            act.wait_ge(max_set, i * (16 * GH * NS) + 16 * GH * NS)

                project_out("a_out", ctxt, w["wout"], None)

        def project_out(name, src, weight, source_norm):
            turned = sem(name + "_turned")
            copied = sem(name + "_copied")
            product = sem(name + "_product")
            added = sem(name + "_added")
            with nc.Block() as block:
                @block.tensor
                def _(pe):
                    for g in range(NC):
                        if g >= 2:
                            pe.wait_ge(copied, g - 1)
                        for t in range(TPC):
                            ins = nc.tensor.transpose(ps[:, g % 2, t * P:(t + 1) * P], src[:, g * TPC + t, :], ident)
                        ins.then_inc(turned, 1)
                    for g in range(NC):
                        pe.wait_ge(copied, g + 1)
                        if g >= 2:
                            pe.wait_ge(added, g - 1)
                        for t in range(TPC):
                            ins = nc.tensor.matmul(ps[:, 2 + g % 2, t * P:(t + 1) * P],
                                                   xT[:, (g * TPC + t) * P:(g * TPC + t + 1) * P], weight[:], start=True, stop=True)
                        ins.then_inc(product, 1)

                @block.scalar
                def _(act):
                    for g in range(NC):
                        act.wait_ge(turned, g + 1)
                        nc.scalar.copy(xT[:, g * CH:(g + 1) * CH], ps[:, g % 2, :]).then_inc(copied, 1)

                @block.vector
                def _(dve):
                    for g in range(NC):
                        dve.wait_ge(product, g + 1)
                        xs = x[:, g * TPC:(g + 1) * TPC, :].rearrange("p t d -> p (t d)")
                        nc.vector.tensor_tensor(xs, ps[:, 2 + g % 2, :], xs, ALU.add).then_inc(added, 1)

        def channel_mix(name):
            xr = arena[:, 0:T]
            xk = arena[:, T:2 * T]
            diff = arena[:, 2 * T:3 * T]
            rk = arena[:, 3 * T:4 * T]
            ka = arena[:, 4 * T:5 * T]
            r = arena[:, 5 * T:6 * T]
            rv = arena[:, 6 * T:7 * T]
            norm = Norm(name, x, xn, NT, 1e-5)
            differed = sem(name + "_differed")
            mixed_r = sem(name + "_mixed_r")
            k_ready = sem(name + "_k_ready")
            k_relu = sem(name + "_k_relu")
            k_squared = sem(name + "_k_squared")
            r_ready = sem(name + "_r_ready")
            r_out = sem(name + "_r_out")
            v_ready = sem(name + "_v_ready")
            gated = sem(name + "_gated")
            with nc.Block() as block:
                @block.vector
                def _(dve):
                    norm.vector(dve)
                    for c in range(NC):
                        o = slice(c * CH, (c + 1) * CH)
                        dve.wait_ge(differed, c + 1)
                        nc.vector.scalar_tensor_tensor(out=xk[:, o], in0=diff[:, o], scalar=col["mu_k"], in1=xt[:, o],
                                                       op0=ALU.mult, op1=ALU.add)
                        nc.vector.scalar_tensor_tensor(out=xr[:, o], in0=diff[:, o], scalar=col["mu_r"], in1=xt[:, o],
                                                       op0=ALU.mult, op1=ALU.add).then_inc(mixed_r, 1)
                    for c in range(NC):
                        o = slice(c * CH, (c + 1) * CH)
                        dve.wait_ge(v_ready, c + 1)
                        dve.wait_ge(r_out, c + 1)
                        nc.vector.tensor_tensor(rv[:, o], ps[:, 6 + c % 2, :], r[:, o], ALU.mult).then_inc(gated, 1)
                        dve.wait_ge(gated, c + 1)
                        xs = x[:, c * TPC:(c + 1) * TPC, :].rearrange("p t d -> p (t d)")
                        nc.vector.tensor_tensor(xs, rv[:, o], xs, ALU.add)

                @block.gpsimd
                def _(pool):
                    norm.gpsimd(pool)
                    for c in range(NC):
                        pool.wait_ge(norm.out, c + 1)
                        nc.gpsimd.tensor_tensor(diff[:, c * CH:(c + 1) * CH], xT[:, c * CH:(c + 1) * CH],
                                                xt[:, c * CH:(c + 1) * CH], ALU.subtract).then_inc(differed, 1)
                    for c in range(NC):
                        o = slice(c * CH, (c + 1) * CH)
                        pool.wait_ge(k_relu, c + 1)
                        nc.gpsimd.tensor_tensor(ka[:, o], rk[:, o], rk[:, o], ALU.mult).then_inc(k_squared, 1)

                @block.scalar
                def _(act):
                    norm.scalar(act)
                    for c in range(NC):
                        o = slice(c * CH, (c + 1) * CH)
                        act.wait_ge(k_ready, c + 1)
                        nc.scalar.activation(rk[:, o], ps[:, 2 + c % 2, :], ACT.Relu).then_inc(k_relu, 1)
                        act.wait_ge(r_ready, c + 1)
                        nc.scalar.activation(r[:, o], ps[:, 4 + c % 2, :], ACT.Sigmoid).then_inc(r_out, 1)

                @block.tensor
                def _(pe):
                    norm.tensor(pe)

                    def value(c):
                        pe.wait_ge(k_squared, c + 1)
                        if c >= 2:
                            pe.wait_ge(gated, c - 1)
                        for t in range(TPC):
                            ins = nc.tensor.matmul(ps[:, 6 + c % 2, t * P:(t + 1) * P],
                                                   ka[:, c * CH + t * P:c * CH + (t + 1) * P], w["wv"][:], start=True, stop=True)
                        ins.then_inc(v_ready, 1)

                    for c in range(NC):
                        pe.wait_ge(mixed_r, c + 1)
                        if c >= 2:
                            pe.wait_ge(k_relu, c - 1)
                        nc.tensor.matmul(ps[:, 2 + c % 2, :], w["wk"][:], xk[:, c * CH:(c + 1) * CH],
                                         start=True, stop=True).then_inc(k_ready, 1)
                        if c >= 2:
                            pe.wait_ge(r_out, c - 1)
                        for t in range(TPC):
                            ins = nc.tensor.matmul(ps[:, 4 + c % 2, t * P:(t + 1) * P],
                                                   xr[:, c * CH + t * P:c * CH + (t + 1) * P], w["wr"][:], start=True, stop=True)
                        ins.then_inc(r_ready, 1)
                        if c >= 1:
                            value(c - 1)
                    value(NC - 1)

        def linear_attention(name, kind):
            wq, wk, wv = {"gated": ("hq", "hk", "hv"), "retention": ("rq", "rk", "rv"), "lightning": ("lq", "lk", "lv")}[kind]
            at = [0]

            def take(words):
                at[0] += words
                return arena[:, at[0] - words:at[0]]

            q = take(2 * CH).rearrange("p (b t) -> p b t", b=2)
            k = take(2 * CH).rearrange("p (b t) -> p b t", b=2)
            dec = take(2 * CH).rearrange("p (b t) -> p b t", b=2)
            vs = take(2 * CH).rearrange("p (b t) -> p b t", b=2)
            upd = take(2 * CH).rearrange("p (b t) -> p b t", b=2)
            state = take(2 * HD * CH).rearrange("p (b e t) -> p b e t", b=2, e=HD)
            z = take(HD * CH).rearrange("p (e t) -> p e t", e=HD)
            vrep = take(HD * P).rearrange("p (e h d) -> p e h d", e=HD, h=H)
            orep = take(HD * P).rearrange("p (e m) -> p e m", e=HD)
            y = take(T)
            gate = take(T)
            g1 = take(2 * CH)[0:HD, :].rearrange("p (b t) -> p b t", b=2)
            negb = take(1)
            norm = Norm(name, x, xn, NT, 1e-5)
            rep_ready = sem(name + "_rep_ready")
            kq_ready = sem(name + "_kq_ready")
            kq_out = sem(name + "_kq_out")
            v_ready = sem(name + "_v_ready")
            v_out = sem(name + "_v_out")
            upd_ready = sem(name + "_upd_ready")
            scanned = sem(name + "_scanned")
            z_ready = sem(name + "_z_ready")
            summed = sem(name + "_summed")
            sum_out = sem(name + "_sum_out")
            g_ready = sem(name + "_g_ready")
            g_out = sem(name + "_g_out")
            gate_ready = sem(name + "_gate_ready")
            gate_out = sem(name + "_gate_out")
            orep_loaded = sem(name + "_orep_loaded")
            if kind == "gated":
                reduce_w = orep
            else:
                reduce_w = pick
            with nc.Block() as block:
                @block.gpsimd
                def _(pool):
                    wvT = w[wv][:].rearrange("p (h e) -> p h e", e=HD)
                    for e in range(HD):
                        nc.gpsimd.tensor_copy(vrep[:, e], wvT[:, :, e:e + 1].to_broadcast([P, H, HD])).then_inc(rep_ready, 1)
                    if kind == "gated":
                        nc.gpsimd.tensor_scalar(negb, col["key_b"], -1.0, None, ALU.mult).then_inc(rep_ready, 1)
                    norm.gpsimd(pool)
                    for c in range(NC):
                        for e in range(HD):
                            n = c * HD + e
                            pool.wait_ge(scanned, n + 1)
                            if e == 0:
                                pool.wait_ge(kq_out, 2 * c + 2)
                                if c >= 1:
                                    pool.wait_ge(summed, c)
                            nc.gpsimd.tensor_tensor(z[:, e, :], state[:, c % 2, e, :], q[:, c % 2, :], ALU.mult).then_inc(z_ready, 1)

                def add(dve, c):
                    dve.wait_ge(summed, c + 1)
                    xs = x[:, c * TPC:(c + 1) * TPC, :]
                    nc.vector.tensor_tensor(xs, ps[:, 6 + c % 2, :].rearrange("p (t d) -> p t d", d=D), xs, ALU.add).then_inc(sum_out, 1)
                    dve.wait_ge(sum_out, c + 1)
                    nc.vector.tensor_tensor(xs, xs, out_bias[:].rearrange("p (a d) -> p a d", a=1).to_broadcast([P, TPC, D]), ALU.add)

                @block.vector
                def _(dve):
                    norm.vector(dve)
                    for c in range(NC):
                        for e in range(HD):
                            n = c * HD + e
                            if kind == "lightning":
                                dve.wait_ge(v_out, n + 1)
                                v_in = vs[:, n % 2, :]
                            else:
                                dve.wait_ge(v_ready, n + 1)
                                v_in = ps[:, 4 + n % 2, :]
                            dve.wait_ge(kq_out, 2 * c + 1)
                            nc.vector.tensor_tensor(upd[:, n % 2, :], v_in, k[:, c % 2, :], ALU.mult).then_inc(upd_ready, 1)
                            dve.wait_ge(upd_ready, n + 1)
                            if c >= 2:
                                dve.wait_ge(z_ready, n - 2 * HD + 1)
                            if c >= 1:
                                dve.wait_ge(scanned, n - HD + 1)
                            a = dec[:, c % 2, :] if kind == "gated" else \
                                cst[:, C_RET if kind == "retention" else C_LT:][:, 0:1].to_broadcast([P, CH])
                            nc.vector.tensor_tensor_scan(
                                out=state[:, c % 2, e, :], data0=a, data1=upd[:, n % 2, :],
                                initial=0.0 if c == 0 else state[:, 1 - c % 2, e, CH - 1:CH],
                                op0=ALU.mult, op1=ALU.add).then_inc(scanned, 1)
                        if kind == "gated" and c >= 1:
                            add(dve, c - 1)
                    if kind == "gated":
                        add(dve, NC - 1)

                def copy_out(act, c):
                    act.wait_ge(summed, c + 1)
                    nc.scalar.copy(y[:, c * CH:(c + 1) * CH], ps[:, 6 + c % 2, :]).then_inc(sum_out, 1)

                @block.scalar
                def _(act):
                    norm.scalar(act)
                    for c in range(NC):
                        act.wait_ge(kq_ready, 2 * c + 1)
                        if c >= 2:
                            act.wait_ge(z_ready, (c - 1) * HD)
                        pk = ps[:, 2, :]
                        if kind == "gated":
                            nc.scalar.activation(dec[:, c % 2, :], pk, ACT.Sigmoid, bias=col["key_b"])
                            if c == 0:
                                act.wait_ge(rep_ready, HD + 1)
                            nc.scalar.activation(k[:, c % 2, :], pk, ACT.Sigmoid, bias=negb, scale=-1.0).then_inc(kq_out, 1)
                        elif kind == "retention":
                            nc.scalar.copy(k[:, c % 2, :], pk).then_inc(kq_out, 1)
                        else:
                            nc.scalar.activation(k[:, c % 2, :], pk, ACT.Silu).then_inc(kq_out, 1)
                        act.wait_ge(kq_ready, 2 * c + 2)
                        pq = ps[:, 3, :]
                        if kind == "gated":
                            nc.scalar.copy(q[:, c % 2, :], pq).then_inc(kq_out, 1)
                        elif kind == "retention":
                            nc.scalar.mul(q[:, c % 2, :], pq, float(HD) ** -0.5).then_inc(kq_out, 1)
                        else:
                            nc.scalar.activation(q[:, c % 2, :], pq, ACT.Silu).then_inc(kq_out, 1)
                            for e in range(HD):
                                n = c * HD + e
                                act.wait_ge(v_ready, n + 1)
                                if n >= 2:
                                    act.wait_ge(upd_ready, n - 1)
                                nc.scalar.activation(vs[:, n % 2, :], ps[:, 4 + n % 2, :], ACT.Silu).then_inc(v_out, 1)
                        if kind != "gated" and c >= 1:
                            copy_out(act, c - 1)
                    if kind != "gated":
                        copy_out(act, NC - 1)
                    if kind == "lightning":
                        for c in range(NC):
                            act.wait_ge(g_ready, c + 1)
                            nc.scalar.copy(g1[:, c % 2, :], ps[0:HD, 2, :]).then_inc(g_out, 1)
                            act.wait_ge(gate_ready, c + 1)
                            nc.scalar.activation(gate[:, c * CH:(c + 1) * CH], ps[:, 3, :], ACT.Sigmoid).then_inc(gate_out, 1)

                @block.tensor
                def _(pe):
                    norm.tensor(pe)
                    pe.wait_ge(rep_ready, HD)
                    if kind == "gated":
                        pe.wait_ge(orep_loaded, 16 * HD)

                    def total(c):
                        pe.wait_ge(z_ready, (c + 1) * HD)
                        if c >= 2:
                            pe.wait_ge(sum_out, c - 1)
                        if kind == "retention":
                            for e in range(HD):
                                ins = nc.tensor.matmul(ps[:, 6 + c % 2, :], reduce_w[:, e, :], z[:, e, :],
                                                       start=e == 0, stop=e == HD - 1)
                        else:
                            for t in range(TPC):
                                for e in range(HD):
                                    ins = nc.tensor.matmul(ps[:, 6 + c % 2, t * P:(t + 1) * P], z[:, e, t * P:(t + 1) * P],
                                                           reduce_w[:, e, :], start=e == 0, stop=e == HD - 1)
                        ins.then_inc(summed, 1)

                    for c in range(NC):
                        o = slice(c * CH, (c + 1) * CH)
                        pe.wait_ge(norm.out, c + 1)
                        if c >= 1:
                            pe.wait_ge(kq_out, 2 * c - 1)
                        nc.tensor.matmul(ps[:, 2, :], w[wk][:], xT[:, o], start=True, stop=True).then_inc(kq_ready, 1)
                        if c >= 1:
                            pe.wait_ge(kq_out, 2 * c)
                        nc.tensor.matmul(ps[:, 3, :], w[wq][:], xT[:, o], start=True, stop=True).then_inc(kq_ready, 1)
                        for e in range(HD):
                            n = c * HD + e
                            if n >= 2:
                                pe.wait_ge(v_out if kind == "lightning" else upd_ready, n - 1)
                            nc.tensor.matmul(ps[:, 4 + n % 2, :], vrep[:, e].rearrange("p h d -> p (h d)"), xT[:, o],
                                             start=True, stop=True).then_inc(v_ready, 1)
                        if c >= 1:
                            total(c - 1)
                    total(NC - 1)
                    if kind == "lightning":
                        for c in range(NC):
                            if c == 0:
                                pe.wait_ge(kq_out, 2 * NC)
                            else:
                                pe.wait_ge(g_out, c)
                            nc.tensor.matmul(ps[0:HD, 2, :], w["lg1"][:], xT[:, c * CH:(c + 1) * CH], start=True, stop=True).then_inc(g_ready, 1)
                            pe.wait_ge(g_out, c + 1)
                            if c >= 1:
                                pe.wait_ge(gate_out, c)
                            nc.tensor.matmul(ps[:, 3, :], w["lg2"][:], g1[:, c % 2, :], start=True, stop=True).then_inc(gate_ready, 1)

                @block.sync
                def _(sp):
                    if kind == "gated":
                        for e in range(HD):
                            sp.dma_start(orep[:, e, :], bass.AP(tensor=io["ho"].tensor, offset=e * D,
                                                                ap=[[HD * D, H], [0, HD], [1, D]])).then_inc(orep_loaded, 16)

            if kind == "retention":
                retention_out(name, y, z)
            if kind == "lightning":
                lightning_out(name, y, gate)

        def retention_out(name, y, z):
            yn = z.rearrange("p e t -> p (e t)")[:, 0:T]
            st = stats[:, 0:NC, :]
            mv, dev, sc = small[:, 0, 0:2], small[:, 1, 0:3], small[:, 2, 0:8]
            link_sem = sem(name + "_gn_link")
            stat_ready = sem(name + "_gn_stat")
            head_mean_ready = sem(name + "_gn_mean")
            dev_ready = sem(name + "_gn_dev")
            head_var_ready = sem(name + "_gn_var")
            var_ready = sem(name + "_gn_vareps")
            rstd_ready = sem(name + "_gn_rstd")
            normed = sem(name + "_gn_normed")
            product = sem(name + "_gn_product")
            added = sem(name + "_gn_added")
            with nc.Block() as block:
                @block.vector
                def _(dve):
                    link = Chain(dve, link_sem)
                    for c in range(NC):
                        ins = nc.vector.bn_stats(st[:, c, :], y[:, c * CH:(c + 1) * CH])
                    link(ins)
                    nc.vector.bn_aggr(mv, st.rearrange("p c s -> p (c s)")).then_inc(stat_ready, 1)
                    dve.wait_ge(head_mean_ready, 1)
                    link(nc.vector.tensor_copy(sc[:, 0:1], ps[:, 0, 0:1]))
                    link(nc.vector.tensor_tensor(dev[:, 0:1], mv[:, 0:1], sc[:, 0:1], ALU.subtract))
                    link(nc.vector.tensor_tensor(dev[:, 1:2], dev[:, 0:1], dev[:, 0:1], ALU.mult))
                    nc.vector.tensor_tensor(dev[:, 2:3], dev[:, 1:2], mv[:, 1:2], ALU.add).then_inc(dev_ready, 1)
                    dve.wait_ge(head_var_ready, 1)
                    nc.vector.tensor_scalar(sc[:, 1:2], ps[:, 1, 0:1], 1e-5, None, ALU.add).then_inc(var_ready, 1)
                    dve.wait_ge(rstd_ready, 1)
                    link(nc.vector.tensor_tensor(sc[:, 3:4], sc[:, 2:3], col["gn_w"], ALU.mult))
                    for c in range(NC):
                        o = slice(c * CH, (c + 1) * CH)
                        link(nc.vector.tensor_scalar(yn[:, o], y[:, o], sc[:, 0:1], sc[:, 3:4], ALU.subtract, ALU.mult))
                        nc.vector.tensor_scalar(yn[:, o], yn[:, o], col["gn_b"], None, ALU.add).then_inc(normed, 1)
                    for c in range(NC):
                        dve.wait_ge(product, c + 1)
                        xs = x[:, c * TPC:(c + 1) * TPC, :].rearrange("p t d -> p (t d)")
                        nc.vector.tensor_tensor(xs, ps[:, 2 + c % 2, :], xs, ALU.add).then_inc(added, 1)

                @block.gpsimd
                def _(pool):
                    pool.wait_ge(var_ready, 1)
                    nc.gpsimd.tensor_tensor(sc[:, 2:3], sc[:, 1:2], neghalf[:, 0:1], ALU.pow).then_inc(rstd_ready, 1)

                @block.tensor
                def _(pe):
                    pe.wait_ge(stat_ready, 1)
                    nc.tensor.matmul(ps[:, 0, 0:1], head_mean, mv[:, 0:1], start=True, stop=True).then_inc(head_mean_ready, 1)
                    pe.wait_ge(dev_ready, 1)
                    nc.tensor.matmul(ps[:, 1, 0:1], head_mean, dev[:, 2:3], start=True, stop=True).then_inc(head_var_ready, 1)
                    for c in range(NC):
                        pe.wait_ge(normed, c + 1)
                        if c >= 2:
                            pe.wait_ge(added, c - 1)
                        for t in range(TPC):
                            ins = nc.tensor.matmul(ps[:, 2 + c % 2, t * P:(t + 1) * P],
                                                   yn[:, c * CH + t * P:c * CH + (t + 1) * P], w["ro"][:], start=True, stop=True)
                        ins.then_inc(product, 1)

        def lightning_out(name, y, gate):
            norm = Norm(name + "_o", y.rearrange("p (t d) -> p t d", d=D), xn, NT, 1e-5)
            gated = sem(name + "_gated")
            product = sem(name + "_product")
            added = sem(name + "_added")
            with nc.Block() as block:
                @block.vector
                def _(dve):
                    norm.vector(dve)
                    for c in range(NC):
                        o = slice(c * CH, (c + 1) * CH)
                        dve.wait_ge(norm.turned, c + 1)
                        nc.vector.tensor_scalar(xT[:, o], ps[:, c % 2, :], col["gamma"], col["beta"], ALU.mult, ALU.add).then_inc(norm.out, 1)
                        dve.wait_ge(norm.out, c + 1)
                        nc.vector.tensor_tensor(xT[:, o], xT[:, o], gate[:, o], ALU.mult).then_inc(gated, 1)
                    for c in range(NC):
                        dve.wait_ge(product, c + 1)
                        xs = x[:, c * TPC:(c + 1) * TPC, :].rearrange("p t d -> p (t d)")
                        nc.vector.tensor_tensor(xs, ps[:, 2 + c % 2, :], xs, ALU.add).then_inc(added, 1)

                @block.gpsimd
                def _(pool):
                    norm.gpsimd(pool)

                @block.tensor
                def _(pe):
                    norm.tensor(pe)
                    for c in range(NC):
                        pe.wait_ge(gated, c + 1)
                        if c >= 2:
                            pe.wait_ge(added, c - 1)
                        for t in range(TPC):
                            ins = nc.tensor.matmul(ps[:, 2 + c % 2, t * P:(t + 1) * P],
                                                   xT[:, c * CH + t * P:c * CH + (t + 1) * P], w["lo"][:], start=True, stop=True)
                        ins.then_inc(product, 1)

        def experts(name):
            at = [0]

            def take(words):
                at[0] += words
                return arena[:, at[0] - words:at[0]]

            lg, l2, eq, oh1, oh2, ex, msk, wt, t0 = (take(NT * E).rearrange("p (t e) -> p t e", e=E) for _ in range(9))
            m1, m2, mx, s1, s2 = (take(NT).rearrange("p (t a) -> p t a", a=1) for _ in range(5))
            act_a = take(2 * CH).rearrange("p (b t) -> p b t", b=2)
            hid = take(2 * NF * CH).rearrange("p (b f t) -> p b f t", b=2, f=NF)
            norm = Norm(name, x, xn, NT, 1e-5)
            logits = sem(name + "_logits")
            link_sem = sem(name + "_link")
            exp_in = sem(name + "_exp_in")
            exp_out = sem(name + "_exp_out")
            up_ready = sem(name + "_up_ready")
            silu_out = sem(name + "_silu_out")
            hid_ready = sem(name + "_hid_ready")
            down_ready = sem(name + "_down_ready")
            down_out = sem(name + "_down_out")
            with nc.Block() as block:
                @block.vector
                def _(dve):
                    norm.vector(dve)
                    link = Chain(dve, link_sem)

                    def wide(a):
                        return a.to_broadcast([P, NT, E])

                    def first_max(src, m, onehot):
                        link(nc.vector.tensor_reduce(out=m[:, :, 0], in_=src, axis=AX.X, op=ALU.max))
                        link(nc.vector.tensor_tensor(eq, src, wide(m), ALU.is_equal))
                        link(nc.vector.tensor_tensor(eq, eq, rank.rearrange("p (a e) -> p a e", a=1).to_broadcast([P, NT, E]), ALU.mult))
                        link(nc.vector.tensor_reduce(out=mx[:, :, 0], in_=eq, axis=AX.X, op=ALU.max))
                        link(nc.vector.tensor_tensor(onehot, eq, wide(mx), ALU.is_equal))

                    def multiplier(k, src, m, s):
                        link(nc.vector.scalar_tensor_tensor(out=msk, in0=lg, scalar=-1.0, in1=lg, op0=ALU.mult, op1=ALU.max))
                        link(nc.vector.tensor_tensor(msk, msk, wide(m), ALU.max))
                        link(nc.vector.tensor_tensor(t0, wide(m), lg, ALU.subtract))
                        link(nc.vector.scalar_tensor_tensor(out=msk, in0=msk, scalar=0.02, in1=t0, op0=ALU.mult, op1=ALU.is_ge))
                        nc.vector.tensor_tensor(t0, src, wide(m), ALU.subtract).then_inc(exp_in, 1)
                        dve.wait_ge(exp_out, k)
                        link(nc.vector.tensor_tensor(ex, ex, msk, ALU.mult))
                        link(nc.vector.tensor_reduce(out=s[:, :, 0], in_=ex, axis=AX.X, op=ALU.add))
                        link(nc.vector.reciprocal(s, s))

                    dve.wait_ge(logits, 1)
                    link(nc.vector.tensor_copy(lg, ps[:, 2, 0:NT * E].rearrange("p (t e) -> p t e", e=E)))
                    first_max(lg, m1, oh1)
                    link(nc.vector.scalar_tensor_tensor(out=l2, in0=oh1, scalar=NEG, in1=lg, op0=ALU.mult, op1=ALU.add))
                    first_max(l2, m2, oh2)
                    multiplier(1, lg, m1, s1)
                    multiplier(2, l2, m2, s2)
                    link(nc.vector.tensor_tensor(oh1, oh1, wide(s1), ALU.mult))
                    link(nc.vector.tensor_tensor(oh2, oh2, wide(s2), ALU.mult))
                    link(nc.vector.tensor_tensor(wt, oh1, oh2, ALU.add))

                    def down(e, c):
                        u = e * NC + c
                        dve.wait_ge(down_ready, u + 1)
                        for t in range(TPC):
                            tt = c * TPC + t
                            ins = nc.vector.scalar_tensor_tensor(
                                out=x[:, tt, :], in0=ps[:, 6 + u % 2, t * P:(t + 1) * P], scalar=wt[:, tt, e:e + 1],
                                in1=x[:, tt, :], op0=ALU.mult, op1=ALU.add)
                        ins.then_inc(down_out, 1)
                        if c == NC - 1:
                            dve.wait_ge(down_out, u + 1)

                    for e in range(E):
                        for c in range(NC):
                            u = e * NC + c
                            for f in range(NF):
                                n = u * NF + f
                                dve.wait_ge(silu_out, n + 1)
                                if f == 0 and u >= 2:
                                    dve.wait_ge(down_ready, u - 1)
                                nc.vector.tensor_tensor(hid[:, u % 2, f, :], ps[:, 4 + n % 2, :], act_a[:, n % 2, :],
                                                        ALU.mult).then_inc(hid_ready, 1)
                            if u >= 1:
                                down((u - 1) // NC, (u - 1) % NC)
                    down(E - 1, NC - 1)

                @block.gpsimd
                def _(pool):
                    norm.gpsimd(pool)

                @block.scalar
                def _(act):
                    norm.scalar(act)
                    for k in (1, 2):
                        act.wait_ge(exp_in, k)
                        nc.scalar.activation(ex, t0, ACT.Exp).then_inc(exp_out, 1)
                    for n in range(E * NC * NF):
                        act.wait_ge(up_ready, n + 1)
                        if n >= 2:
                            act.wait_ge(hid_ready, n - 1)
                        nc.scalar.activation(act_a[:, n % 2, :], ps[:, 2 + n % 2, :], ACT.Silu).then_inc(silu_out, 1)

                @block.tensor
                def _(pe):
                    norm.tensor(pe)
                    for t in range(NT):
                        pe.wait_ge(norm.out, t // TPC + 1)
                        ins = nc.tensor.matmul(ps[:, 2, t * E:(t + 1) * E], xT[:, t * P:(t + 1) * P], w["gate"][:], start=True, stop=True)
                    ins.then_inc(logits, 1)
                    pe.wait_ge(moe_loaded, 48)
                    pe.wait_ge(link_sem, 1)

                    def down(e, c):
                        u = e * NC + c
                        pe.wait_ge(hid_ready, (u + 1) * NF)
                        if u >= 2:
                            pe.wait_ge(down_out, u - 1)
                        for t in range(TPC):
                            for f in range(NF):
                                ins = nc.tensor.matmul(ps[:, 6 + u % 2, t * P:(t + 1) * P], hid[:, u % 2, f, t * P:(t + 1) * P],
                                                       w2[:, e, f, :], start=f == 0, stop=f == NF - 1)
                        ins.then_inc(down_ready, 1)

                    for e in range(E):
                        for c in range(NC):
                            u = e * NC + c
                            o = slice(c * CH, (c + 1) * CH)
                            for f in range(NF):
                                n = u * NF + f
                                if n >= 2:
                                    pe.wait_ge(hid_ready, n - 1)
                                nc.tensor.matmul(ps[:, 2 + n % 2, :], w1[:, e, f * P:(f + 1) * P], xT[:, o], start=True, stop=True)
                                nc.tensor.matmul(ps[:, 4 + n % 2, :], w3[:, e, f * P:(f + 1) * P], xT[:, o],
                                                 start=True, stop=True).then_inc(up_ready, 1)
                            if u >= 1:
                                down((u - 1) // NC, (u - 1) % NC)
                    down(E - 1, NC - 1)

        softmax_attention()
        load_experts()
        end_stage()
        channel_mix("f0")
        end_stage()
        linear_attention("g", "gated")
        end_stage()
        channel_mix("f1")
        end_stage()
        linear_attention("r", "retention")
        end_stage()
        experts("m0")
        end_stage()
        linear_attention("l", "lightning")
        end_stage()
        experts("m1")
        x_stored = sem("x_stored")
        with nc.Block() as block:
            @block.sync
            def _(sp):
                sp.dma_start(io["out"].rearrange("a (t p) d -> p (a t) d", p=P), x[:]).then_inc(x_stored, 16)
                sp.wait_ge(x_stored, 16)


def constants():
    import numpy as np
    c = np.zeros((P, C_F32), np.float32)
    c[:, C_IDENT:C_IDENT + P] = np.eye(P)
    ch = np.arange(P)
    for e in range(HD):
        c[ch, C_PICK + e * P + ch // HD * HD + e] = 1.0
    c[:, C_HEAD:C_HEAD + P] = (ch[:, None] // HD == ch[None, :] // HD) / HD
    h = ch // HD
    c[:, C_RET] = 1.0 - 2.0 ** (-5.0 - h * (8.0 / H))
    start = 2.0 ** (-2.0 ** (-(np.log2(H) - 3)))
    slope = np.array([start * start ** i for i in range(H)], np.float32) * np.float32(1.0 + 1e-05)
    c[:, C_LT] = np.exp(-slope.astype(np.float64))[h]
    c[:, C_RANK:C_RANK + E] = E - np.arange(E)
    c[:, C_QMASK:C_QMASK + P] = np.where(ch[None, :] > ch[:, None], NEG, 0.0)
    c[:, C_KMASK:C_KMASK + P] = np.where(ch[:, None] > ch[None, :], NEG, 0.0)
    return c


def kernel(**inputs):
    import numpy as np
    import concourse.bacc as bacc
    from concourse.bass_utils import run_bass_kernel_spmd

    a = {k: np.asarray(v) for k, v in inputs.items()}
    vq = a["L0_attn_b_vq_w"]
    given = {
        "x": a["L0_attn_a_x"], "cst": constants(),
        "qkv": a["L0_attn_a_W_qkv"], "wout": a["L0_attn_a_W_out"],
        "wr": a["L0_ffn_W_r"].T, "wk": a["L0_ffn_W_k"].T, "wv": a["L0_ffn_W_v"].T,
        "hk": a["L0_attn_b_key_w"].T, "hv": vq[:D].T, "hq": vq[D:].T, "ho": a["L0_attn_b_out_w"].T,
        "rq": a["L1_attn_a_Wq"].T, "rk": a["L1_attn_a_Wk"].T, "rv": a["L1_attn_a_Wv"].T, "ro": a["L1_attn_a_Wo"].T,
        "lq": a["L1_attn_b_Wq"], "lk": a["L1_attn_b_Wk"], "lv": a["L1_attn_b_Wv"], "lo": a["L1_attn_b_Wo"],
        "lg1": a["L1_attn_b_Wg1"], "lg2": a["L1_attn_b_Wg2"], "gate": a["L1_ffn_gate_w"],
        "out_b": a["L0_attn_b_out_b"], "w1": a["L1_ffn_w1"], "w2": a["L1_ffn_w2"], "w3": a["L1_ffn_w3"],
        "q_scale": a["L0_attn_a_q_scale"], "k_scale": a["L0_attn_a_k_scale"], "key_b": a["L0_attn_b_key_b"],
        "mu_r": a["L0_ffn_mu_r"], "mu_k": a["L0_ffn_mu_k"], "gn_w": a["L1_attn_a_gn_w"], "gn_b": a["L1_attn_a_gn_b"],
        "gamma": a["L1_attn_b_gamma"], "beta": a["L1_attn_b_beta"],
    }
    nc = bacc.Bacc("TRN2", target_bir_lowering=False, num_devices=1)
    arrays, io = {}, {}
    for name, v in given.items():
        v = np.ascontiguousarray(v)
        arrays["in_" + name] = v
        io[name] = nc.dram_tensor("in_" + name, v.shape, mybir.dt.from_np(v.dtype), kind="ExternalInput").ap()
    io["out"] = nc.dram_tensor("out_x", (1, T, D), FP32, kind="ExternalOutput").ap()
    build(nc, io)
    r = run_bass_kernel_spmd(nc, [arrays], core_ids=[0])
    return r.results[0]["out_x"]
```

```python
import concourse.bass as bass
from concourse import mybir
from contextlib import ExitStack

FP32 = mybir.dt.float32
BF16 = mybir.dt.bfloat16
U32 = mybir.dt.uint32
ACT = mybir.ActivationFunctionType
ALU = mybir.AluOpType
AX = mybir.AxisListType

T = 2048
D = 128
H = 16
HD = D // H
P = 128
NT = T // P
CH = 512
NC = T // CH
TPC = CH // P
E = 8
F = 512
NF = F // P
TOP = 2
ST = TOP * NT + E - 1
ROW = D + 1
PARTS = 3
KROWS = PARTS * PARTS * HD
MROW = 96
GH = 4
NG = H // GH
NEG = -1.0e30

C_IDENT = 0
C_PICK = C_IDENT + P
C_HEAD = C_PICK + HD * P
C_RET = C_HEAD + P
C_LT = C_RET + 1
C_RANK = C_LT + 1
C_QMASK = C_RANK + E
C_KMASK = C_QMASK + P
C_COUNT = C_KMASK + P
C_PART = C_COUNT + TOP * NT + ST
C_F32 = C_PART + 1

WEIGHTS = [("qkv", 3 * D), ("wout", D), ("wr", D), ("wk", D), ("wv", D), ("hk", D), ("hv", D), ("hq", D), ("ho", D),
           ("rq", D), ("rk", D), ("rv", D), ("ro", D), ("lq", D), ("lk", D), ("lv", D), ("lo", D), ("lg1", HD),
           ("gate", E)]
VECTORS = ["q_scale", "k_scale", "key_b", "mu_r", "mu_k", "gn_w", "gn_b", "gamma", "beta"]
LOADS = 4 + len(WEIGHTS) + len(VECTORS)


def build(nc, io):
    ctx = ExitStack()
    with ctx:
        def sb(name, shape, dt=FP32):
            return ctx.enter_context(nc.sbuf_tensor(name, shape, dt))

        stage_sems = []

        def sem(name):
            stage_sems.append(nc.alloc_semaphore(name=name))
            return stage_sems[-1]

        def end_stage():
            with nc.Block() as block:
                @block.gpsimd
                def _(pool):
                    nc.clear_and_free_semaphores(stage_sems)
            stage_sems.clear()

        x = sb("x", [P, NT, D])
        xn = sb("xn", [P, NT, D])
        xt = sb("xt", [P, 1 + T])
        xT = xt[:, 1:1 + T]
        cst = sb("cst", [P, C_F32])
        cstb = sb("cstb", [P, 3 * P], BF16)
        w = {}
        for name, width in WEIGHTS:
            w[name] = sb("w_" + name, [P, width])
        w["lg2"] = sb("w_lg2", [HD, D])
        vec = sb("vec", [P, len(VECTORS)])
        col = {name: vec[:, i:i + 1] for i, name in enumerate(VECTORS)}
        out_bias = sb("out_bias", [P, D])
        w1 = sb("w1", [P, E, F])
        w3 = sb("w3", [P, E, F])
        w2 = sb("w2", [P, E, NF, D])
        stats = sb("stats", [P, 2 * NT, 6])
        small = sb("small", [P, 10, 2 * NT])
        neghalf = sb("neghalf", [P, NT])
        arena = sb("arena", [P, 24 * 1024 + 8])
        ps = ctx.enter_context(nc.psum_tensor("ps", [P, 8, CH], FP32))

        ident = cst[:, C_IDENT:C_IDENT + P]
        pick = cst[:, C_PICK:C_PICK + HD * P].rearrange("p (e m) -> p e m", e=HD)
        head_mean = cst[:, C_HEAD:C_HEAD + P]
        rank = cst[:, C_RANK:C_RANK + E]
        count = cst[:, C_COUNT:C_PART]
        row_number = cst[:, C_PART:C_PART + 1]
        identb, qmask, kmask = (cstb[:, i * P:(i + 1) * P] for i in range(3))

        q_parts = nc.dram_tensor("q_parts", [H, PARTS, HD, T], BF16, kind="Internal").ap()
        k_parts = nc.dram_tensor("k_parts", [H, 2 * PARTS - 1, HD, T], BF16, kind="Internal").ap()

        slots = [nc.dram_tensor(f"slots{i}", [ST * P, ROW], FP32, kind="Internal").ap() for i in range(2)]
        results = [nc.dram_tensor(f"results{i}", [(TOP * NT + ST) * P, D], FP32, kind="Internal").ap() for i in range(2)]
        slots_cleared = ctx.enter_context(nc.semaphore("slots_cleared"))
        EMPTY1 = E * F // ROW
        empty = [(0, EMPTY1, w2[:].rearrange("p e f d -> p (e f d)")[:, 0:EMPTY1 * ROW].rearrange("p (s c) -> p s c", c=ROW)),
                 (EMPTY1, ST, arena[:, 11 * NT * D:11 * NT * D + (ST - EMPTY1) * ROW].rearrange("p (s c) -> p s c", c=ROW))]

        loaded = ctx.enter_context(nc.semaphore("loaded"))
        moe_loaded = ctx.enter_context(nc.semaphore("moe_loaded"))

        class Chain:

            def __init__(self, eng, s):
                self.eng, self.s, self.n = eng, s, 0

            def __call__(self, ins):
                self.n += 1
                ins.then_inc(self.s, 1)
                self.eng.wait_ge(self.s, self.n)

        class Norm:

            def __init__(self, name, src, dst, n, eps, banks=(0, 1)):
                self.src, self.dst, self.n, self.eps, self.banks = src, dst, n, eps, banks
                self.chain = sem(name + "_chain")
                self.var_ready = sem(name + "_var_ready")
                self.rstd_ready = sem(name + "_rstd_ready")
                self.normed = sem(name + "_normed")
                self.turned = sem(name + "_turned")
                self.out = sem(name + "_out")

            def vector(self, dve):
                n = self.n
                link = Chain(dve, self.chain)
                st = stats[:, 0:n, :]
                for t in range(n):
                    ins = nc.vector.bn_stats(st[:, t, :], self.src[:, t, :])
                link(ins)
                me, se, mo, so = st[:, :, 1], st[:, :, 2], st[:, :, 4], st[:, :, 5]
                mean, diff, m2, sq, var = (small[:, i, 0:n] for i in range(5))
                link(nc.vector.tensor_tensor(mean, me, mo, ALU.add))
                link(nc.vector.tensor_tensor(diff, me, mo, ALU.subtract))
                link(nc.vector.tensor_tensor(m2, se, so, ALU.add))
                link(nc.vector.tensor_tensor(sq, diff, diff, ALU.mult))
                link(nc.vector.tensor_scalar(mean, mean, 0.5, None, ALU.mult))
                link(nc.vector.tensor_scalar(m2, m2, 1.0 / D, self.eps, ALU.mult, ALU.add))
                nc.vector.scalar_tensor_tensor(out=var, in0=sq, scalar=0.25, in1=m2, op0=ALU.mult,
                                               op1=ALU.add).then_inc(self.var_ready, 1)
                for g in range(n // 4):
                    dve.wait_ge(self.rstd_ready, g + 1)
                    for t in range(4 * g, 4 * g + 4):
                        ins = nc.vector.tensor_scalar(self.dst[:, t, :], self.src[:, t, :], small[:, 0, t:t + 1],
                                                      small[:, 5, t:t + 1], ALU.subtract, ALU.mult)
                    ins.then_inc(self.normed, 1)

            def gpsimd(self, pool):
                pool.wait_ge(self.var_ready, 1)
                for g in range(self.n // 4):
                    nc.gpsimd.tensor_tensor(small[:, 5, 4 * g:4 * g + 4], small[:, 4, 4 * g:4 * g + 4],
                                            neghalf[:, 0:4], ALU.pow).then_inc(self.rstd_ready, 1)

            def tensor(self, pe):
                for g in range(self.n // 4):
                    pe.wait_ge(self.normed, g + 1)
                    if g >= 2:
                        pe.wait_ge(self.out, g - 1)
                    for i in range(4):
                        ins = nc.tensor.transpose(ps[:, self.banks[g % 2], i * P:(i + 1) * P],
                                                  self.dst[:, 4 * g + i, :], ident)
                    ins.then_inc(self.turned, 1)

            def scalar(self, act):
                for g in range(self.n // 4):
                    act.wait_ge(self.turned, g + 1)
                    nc.scalar.copy(xT[:, g * CH:(g + 1) * CH], ps[:, self.banks[g % 2], :]).then_inc(self.out, 1)

        empty_zeroed = sem("empty_zeroed")
        empty_ready = sem("empty_ready")
        with nc.Block() as block:
            @block.sync
            def _(sp):
                sp.dma_start(x[:], io["x"].rearrange("a (t p) d -> p (a t) d", p=P)).then_inc(loaded, 16)
                sp.dma_start(cst[:], io["cst"]).then_inc(loaded, 16)
                for name, _ in WEIGHTS:
                    sp.dma_start(w[name][:], io[name]).then_inc(loaded, 16)
                sp.dma_start(w["lg2"][:], io["lg2"]).then_inc(loaded, 16)
                sp.dma_start(out_bias[:], io["out_b"].rearrange("(a n) -> a n", a=1).to_broadcast([P, D])).then_inc(loaded, 16)
                for i, name in enumerate(VECTORS):
                    sp.dma_start(vec[:, i:i + 1], io[name].rearrange("(n a) -> n a", a=1)).then_inc(loaded, 16)
                sp.wait_ge(loaded, 16 * LOADS)
                sp.wait_ge(empty_ready, len(empty))
                for rows in slots:
                    for a, b, src in empty:
                        sp.dma_start(rows[a * P:b * P, :].rearrange("(s p) c -> p s c", p=P), src).then_inc(slots_cleared, 16)

            @block.gpsimd
            def _(pool):
                for _, _, dst in empty:
                    ins = nc.gpsimd.memset(dst, 0.0).then_inc(empty_zeroed, 1)

            @block.vector
            def _(dve):
                nc.vector.memset(xt[:, 0:1], 0.0)
                nc.vector.memset(neghalf[:], -0.5)
                dve.wait_ge(loaded, 16 * LOADS)
                nc.vector.tensor_copy(identb, ident)
                nc.vector.tensor_copy(cstb[:, P:3 * P], cst[:, C_QMASK:C_QMASK + 2 * P])
                dve.wait_ge(empty_zeroed, len(empty))
                for a, b, dst in empty:
                    nc.vector.tensor_scalar(dst[:, :, D].bitcast(U32), count[:, TOP * NT + a:TOP * NT + b], float(P), row_number,
                                            ALU.mult, ALU.add).then_inc(empty_ready, 1)
        end_stage()

        def load_experts():
            with nc.Block() as block:
                @block.sync
                def _(sp):
                    sp.dma_start(w1[:], io["w1"].rearrange("e h f -> h e f")).then_inc(moe_loaded, 16)
                    sp.dma_start(w3[:], io["w3"].rearrange("e h f -> h e f")).then_inc(moe_loaded, 16)
                    sp.dma_start(w2[:], io["w2"].rearrange("e (t f) h -> f e t h", f=P)).then_inc(moe_loaded, 16)


        def attention_order(units, u0, m0, steps):
            FIRST, LEAD, RATE, SLOTS = 52, 2, 4.3, GH + 2
            plan, given, turned = [], 0, 0

            def give():
                nonlocal given, turned
                plan.append(("max", given))
                given += 1
                if turned < steps and given >= min(m0[turned + 1] + 3, m0[-1]):
                    plan.append(("turn max", turned))
                    turned += 1

            for _ in range(FIRST):
                give()
            owed = 0.0

            def slot(place):
                nonlocal owed
                need = [(m0[k + 1] + 4 - given) / (u0[k] - LEAD - place) for k in range(steps) if u0[k] - LEAD > place]
                owed += max([RATE] + need) / SLOTS
                while owed >= 1.0 and given < m0[-1]:
                    give()
                    owed -= 1.0

            for u, (k, kt, _) in enumerate(units):
                for j in range(GH):
                    plan.append(("scores", u, j))
                    slot(u + j / SLOTS)
                if u >= 1:
                    plan.append(("values", u - 1))
                slot(u + GH / SLOTS)
                if k >= 1 and kt == 1:
                    plan.append(("turn values", k - 1))
                slot(u + (GH + 1) / SLOTS)
            plan.append(("values", len(units) - 1))
            plan.append(("turn values", steps - 1))
            return plan

        def softmax_attention():
            QK = GH * T // 2
            Qs = [arena[:, 2 * b * QK:(2 * b + 1) * QK].bitcast(BF16).rearrange("p (j t) -> p j t", j=GH) for b in (0, 1)]
            Ks = [arena[:, (2 * b + 1) * QK:(2 * b + 2) * QK].bitcast(BF16).rearrange("p (j t) -> p j t", j=GH) for b in (0, 1)]
            at = 4 * QK
            probs = arena[:, at:at + 2 * GH * CH].rearrange("p (b j q) -> p b j q", b=2, j=GH)
            at += 2 * GH * CH
            qk = arena[:, 0:2 * NT * D].rearrange("p (n d) -> p n d", d=D)
            qkn = arena[:, 2 * NT * D:4 * NT * D].rearrange("p (n d) -> p n d", d=D)
            feat = arena[:, 4 * NT * D:6 * NT * D].rearrange("p (s t) -> p s t", s=2)
            parts = arena[:, 6 * NT * D:9 * NT * D].bitcast(BF16).rearrange("p (s r t) -> p s r t", s=2, r=PARTS)
            rest = arena[:, 9 * NT * D:9 * NT * D + 2 * T].rearrange("p (s t) -> p s t", s=2)
            ctxt = xn
            with ExitStack() as mem:
                def own(name, shape, dt=FP32):
                    return mem.enter_context(nc.sbuf_tensor(name, shape, dt))

                spare = w1[:].rearrange("p e f -> p (e f)")
                nv = NT * H * (HD + 1)
                vaug = spare[:, 0:nv].rearrange("p (t h d) -> p t h d", t=NT, h=H)
                osb = spare[:, nv:nv + 2 * CH].rearrange("p (b q) -> p b q", b=2)
                vg = w3[:].rearrange("p e f -> p (e f)").rearrange("p (b t j m) -> p b t j m", b=2, t=NT, j=GH)
                qscaled = own("qscaled", [P, 1])
                rec = own("rec", [P, 2, TPC, GH])
                mpart = own("mpart", [P, GH, TPC, NC])
                negmax = own("negmax", [P, 2, GH, TPC])
                mwide = own("mwide", [P, GH, P // GH], BF16)
                mparts = mwide[:, :, 0:PARTS * TPC].rearrange("p j (r t) -> p j r t", r=PARTS)
                ones = own("ones", [PARTS, T], BF16)
                mrow = own("mrow", [P, P], BF16)

                norm = Norm("a0", x, xn, NT, 1e-5)
                qkn_norm = Norm("a1", qk, qkn, 2 * NT, 1e-6, banks=(6, 7))
                projected = sem("a_projected")
                split_out = sem("a_split_out")
                v_out = sem("a_v_out")
                scaled = sem("a_scaled")
                with nc.Block() as block:
                    @block.vector
                    def _(dve):
                        dve.wait_ge(loaded, 16 * LOADS)
                        nc.vector.tensor_scalar(qscaled[:], col["q_scale"], float(HD) ** -0.5, None, ALU.mult).then_inc(scaled, 1)
                        norm.vector(dve)
                        for t in range(NT):
                            dve.wait_ge(projected, t + 1)
                            dve.wait_ge(split_out, t + 1)
                            nc.vector.tensor_copy(vaug[:, t, :, 0:HD],
                                                  ps[:, 2 + t % 4, 2 * D:3 * D].rearrange("p (h d) -> p h d", h=H)).then_inc(v_out, 1)

                    @block.gpsimd
                    def _(pool):
                        nc.gpsimd.memset(vaug[:, :, :, HD:HD + 1], 1.0)
                        norm.gpsimd(pool)

                    @block.tensor
                    def _(pe):
                        pe.wait_ge(loaded, 16 * LOADS)
                        norm.tensor(pe)
                        for t in range(NT):
                            pe.wait_ge(norm.out, t // TPC + 1)
                            if t >= 4:
                                pe.wait_ge(v_out, t - 3)
                            nc.tensor.matmul(ps[:, 2 + t % 4, 0:3 * D], xT[:, t * P:(t + 1) * P], w["qkv"][:],
                                             start=True, stop=True).then_inc(projected, 1)

                    @block.scalar
                    def _(act):
                        norm.scalar(act)
                        for t in range(NT):
                            act.wait_ge(projected, t + 1)
                            nc.scalar.copy(qk.rearrange("p (s t) d -> p s t d", s=2)[:, :, t, :],
                                           ps[:, 2 + t % 4, 0:2 * D].rearrange("p (s d) -> p s d", s=2)).then_inc(split_out, 1)

                high = sem("a_high")
                mid = sem("a_mid")
                rest_ready = sem("a_rest_ready")
                low = sem("a_low")
                stored = sem("a_stored")
                with nc.Block() as block:
                    @block.vector
                    def _(dve):
                        qkn_norm.vector(dve)
                        link = Chain(dve, sem("a_split_chain"))
                        for s in range(2):
                            for c in range(NC):
                                g = s * NC + c
                                o = slice(c * CH, (c + 1) * CH)
                                dve.wait_ge(high, g + 1)
                                nc.vector.tensor_tensor(rest[:, s, o], feat[:, s, o], parts[:, s, 0, o],
                                                        ALU.subtract).then_inc(rest_ready, 1)
                                dve.wait_ge(mid, g + 1)
                                nc.vector.tensor_tensor(parts[:, s, 2, o], rest[:, s, o], parts[:, s, 1, o],
                                                        ALU.subtract).then_inc(low, 1)

                    @block.gpsimd
                    def _(pool):
                        qkn_norm.gpsimd(pool)

                    @block.tensor
                    def _(pe):
                        qkn_norm.tensor(pe)

                    @block.scalar
                    def _(act):
                        act.wait_ge(scaled, 1)
                        for g in range(2 * NC):
                            s, c = g // NC, g % NC
                            o = slice(c * CH, (c + 1) * CH)
                            act.wait_ge(qkn_norm.turned, g + 1)
                            nc.scalar.mul(feat[:, s, o], ps[:, 6 + g % 2, :],
                                          qscaled[:, 0:1] if s == 0 else col["k_scale"]).then_inc(qkn_norm.out, 1)
                            act.wait_ge(qkn_norm.out, g + 1)
                            nc.scalar.copy(parts[:, s, 0, o], feat[:, s, o]).then_inc(high, 1)
                            act.wait_ge(rest_ready, g + 1)
                            nc.scalar.copy(parts[:, s, 1, o], rest[:, s, o]).then_inc(mid, 1)

                    @block.sync
                    def _(sp):
                        for s, dst, n in ((0, q_parts, PARTS), (1, k_parts, 2 * PARTS - 1)):
                            sp.wait_ge(low, NC * (s + 1))
                            for r in range(n):
                                sp.dma_start(dst[:, r],
                                             parts[:, s, r % PARTS, :]).then_inc(stored, 16)
                        sp.wait_ge(stored, 16 * (3 * PARTS - 1))

                STEPS = [(0, 0), (0, 1), (0, 2), (0, 3), (1, 3), (1, 2), (1, 1), (1, 0)]
                UNITS = [TPC * (c + 1) for _, c in STEPS]
                CHUNKS = [GH * TPC * (c + 1) for _, c in STEPS]
                NU, NM, NS = sum(UNITS), sum(CHUNKS), len(STEPS)
                u0 = [sum(UNITS[:k]) for k in range(NS + 1)]
                m0 = [sum(CHUNKS[:k]) for k in range(NS + 1)]
                MAXIMA = [(k, t, j, kc, CH if kc < c else (t + 1) * P) for k, (_, c) in enumerate(STEPS)
                          for t in range(TPC) for j in range(GH) for kc in range(c + 1)]
                UNIT = [(k, kt, max(0, (kt - c * TPC) * P)) for k, (_, c) in enumerate(STEPS) for kt in range(UNITS[k])]
                PLAN = attention_order(UNIT, u0, m0, NS)
                RING = {(p[0], p[1]): m for m, p in enumerate(p for p in PLAN if p[0] in ("max", "turn max", "turn values"))}

                ones_set = sem("a_ones_set")
                cleared = [sem("a_cleared_q"), sem("a_cleared_k")]
                ones_loaded = sem("a_ones_loaded")
                first_loaded = sem("a_first_loaded")
                mark = len(stage_sems)
                stack_loaded = sem("a_stack_loaded")
                next_loaded = sem("a_next_loaded")
                vg_ready = sem("a_vg_ready")
                ring_ready = sem("a_ring_ready")
                ring_read = sem("a_ring_read")
                max_split = sem("a_max_split")
                max_set = sem("a_max_set")
                st_ready = sem("a_st_ready")
                exp_done = sem("a_exp_done")
                pv_done = sem("a_pv_done")
                o_out = sem("a_o_out")
                split_link = sem("a_split_link")
                keep_link = sem("a_keep_link")
                rows_cleared = sem("a_rows_cleared")
                body_sems = stage_sems[mark:]
                ST, S, O = 0, 4, 7
                DEPTH = 3

                def load(sp, g, b, loaded_sem):
                    for j in range(GH):
                        sp.dma_start(Qs[b][0:KROWS, j, :], bass.AP(
                            tensor=q_parts.tensor, offset=g * (GH * PARTS * HD * T) + j * PARTS * HD * T,
                            ap=[[0, PARTS], [T, PARTS * HD], [1, T]])).then_inc(loaded_sem, 16)
                        sp.dma_start(Ks[b][0:KROWS, j, :], bass.AP(
                            tensor=k_parts.tensor, offset=g * (GH * (2 * PARTS - 1) * HD * T) + j * (2 * PARTS - 1) * HD * T,
                            ap=[[HD * T, PARTS], [T, PARTS * HD], [1, T]])).then_inc(loaded_sem, 16)

                with nc.Block() as block:
                    @block.sync
                    def _(sp):
                        sp.wait_ge(cleared[0], 2)
                        sp.wait_ge(cleared[1], 2)
                        sp.wait_ge(slots_cleared, 16 * len(empty) * len(slots))
                        load(sp, 0, 0, first_loaded)
                        sp.wait_ge(ones_set, 1)
                        for b in (0, 1):
                            for j in range(GH):
                                sp.dma_start(Ks[b][MROW:MROW + PARTS, j, :], ones[:]).then_inc(ones_loaded, 16)
                        sp.wait_ge(ones_loaded, 16 * 2 * GH)
                        sp.wait_ge(first_loaded, 16 * 2 * GH)

                    @block.gpsimd
                    def _(pool):
                        for b in (0, 1):
                            nc.gpsimd.memset(Ks[b][64:P].bitcast(FP32), 0.0).then_inc(cleared[1], 1)
                            pool.wait_ge(cleared[1], b + 1)
                        nc.gpsimd.memset(ones[:], 1.0).then_inc(ones_set, 1)

                    @block.vector
                    def _(dve):
                        for b in (0, 1):
                            nc.vector.memset(Qs[b][64:P].bitcast(FP32), 0.0).then_inc(cleared[0], 1)
                        nc.vector.memset(mwide[:], 0.0)
                        nc.vector.memset(vg, 0.0)

                with nc.Fori(0, 2) as i:
                    with nc.Block() as block:
                        @block.sync
                        def _(sp):
                            def set_maxima(k):
                                b, c = STEPS[k]
                                n = k + 1
                                if k == 4:
                                    sp.wait_ge(rows_cleared, 1)
                                sp.wait_ge(ring_read, RING["turn max", k] + 1)
                                for j in range(GH):
                                    sp.dma_start(Qs[b][MROW:MROW + PARTS, j, c * CH:(c + 1) * CH],
                                                 mrow[j * P // GH:j * P // GH + PARTS * TPC, :]).then_inc(max_set, 16)
                                sp.wait_ge(max_set, 16 * GH * n)

                            load(sp, i * 2 + 1, 1, stack_loaded)
                            for k in range(NS):
                                set_maxima(k)
                            sp.wait_ge(pv_done, u0[4])
                            load(sp, 2 - i * 2, 0, next_loaded)
                            sp.wait_ge(next_loaded, 16 * 2 * GH)

                        @block.gpsimd
                        def _(pool):
                            nc.gpsimd.memset(Qs[1][MROW:P].bitcast(FP32), 0.0).then_inc(rows_cleared, 1)
                            pool.wait_ge(rows_cleared, 1)
                            for b in (0, 1):
                                nc.gpsimd.tensor_copy(vg[:, b, :, :, 0:HD + 1],
                                                      vaug[:, :, bass.ds(i * (2 * GH) + b * GH, GH), :]).then_inc(vg_ready, 1)
                            pool.wait_ge(pv_done, u0[4])
                            pool.wait_ge(vg_ready, 2)
                            nc.gpsimd.memset(Qs[0][MROW:P].bitcast(FP32), 0.0).then_inc(rows_cleared, 1)

                        def keep_values(dve, k):
                            b, c = STEPS[k]
                            m = RING["turn values", k]
                            dve.wait_ge(ring_ready, m + 1)
                            o = ps[:, S + m % DEPTH, :].rearrange("p (t j m) -> p t j m", t=TPC, j=GH)
                            nc.vector.reciprocal(rec[:, k % 2], o[:, :, :, HD]).then_inc(keep_link, 1)
                            dve.wait_ge(keep_link, k + 1)
                            for t in range(TPC):
                                ins = nc.vector.tensor_tensor(
                                    ctxt[:, c * TPC + t, bass.ds(i * (2 * GH * HD) + b * GH * HD, GH * HD)].rearrange("p (j d) -> p j d", j=GH),
                                    o[:, t, :, 0:HD],
                                    rec[:, k % 2, t].rearrange("p (j a) -> p j a", a=1).to_broadcast([P, GH, HD]), ALU.mult)
                            ins.then_inc(ring_read, 1)

                        def split_maxima(dve, k):
                            c = STEPS[k][1]
                            m, r1 = negmax[:, 0], negmax[:, 1]
                            dve.wait_ge(ring_read, RING["max", m0[k + 1] - 1] + 1)
                            nc.vector.tensor_reduce(out=m, in_=mpart[:, :, :, 0:c + 1],
                                                    axis=AX.X, op=ALU.max, negate=True).then_inc(split_link, 1)
                            dve.wait_ge(split_link, 4 * k + 1)
                            if k >= 1:
                                dve.wait_ge(ring_ready, RING["turn max", k - 1] + 1)
                            nc.vector.tensor_copy(mparts[:, :, 0, :], m).then_inc(split_link, 1)
                            dve.wait_ge(split_link, 4 * k + 2)
                            nc.vector.tensor_tensor(r1, m, mparts[:, :, 0, :], ALU.subtract).then_inc(split_link, 1)
                            dve.wait_ge(split_link, 4 * k + 3)
                            nc.vector.tensor_copy(mparts[:, :, 1, :], r1).then_inc(split_link, 1)
                            dve.wait_ge(split_link, 4 * k + 4)
                            nc.vector.tensor_tensor(mparts[:, :, 2, :], r1, mparts[:, :, 1, :], ALU.subtract).then_inc(max_split, 1)

                        @block.vector
                        def _(dve):
                            for what, n, *_ in PLAN:
                                if what == "max":
                                    k, t, j, kc, width = MAXIMA[n]
                                    m = RING[what, n]
                                    dve.wait_ge(ring_ready, m + 1)
                                    nc.vector.tensor_reduce(out=mpart[:, j, t, kc:kc + 1], in_=ps[:, S + m % DEPTH, 0:width],
                                                            axis=AX.X, op=ALU.max).then_inc(ring_read, 1)
                                    if n + 1 == m0[k + 1]:
                                        split_maxima(dve, k)
                                if what == "turn max":
                                    m = RING[what, n]
                                    dve.wait_ge(ring_ready, m + 1)
                                    if n >= 1:
                                        dve.wait_ge(max_set, 16 * GH * n)
                                    nc.vector.tensor_copy(mrow[:], ps[:, S + m % DEPTH, 0:P // 2].bitcast(BF16)).then_inc(ring_read, 1)
                                if what == "turn values":
                                    keep_values(dve, n)

                        @block.tensor
                        def _(pe):
                            def free_bank(what, n):
                                m = RING[what, n]
                                if m >= DEPTH:
                                    pe.wait_ge(ring_read, m - DEPTH + 1)
                                return m

                            def scores_for_max(n):
                                k, t, j, kc, width = MAXIMA[n]
                                b, c = STEPS[k]
                                if n == m0[4]:
                                    pe.wait_ge(stack_loaded, 16 * 2 * GH)
                                    pe.wait_ge(rows_cleared, 1)
                                m = free_bank("max", n)
                                out = ps[:, S + m % DEPTH, 0:width]
                                ins = nc.tensor.matmul(out, Qs[b][:, j, (c * TPC + t) * P:(c * TPC + t + 1) * P],
                                                       Ks[b][:, j, kc * CH:kc * CH + width], start=True, stop=kc < c)
                                if kc == c:
                                    ins = nc.tensor.matmul(out[:, width - P:width], identb, qmask, start=False, stop=True)
                                ins.then_inc(ring_ready, 1)

                            def scores(u, j):
                                k, kt, off = UNIT[u]
                                b, c = STEPS[k]
                                if kt == 0 and j == 0:
                                    pe.wait_ge(max_set, 16 * GH * (k + 1))
                                if u >= 1:
                                    pe.wait_ge(exp_done, GH * (u - 1) + j + 1)
                                diagonal = kt >= c * TPC
                                ins = nc.tensor.matmul(ps[:, ST + j, off:CH], Ks[b][:, j, kt * P:(kt + 1) * P],
                                                       Qs[b][:, j, c * CH + off:(c + 1) * CH], start=True, stop=not diagonal)
                                if diagonal:
                                    ins = nc.tensor.matmul(ps[:, ST + j, off:off + P], identb, kmask, start=False, stop=True)
                                ins.then_inc(st_ready, 1)

                            def values(u):
                                k, kt, off = UNIT[u]
                                b = STEPS[k][0]
                                pe.wait_ge(exp_done, GH * (u + 1))
                                pe.wait_ge(vg_ready, b + 1)
                                if kt == 0 and k >= 1:
                                    pe.wait_ge(o_out, k)
                                for j in range(GH):
                                    ins = nc.tensor.matmul(ps[32 * j:32 * j + 32, O, off:CH], vg[:, b, kt, j, :],
                                                           probs[:, u % 2, j, off:CH], start=kt == 0, stop=kt == UNITS[k] - 1)
                                ins.then_inc(pv_done, 1)

                            for what, n, *j in PLAN:
                                if what == "max":
                                    scores_for_max(n)
                                if what == "scores":
                                    scores(n, j[0])
                                if what == "values":
                                    values(n)
                                if what == "turn max":
                                    pe.wait_ge(max_split, n + 1)
                                    m = free_bank(what, n)
                                    nc.tensor.transpose(ps[:, S + m % DEPTH, 0:P // 2].bitcast(BF16),
                                                        mwide[:].rearrange("p j m -> p (j m)"), identb).then_inc(ring_ready, 1)
                                if what == "turn values":
                                    pe.wait_ge(o_out, n + 1)
                                    m = free_bank(what, n)
                                    for t in range(TPC):
                                        ins = nc.tensor.transpose(ps[:, S + m % DEPTH, t * P:(t + 1) * P],
                                                                  osb[:, n % 2, t * P:(t + 1) * P], ident)
                                    ins.then_inc(ring_ready, 1)

                        @block.scalar
                        def _(act):
                            for what, n, *j in PLAN:
                                if what == "scores":
                                    k, kt, off = UNIT[n]
                                    if n >= 2 and j[0] == 0:
                                        act.wait_ge(pv_done, n - 1)
                                    act.wait_ge(st_ready, GH * n + j[0] + 1)
                                    nc.scalar.activation(probs[:, n % 2, j[0], off:CH], ps[:, ST + j[0], off:CH],
                                                         ACT.Exp).then_inc(exp_done, 1)
                                if what == "values":
                                    k = UNIT[n][0]
                                    if n + 1 == u0[k + 1]:
                                        act.wait_ge(pv_done, n + 1)
                                        if k >= 2:
                                            act.wait_ge(ring_ready, RING["turn values", k - 2] + 1)
                                        nc.scalar.copy(osb[:, k % 2, :], ps[:, O, :]).then_inc(o_out, 1)

                    with nc.Block() as block:
                        @block.gpsimd
                        def _(pool):
                            for s in body_sems:
                                pool.sem_clear(s)

                project_out("a_out", ctxt, w["wout"], None)

        def project_out(name, src, weight, source_norm):
            turned = sem(name + "_turned")
            copied = sem(name + "_copied")
            product = sem(name + "_product")
            added = sem(name + "_added")
            with nc.Block() as block:
                @block.tensor
                def _(pe):
                    for g in range(NC):
                        if g >= 2:
                            pe.wait_ge(copied, g - 1)
                        for t in range(TPC):
                            ins = nc.tensor.transpose(ps[:, g % 2, t * P:(t + 1) * P], src[:, g * TPC + t, :], ident)
                        ins.then_inc(turned, 1)
                    for g in range(NC):
                        pe.wait_ge(copied, g + 1)
                        if g >= 2:
                            pe.wait_ge(added, g - 1)
                        for t in range(TPC):
                            ins = nc.tensor.matmul(ps[:, 2 + g % 2, t * P:(t + 1) * P],
                                                   xT[:, (g * TPC + t) * P:(g * TPC + t + 1) * P], weight[:], start=True, stop=True)
                        ins.then_inc(product, 1)

                @block.scalar
                def _(act):
                    for g in range(NC):
                        act.wait_ge(turned, g + 1)
                        nc.scalar.copy(xT[:, g * CH:(g + 1) * CH], ps[:, g % 2, :]).then_inc(copied, 1)

                @block.vector
                def _(dve):
                    for g in range(NC):
                        dve.wait_ge(product, g + 1)
                        xs = x[:, g * TPC:(g + 1) * TPC, :].rearrange("p t d -> p (t d)")
                        nc.vector.tensor_tensor(xs, ps[:, 2 + g % 2, :], xs, ALU.add).then_inc(added, 1)

        def channel_mix(name):
            xr = arena[:, 0:T]
            xk = arena[:, T:2 * T]
            diff = arena[:, 2 * T:3 * T]
            rk = arena[:, 3 * T:4 * T]
            ka = arena[:, 4 * T:5 * T]
            r = arena[:, 5 * T:6 * T]
            rv = arena[:, 6 * T:7 * T]
            norm = Norm(name, x, xn, NT, 1e-5)
            differed = sem(name + "_differed")
            mixed_r = sem(name + "_mixed_r")
            k_ready = sem(name + "_k_ready")
            k_relu = sem(name + "_k_relu")
            k_squared = sem(name + "_k_squared")
            r_ready = sem(name + "_r_ready")
            r_out = sem(name + "_r_out")
            v_ready = sem(name + "_v_ready")
            gated = sem(name + "_gated")
            with nc.Block() as block:
                @block.vector
                def _(dve):
                    norm.vector(dve)
                    for c in range(NC):
                        o = slice(c * CH, (c + 1) * CH)
                        dve.wait_ge(differed, c + 1)
                        nc.vector.scalar_tensor_tensor(out=xk[:, o], in0=diff[:, o], scalar=col["mu_k"], in1=xt[:, o],
                                                       op0=ALU.mult, op1=ALU.add)
                        nc.vector.scalar_tensor_tensor(out=xr[:, o], in0=diff[:, o], scalar=col["mu_r"], in1=xt[:, o],
                                                       op0=ALU.mult, op1=ALU.add).then_inc(mixed_r, 1)
                    for c in range(NC):
                        o = slice(c * CH, (c + 1) * CH)
                        dve.wait_ge(v_ready, c + 1)
                        dve.wait_ge(r_out, c + 1)
                        nc.vector.tensor_tensor(rv[:, o], ps[:, 6 + c % 2, :], r[:, o], ALU.mult).then_inc(gated, 1)
                        dve.wait_ge(gated, c + 1)
                        xs = x[:, c * TPC:(c + 1) * TPC, :].rearrange("p t d -> p (t d)")
                        nc.vector.tensor_tensor(xs, rv[:, o], xs, ALU.add)

                @block.gpsimd
                def _(pool):
                    norm.gpsimd(pool)
                    for c in range(NC):
                        pool.wait_ge(norm.out, c + 1)
                        nc.gpsimd.tensor_tensor(diff[:, c * CH:(c + 1) * CH], xT[:, c * CH:(c + 1) * CH],
                                                xt[:, c * CH:(c + 1) * CH], ALU.subtract).then_inc(differed, 1)
                    for c in range(NC):
                        o = slice(c * CH, (c + 1) * CH)
                        pool.wait_ge(k_relu, c + 1)
                        nc.gpsimd.tensor_tensor(ka[:, o], rk[:, o], rk[:, o], ALU.mult).then_inc(k_squared, 1)

                @block.scalar
                def _(act):
                    norm.scalar(act)
                    for c in range(NC):
                        o = slice(c * CH, (c + 1) * CH)
                        act.wait_ge(k_ready, c + 1)
                        nc.scalar.activation(rk[:, o], ps[:, 2 + c % 2, :], ACT.Relu).then_inc(k_relu, 1)
                        act.wait_ge(r_ready, c + 1)
                        nc.scalar.activation(r[:, o], ps[:, 4 + c % 2, :], ACT.Sigmoid).then_inc(r_out, 1)

                @block.tensor
                def _(pe):
                    norm.tensor(pe)

                    def value(c):
                        pe.wait_ge(k_squared, c + 1)
                        if c >= 2:
                            pe.wait_ge(gated, c - 1)
                        for t in range(TPC):
                            ins = nc.tensor.matmul(ps[:, 6 + c % 2, t * P:(t + 1) * P],
                                                   ka[:, c * CH + t * P:c * CH + (t + 1) * P], w["wv"][:], start=True, stop=True)
                        ins.then_inc(v_ready, 1)

                    for c in range(NC):
                        pe.wait_ge(mixed_r, c + 1)
                        if c >= 2:
                            pe.wait_ge(k_relu, c - 1)
                        nc.tensor.matmul(ps[:, 2 + c % 2, :], w["wk"][:], xk[:, c * CH:(c + 1) * CH],
                                         start=True, stop=True).then_inc(k_ready, 1)
                        if c >= 2:
                            pe.wait_ge(r_out, c - 1)
                        for t in range(TPC):
                            ins = nc.tensor.matmul(ps[:, 4 + c % 2, t * P:(t + 1) * P],
                                                   xr[:, c * CH + t * P:c * CH + (t + 1) * P], w["wr"][:], start=True, stop=True)
                        ins.then_inc(r_ready, 1)
                        if c >= 1:
                            value(c - 1)
                    value(NC - 1)

        def linear_attention(name, kind):
            wq, wk, wv = {"gated": ("hq", "hk", "hv"), "retention": ("rq", "rk", "rv"), "lightning": ("lq", "lk", "lv")}[kind]
            at = [0]

            def take(words):
                at[0] += words
                return arena[:, at[0] - words:at[0]]

            q = take(2 * CH).rearrange("p (b t) -> p b t", b=2)
            k = take(2 * CH).rearrange("p (b t) -> p b t", b=2)
            dec = take(2 * CH).rearrange("p (b t) -> p b t", b=2)
            vs = take(2 * CH).rearrange("p (b t) -> p b t", b=2)
            upd = take(2 * CH).rearrange("p (b t) -> p b t", b=2)
            state = take(2 * HD * CH).rearrange("p (b e t) -> p b e t", b=2, e=HD)
            z = take(HD * CH).rearrange("p (e t) -> p e t", e=HD)
            vrep = take(HD * P).rearrange("p (e h d) -> p e h d", e=HD, h=H)
            orep = take(HD * P).rearrange("p (e m) -> p e m", e=HD)
            y = take(T)
            gate = take(T)
            g1 = take(2 * CH)[0:HD, :].rearrange("p (b t) -> p b t", b=2)
            negb = take(1)
            norm = Norm(name, x, xn, NT, 1e-5)
            rep_ready = sem(name + "_rep_ready")
            kq_ready = sem(name + "_kq_ready")
            kq_out = sem(name + "_kq_out")
            v_ready = sem(name + "_v_ready")
            v_out = sem(name + "_v_out")
            upd_ready = sem(name + "_upd_ready")
            scanned = sem(name + "_scanned")
            z_ready = sem(name + "_z_ready")
            summed = sem(name + "_summed")
            sum_out = sem(name + "_sum_out")
            g_ready = sem(name + "_g_ready")
            g_out = sem(name + "_g_out")
            gate_ready = sem(name + "_gate_ready")
            gate_out = sem(name + "_gate_out")
            orep_loaded = sem(name + "_orep_loaded")
            if kind == "gated":
                reduce_w = orep
            else:
                reduce_w = pick
            with nc.Block() as block:
                @block.gpsimd
                def _(pool):
                    wvT = w[wv][:].rearrange("p (h e) -> p h e", e=HD)
                    for e in range(HD):
                        nc.gpsimd.tensor_copy(vrep[:, e], wvT[:, :, e:e + 1].to_broadcast([P, H, HD])).then_inc(rep_ready, 1)
                    if kind == "gated":
                        nc.gpsimd.tensor_scalar(negb, col["key_b"], -1.0, None, ALU.mult).then_inc(rep_ready, 1)
                    norm.gpsimd(pool)
                    for c in range(NC):
                        for e in range(HD):
                            n = c * HD + e
                            pool.wait_ge(scanned, n + 1)
                            if e == 0:
                                pool.wait_ge(kq_out, 2 * c + 2)
                                if c >= 1:
                                    pool.wait_ge(summed, c)
                            nc.gpsimd.tensor_tensor(z[:, e, :], state[:, c % 2, e, :], q[:, c % 2, :], ALU.mult).then_inc(z_ready, 1)

                def add(dve, c):
                    dve.wait_ge(summed, c + 1)
                    xs = x[:, c * TPC:(c + 1) * TPC, :]
                    nc.vector.tensor_tensor(xs, ps[:, 6 + c % 2, :].rearrange("p (t d) -> p t d", d=D), xs, ALU.add).then_inc(sum_out, 1)
                    dve.wait_ge(sum_out, c + 1)
                    nc.vector.tensor_tensor(xs, xs, out_bias[:].rearrange("p (a d) -> p a d", a=1).to_broadcast([P, TPC, D]), ALU.add)

                @block.vector
                def _(dve):
                    norm.vector(dve)
                    for c in range(NC):
                        for e in range(HD):
                            n = c * HD + e
                            if kind == "lightning":
                                dve.wait_ge(v_out, n + 1)
                                v_in = vs[:, n % 2, :]
                            else:
                                dve.wait_ge(v_ready, n + 1)
                                v_in = ps[:, 4 + n % 2, :]
                            dve.wait_ge(kq_out, 2 * c + 1)
                            nc.vector.tensor_tensor(upd[:, n % 2, :], v_in, k[:, c % 2, :], ALU.mult).then_inc(upd_ready, 1)
                            dve.wait_ge(upd_ready, n + 1)
                            if c >= 2:
                                dve.wait_ge(z_ready, n - 2 * HD + 1)
                            if c >= 1:
                                dve.wait_ge(scanned, n - HD + 1)
                            a = dec[:, c % 2, :] if kind == "gated" else \
                                cst[:, C_RET if kind == "retention" else C_LT:][:, 0:1].to_broadcast([P, CH])
                            nc.vector.tensor_tensor_scan(
                                out=state[:, c % 2, e, :], data0=a, data1=upd[:, n % 2, :],
                                initial=0.0 if c == 0 else state[:, 1 - c % 2, e, CH - 1:CH],
                                op0=ALU.mult, op1=ALU.add).then_inc(scanned, 1)
                        if kind == "gated" and c >= 1:
                            add(dve, c - 1)
                    if kind == "gated":
                        add(dve, NC - 1)

                def copy_out(act, c):
                    act.wait_ge(summed, c + 1)
                    nc.scalar.copy(y[:, c * CH:(c + 1) * CH], ps[:, 6 + c % 2, :]).then_inc(sum_out, 1)

                @block.scalar
                def _(act):
                    norm.scalar(act)
                    for c in range(NC):
                        act.wait_ge(kq_ready, 2 * c + 1)
                        if c >= 2:
                            act.wait_ge(z_ready, (c - 1) * HD)
                        pk = ps[:, 2, :]
                        if kind == "gated":
                            nc.scalar.activation(dec[:, c % 2, :], pk, ACT.Sigmoid, bias=col["key_b"])
                            if c == 0:
                                act.wait_ge(rep_ready, HD + 1)
                            nc.scalar.activation(k[:, c % 2, :], pk, ACT.Sigmoid, bias=negb, scale=-1.0).then_inc(kq_out, 1)
                        elif kind == "retention":
                            nc.scalar.copy(k[:, c % 2, :], pk).then_inc(kq_out, 1)
                        else:
                            nc.scalar.activation(k[:, c % 2, :], pk, ACT.Silu).then_inc(kq_out, 1)
                        act.wait_ge(kq_ready, 2 * c + 2)
                        pq = ps[:, 3, :]
                        if kind == "gated":
                            nc.scalar.copy(q[:, c % 2, :], pq).then_inc(kq_out, 1)
                        elif kind == "retention":
                            nc.scalar.mul(q[:, c % 2, :], pq, float(HD) ** -0.5).then_inc(kq_out, 1)
                        else:
                            nc.scalar.activation(q[:, c % 2, :], pq, ACT.Silu).then_inc(kq_out, 1)
                            for e in range(HD):
                                n = c * HD + e
                                act.wait_ge(v_ready, n + 1)
                                if n >= 2:
                                    act.wait_ge(upd_ready, n - 1)
                                nc.scalar.activation(vs[:, n % 2, :], ps[:, 4 + n % 2, :], ACT.Silu).then_inc(v_out, 1)
                        if kind != "gated" and c >= 1:
                            copy_out(act, c - 1)
                    if kind != "gated":
                        copy_out(act, NC - 1)
                    if kind == "lightning":
                        for c in range(NC):
                            act.wait_ge(g_ready, c + 1)
                            nc.scalar.copy(g1[:, c % 2, :], ps[0:HD, 2, :]).then_inc(g_out, 1)
                            act.wait_ge(gate_ready, c + 1)
                            nc.scalar.activation(gate[:, c * CH:(c + 1) * CH], ps[:, 3, :], ACT.Sigmoid).then_inc(gate_out, 1)

                @block.tensor
                def _(pe):
                    norm.tensor(pe)
                    pe.wait_ge(rep_ready, HD)
                    if kind == "gated":
                        pe.wait_ge(orep_loaded, 16 * HD)

                    def total(c):
                        pe.wait_ge(z_ready, (c + 1) * HD)
                        if c >= 2:
                            pe.wait_ge(sum_out, c - 1)
                        if kind == "retention":
                            for e in range(HD):
                                ins = nc.tensor.matmul(ps[:, 6 + c % 2, :], reduce_w[:, e, :], z[:, e, :],
                                                       start=e == 0, stop=e == HD - 1)
                        else:
                            for t in range(TPC):
                                for e in range(HD):
                                    ins = nc.tensor.matmul(ps[:, 6 + c % 2, t * P:(t + 1) * P], z[:, e, t * P:(t + 1) * P],
                                                           reduce_w[:, e, :], start=e == 0, stop=e == HD - 1)
                        ins.then_inc(summed, 1)

                    for c in range(NC):
                        o = slice(c * CH, (c + 1) * CH)
                        pe.wait_ge(norm.out, c + 1)
                        if c >= 1:
                            pe.wait_ge(kq_out, 2 * c - 1)
                        nc.tensor.matmul(ps[:, 2, :], w[wk][:], xT[:, o], start=True, stop=True).then_inc(kq_ready, 1)
                        if c >= 1:
                            pe.wait_ge(kq_out, 2 * c)
                        nc.tensor.matmul(ps[:, 3, :], w[wq][:], xT[:, o], start=True, stop=True).then_inc(kq_ready, 1)
                        for e in range(HD):
                            n = c * HD + e
                            if n >= 2:
                                pe.wait_ge(v_out if kind == "lightning" else upd_ready, n - 1)
                            nc.tensor.matmul(ps[:, 4 + n % 2, :], vrep[:, e].rearrange("p h d -> p (h d)"), xT[:, o],
                                             start=True, stop=True).then_inc(v_ready, 1)
                        if c >= 1:
                            total(c - 1)
                    total(NC - 1)
                    if kind == "lightning":
                        for c in range(NC):
                            if c == 0:
                                pe.wait_ge(kq_out, 2 * NC)
                            else:
                                pe.wait_ge(g_out, c)
                            nc.tensor.matmul(ps[0:HD, 2, :], w["lg1"][:], xT[:, c * CH:(c + 1) * CH], start=True, stop=True).then_inc(g_ready, 1)
                            pe.wait_ge(g_out, c + 1)
                            if c >= 1:
                                pe.wait_ge(gate_out, c)
                            nc.tensor.matmul(ps[:, 3, :], w["lg2"][:], g1[:, c % 2, :], start=True, stop=True).then_inc(gate_ready, 1)

                @block.sync
                def _(sp):
                    if kind == "gated":
                        for e in range(HD):
                            sp.dma_start(orep[:, e, :], bass.AP(tensor=io["ho"].tensor, offset=e * D,
                                                                ap=[[HD * D, H], [0, HD], [1, D]])).then_inc(orep_loaded, 16)

            if kind == "retention":
                retention_out(name, y, z)
            if kind == "lightning":
                lightning_out(name, y, gate)

        def retention_out(name, y, z):
            yn = z.rearrange("p e t -> p (e t)")[:, 0:T]
            st = stats[:, 0:NC, :]
            mv, dev, sc = small[:, 0, 0:2], small[:, 1, 0:3], small[:, 2, 0:8]
            link_sem = sem(name + "_gn_link")
            stat_ready = sem(name + "_gn_stat")
            head_mean_ready = sem(name + "_gn_mean")
            dev_ready = sem(name + "_gn_dev")
            head_var_ready = sem(name + "_gn_var")
            var_ready = sem(name + "_gn_vareps")
            rstd_ready = sem(name + "_gn_rstd")
            normed = sem(name + "_gn_normed")
            product = sem(name + "_gn_product")
            added = sem(name + "_gn_added")
            with nc.Block() as block:
                @block.vector
                def _(dve):
                    link = Chain(dve, link_sem)
                    for c in range(NC):
                        ins = nc.vector.bn_stats(st[:, c, :], y[:, c * CH:(c + 1) * CH])
                    link(ins)
                    nc.vector.bn_aggr(mv, st.rearrange("p c s -> p (c s)")).then_inc(stat_ready, 1)
                    dve.wait_ge(head_mean_ready, 1)
                    link(nc.vector.tensor_copy(sc[:, 0:1], ps[:, 0, 0:1]))
                    link(nc.vector.tensor_tensor(dev[:, 0:1], mv[:, 0:1], sc[:, 0:1], ALU.subtract))
                    link(nc.vector.tensor_tensor(dev[:, 1:2], dev[:, 0:1], dev[:, 0:1], ALU.mult))
                    nc.vector.tensor_tensor(dev[:, 2:3], dev[:, 1:2], mv[:, 1:2], ALU.add).then_inc(dev_ready, 1)
                    dve.wait_ge(head_var_ready, 1)
                    nc.vector.tensor_scalar(sc[:, 1:2], ps[:, 1, 0:1], 1e-5, None, ALU.add).then_inc(var_ready, 1)
                    dve.wait_ge(rstd_ready, 1)
                    link(nc.vector.tensor_tensor(sc[:, 3:4], sc[:, 2:3], col["gn_w"], ALU.mult))
                    for c in range(NC):
                        o = slice(c * CH, (c + 1) * CH)
                        link(nc.vector.tensor_scalar(yn[:, o], y[:, o], sc[:, 0:1], sc[:, 3:4], ALU.subtract, ALU.mult))
                        nc.vector.tensor_scalar(yn[:, o], yn[:, o], col["gn_b"], None, ALU.add).then_inc(normed, 1)
                    for c in range(NC):
                        dve.wait_ge(product, c + 1)
                        xs = x[:, c * TPC:(c + 1) * TPC, :].rearrange("p t d -> p (t d)")
                        nc.vector.tensor_tensor(xs, ps[:, 2 + c % 2, :], xs, ALU.add).then_inc(added, 1)

                @block.gpsimd
                def _(pool):
                    pool.wait_ge(var_ready, 1)
                    nc.gpsimd.tensor_tensor(sc[:, 2:3], sc[:, 1:2], neghalf[:, 0:1], ALU.pow).then_inc(rstd_ready, 1)

                @block.tensor
                def _(pe):
                    pe.wait_ge(stat_ready, 1)
                    nc.tensor.matmul(ps[:, 0, 0:1], head_mean, mv[:, 0:1], start=True, stop=True).then_inc(head_mean_ready, 1)
                    pe.wait_ge(dev_ready, 1)
                    nc.tensor.matmul(ps[:, 1, 0:1], head_mean, dev[:, 2:3], start=True, stop=True).then_inc(head_var_ready, 1)
                    for c in range(NC):
                        pe.wait_ge(normed, c + 1)
                        if c >= 2:
                            pe.wait_ge(added, c - 1)
                        for t in range(TPC):
                            ins = nc.tensor.matmul(ps[:, 2 + c % 2, t * P:(t + 1) * P],
                                                   yn[:, c * CH + t * P:c * CH + (t + 1) * P], w["ro"][:], start=True, stop=True)
                        ins.then_inc(product, 1)

        def lightning_out(name, y, gate):
            norm = Norm(name + "_o", y.rearrange("p (t d) -> p t d", d=D), xn, NT, 1e-5)
            gated = sem(name + "_gated")
            product = sem(name + "_product")
            added = sem(name + "_added")
            with nc.Block() as block:
                @block.vector
                def _(dve):
                    norm.vector(dve)
                    for c in range(NC):
                        o = slice(c * CH, (c + 1) * CH)
                        dve.wait_ge(norm.turned, c + 1)
                        nc.vector.tensor_scalar(xT[:, o], ps[:, c % 2, :], col["gamma"], col["beta"], ALU.mult, ALU.add).then_inc(norm.out, 1)
                        dve.wait_ge(norm.out, c + 1)
                        nc.vector.tensor_tensor(xT[:, o], xT[:, o], gate[:, o], ALU.mult).then_inc(gated, 1)
                    for c in range(NC):
                        dve.wait_ge(product, c + 1)
                        xs = x[:, c * TPC:(c + 1) * TPC, :].rearrange("p t d -> p (t d)")
                        nc.vector.tensor_tensor(xs, ps[:, 2 + c % 2, :], xs, ALU.add).then_inc(added, 1)

                @block.gpsimd
                def _(pool):
                    norm.gpsimd(pool)

                @block.tensor
                def _(pe):
                    norm.tensor(pe)
                    for c in range(NC):
                        pe.wait_ge(gated, c + 1)
                        if c >= 2:
                            pe.wait_ge(added, c - 1)
                        for t in range(TPC):
                            ins = nc.tensor.matmul(ps[:, 2 + c % 2, t * P:(t + 1) * P],
                                                   xT[:, c * CH + t * P:c * CH + (t + 1) * P], w["lo"][:], start=True, stop=True)
                        ins.then_inc(product, 1)

        def experts(name, slot_rows, result_rows):
            at = [0]

            def take(words):
                at[0] += words
                return arena[:, at[0] - words:at[0]]

            lg, l2, eq, oh1, oh2, ex, msk, t0, place = (take(NT * E).rearrange("p (t e) -> p t e", e=E) for _ in range(9))
            both = take(NT * E).rearrange("p (t e) -> p t e", e=E)
            m1, m2, mx, s1, s2 = (take(NT).rearrange("p (t a) -> p t a", a=1) for _ in range(5))
            carry, tot, upto = (take(NT * E).rearrange("p (e t) -> p e t", e=E) for _ in range(3))
            over = take(E * NT).rearrange("p (e t) -> p e t", e=E)
            tiles, tiles_upto, first_slot, ones8 = (take(E) for _ in range(4))
            before = take(P)
            ones = take(P)
            passed = take(ST * E).rearrange("p (s e) -> p s e", e=E)
            expert_f = take(ST)
            expert_of = take(ST).bitcast(U32)
            spot = take(TOP * NT).rearrange("p (k t) -> p k t", k=TOP)
            slot_of = take(TOP * NT).bitcast(U32).rearrange("p (k t) -> p k t", k=TOP)
            sent = take(TOP * NT * ROW).rearrange("p (k t c) -> p k t c", k=TOP, t=NT)
            xs = take(ST * ROW).rearrange("p (s c) -> p s c", c=ROW)
            xsT = take(2 * P).rearrange("p (b t) -> p b t", b=2)
            act_a = take(2 * F).rearrange("p (b f) -> p b f", b=2)
            hid = take(2 * F).rearrange("p (b f) -> p b f", b=2)
            hidT = take(2 * F).rearrange("p (b f t) -> p b f t", b=2, f=NF)
            YB = 4
            y = take(YB * D).rearrange("p (b d) -> p b d", b=YB)
            back = take(TOP * NT * D).rearrange("p (k t d) -> p k t d", k=TOP, t=NT)
            norm = Norm(name, x, sent[:, 0, :, 0:D], NT, 1e-5)
            LOAD_AT = [0, 3, 9, 21, ST]
            logits, link_sem, exp_in, exp_out, chosen, counted, sent_ready, slots_known = (sem(f"{name}_{n}") for n in (
                "logits", "link", "exp_in", "exp_out", "chosen", "counted", "sent_ready", "slots_known"))
            dispatched, x_turned, xsT_ready, up_ready, silu_out, hid_ready, hid_turned, hidT_ready, down_ready, y_ready = (
                sem(f"{name}_{n}") for n in ("dispatched", "x_turned", "xsT_ready", "up_ready", "silu_out", "hid_ready",
                                             "hid_turned", "hidT_ready", "down_ready", "y_ready"))
            slots_loaded = [sem(f"{name}_slots_loaded{i}") for i in range(len(LOAD_AT) - 1)]
            y_stored = [sem(f"{name}_y_stored{i}") for i in range(YB)]
            y_back = [sem(f"{name}_y_back{g}") for g in range(NC)]
            with nc.Block() as block:
                @block.vector
                def _(dve):
                    nc.vector.memset(ones, 1.0)
                    nc.vector.memset(ones8, 1.0)
                    nc.vector.tensor_scalar(before, cst[:, C_QMASK:C_QMASK + P], 0.0, None, ALU.is_lt)
                    nc.vector.tensor_scalar(sent[:, :, :, D].bitcast(U32), count[:, 0:TOP * NT].rearrange("p (k t) -> p k t", k=TOP),
                                            float(P), row_number, ALU.mult, ALU.add)
                    nc.vector.tensor_scalar(carry, count[:, 0:NT].rearrange("p (a t) -> p a t", a=1).to_broadcast([P, E, NT]),
                                            0.0, None, ALU.is_gt)
                    norm.vector(dve)
                    link = Chain(dve, link_sem)

                    def wide(a):
                        return a.to_broadcast([P, NT, E])

                    def per_expert(a):
                        return a.rearrange("p (a e) -> p a e", a=1).to_broadcast([P, NT, E])

                    def first_max(src, m, onehot):
                        link(nc.vector.tensor_reduce(out=m[:, :, 0], in_=src, axis=AX.X, op=ALU.max))
                        link(nc.vector.tensor_tensor(eq, src, wide(m), ALU.is_equal))
                        link(nc.vector.tensor_tensor(eq, eq, per_expert(rank), ALU.mult))
                        link(nc.vector.tensor_reduce(out=mx[:, :, 0], in_=eq, axis=AX.X, op=ALU.max))
                        link(nc.vector.tensor_tensor(onehot, eq, wide(mx), ALU.is_equal))

                    def multiplier(k, src, m, s):
                        link(nc.vector.scalar_tensor_tensor(out=msk, in0=lg, scalar=-1.0, in1=lg, op0=ALU.mult, op1=ALU.max))
                        link(nc.vector.tensor_tensor(msk, msk, wide(m), ALU.max))
                        link(nc.vector.tensor_tensor(t0, wide(m), lg, ALU.subtract))
                        link(nc.vector.scalar_tensor_tensor(out=msk, in0=msk, scalar=0.02, in1=t0, op0=ALU.mult, op1=ALU.is_ge))
                        nc.vector.tensor_tensor(t0, src, wide(m), ALU.subtract).then_inc(exp_in, 1)
                        dve.wait_ge(exp_out, k)
                        link(nc.vector.tensor_tensor(ex, ex, msk, ALU.mult))
                        link(nc.vector.tensor_reduce(out=s[:, :, 0], in_=ex, axis=AX.X, op=ALU.add))
                        link(nc.vector.reciprocal(s, s))

                    dve.wait_ge(logits, 1)
                    link(nc.vector.tensor_copy(lg, ps[:, 2, 0:NT * E].rearrange("p (t e) -> p t e", e=E)))
                    first_max(lg, m1, oh1)
                    link(nc.vector.scalar_tensor_tensor(out=l2, in0=oh1, scalar=NEG, in1=lg, op0=ALU.mult, op1=ALU.add))
                    first_max(l2, m2, oh2)
                    nc.vector.tensor_tensor(both, oh1, oh2, ALU.add).then_inc(chosen, 1)
                    dve.wait_ge(counted, 1)
                    link(nc.vector.tensor_copy(tot, ps[:, 3, NT * E:2 * NT * E].rearrange("p (t e) -> p e t", e=E)))
                    link(nc.vector.tensor_tensor_scan(upto.rearrange("p e t -> p (e t)"), carry.rearrange("p e t -> p (e t)"),
                                                      tot.rearrange("p e t -> p (e t)"), 0.0, ALU.mult, ALU.add))
                    link(nc.vector.scalar_tensor_tensor(
                        out=over, in0=count[:, 0:NT].rearrange("p (a t) -> p a t", a=1).to_broadcast([P, E, NT]), scalar=float(P),
                        in1=upto[:, :, NT - 1:NT].to_broadcast([P, E, NT]), op0=ALU.mult, op1=ALU.is_lt))
                    link(nc.vector.tensor_reduce(out=tiles, in_=over, axis=AX.X, op=ALU.add))
                    link(nc.vector.tensor_tensor_scan(tiles_upto, ones8, tiles, 0.0, ALU.mult, ALU.add))
                    link(nc.vector.tensor_tensor(first_slot, tiles_upto, tiles, ALU.subtract))
                    link(nc.vector.tensor_tensor(place, upto.rearrange("p e t -> p t e"), tot.rearrange("p e t -> p t e"), ALU.subtract))
                    link(nc.vector.scalar_tensor_tensor(out=place, in0=per_expert(first_slot), scalar=float(P), in1=place,
                                                        op0=ALU.mult, op1=ALU.add))
                    link(nc.vector.tensor_tensor(place, place, ps[:, 3, 0:NT * E].rearrange("p (t e) -> p t e", e=E), ALU.add))
                    link(nc.vector.tensor_tensor(t0, oh1, place, ALU.mult))
                    link(nc.vector.tensor_reduce(out=spot[:, 0, :], in_=t0, axis=AX.X, op=ALU.add))
                    link(nc.vector.tensor_tensor(t0, oh2, place, ALU.mult))
                    link(nc.vector.tensor_reduce(out=spot[:, 1, :], in_=t0, axis=AX.X, op=ALU.add))
                    nc.vector.tensor_copy(slot_of, spot).then_inc(slots_known, 1)
                    link(nc.vector.tensor_tensor(passed, count[:, 0:ST].rearrange("p (s a) -> p s a", a=1).to_broadcast([P, ST, E]),
                                                 tiles_upto.rearrange("p (a e) -> p a e", a=1).to_broadcast([P, ST, E]), ALU.is_ge))
                    link(nc.vector.tensor_reduce(out=expert_f, in_=passed, axis=AX.X, op=ALU.add))
                    nc.vector.tensor_scalar(expert_of, expert_f, float(E - 1), None, ALU.min).then_inc(slots_known, 1)
                    multiplier(1, lg, m1, s1)
                    multiplier(2, l2, m2, s2)

                    def take_turned(s):
                        dve.wait_ge(x_turned, s + 1)
                        if s >= 2:
                            dve.wait_ge(up_ready, s - 1)
                        nc.vector.tensor_copy(xsT[:, s % 2, :], ps[:, 6, 0:P]).then_inc(xsT_ready, 1)

                    take_turned(0)
                    for i in range(ST + 2):
                        if i + 1 < ST:
                            take_turned(i + 1)
                        if i < ST:
                            dve.wait_ge(silu_out, i + 1)
                            if i >= 2:
                                dve.wait_ge(hid_turned, i - 1)
                            nc.vector.tensor_tensor(hid[:, i % 2, :], ps[:, 2 + i % 2, :], act_a[:, i % 2, :],
                                                    ALU.mult).then_inc(hid_ready, 1)
                        s = i - 2
                        if s >= 0:
                            dve.wait_ge(down_ready, s + 1)
                            if s >= YB:
                                dve.wait_ge(y_stored[s % YB], 16 * (s // YB))
                            nc.vector.tensor_copy(y[:, s % YB, :], ps[:, 7, 0:D]).then_inc(y_ready, 1)
                    for g in range(NC):
                        dve.wait_ge(y_back[g], 16 * TOP)
                        for k, weight in ((0, s1), (1, s2)):
                            for t in range(g * TPC, (g + 1) * TPC):
                                ins = nc.vector.scalar_tensor_tensor(out=x[:, t, :], in0=back[:, k, t, :], scalar=weight[:, t, :],
                                                                     in1=x[:, t, :], op0=ALU.mult, op1=ALU.add)
                            link(ins)

                @block.gpsimd
                def _(pool):
                    norm.gpsimd(pool)
                    pool.wait_ge(sent_ready, NC)
                    pool.wait_ge(slots_known, 1)
                    for t in range(NT):
                        for k in range(TOP):
                            nc.gpsimd.indirect_dma_start(
                                out=slot_rows, out_offset=bass.IndirectOffsetOnAxis(ap=slot_of[:, k, t:t + 1], axis=0),
                                in_=sent[:, k, t, :], in_offset=None).then_inc(dispatched, 16)
                    for s in range(ST):
                        pool.wait_ge(y_ready, s + 1)
                        nc.gpsimd.indirect_dma_start(
                            out=result_rows, out_offset=bass.IndirectOffsetOnAxis(ap=xs[:, s, D:ROW].bitcast(U32), axis=0),
                            in_=y[:, s % YB, :], in_offset=None).then_inc(y_stored[s % YB], 16)

                @block.sync
                def _(sp):
                    sp.wait_ge(dispatched, 16 * TOP * NT)
                    for i, done in enumerate(slots_loaded):
                        a, b = LOAD_AT[i], LOAD_AT[i + 1]
                        sp.dma_start(xs[:, a:b, :], slot_rows[a * P:b * P, :].rearrange("(s p) c -> p s c", p=P)).then_inc(done, 16)
                    for b in range(YB):
                        sp.wait_ge(y_stored[b], 16 * len(range(b, ST, YB)))
                    for g in range(NC):
                        for k in range(TOP):
                            r = k * T + g * CH
                            sp.dma_start(back[:, k, g * TPC:(g + 1) * TPC, :],
                                         result_rows[r:r + CH, :].rearrange("(t p) d -> p t d", p=P)).then_inc(y_back[g], 16)

                @block.scalar
                def _(act):
                    for g in range(NC):
                        t = slice(g * TPC, (g + 1) * TPC)
                        act.wait_ge(norm.turned, g + 1)
                        nc.scalar.copy(xT[:, g * CH:(g + 1) * CH], ps[:, norm.banks[g % 2], :]).then_inc(norm.out, 1)
                        nc.scalar.copy(sent[:, 1, t, 0:D], sent[:, 0, t, 0:D]).then_inc(sent_ready, 1)
                    for k in (1, 2):
                        act.wait_ge(exp_in, k)
                        nc.scalar.activation(ex, t0, ACT.Exp).then_inc(exp_out, 1)
                    for i in range(ST + 1):
                        if i < ST:
                            act.wait_ge(up_ready, i + 1)
                            if i >= 2:
                                act.wait_ge(hid_ready, i - 1)
                            nc.scalar.activation(act_a[:, i % 2, :], ps[:, i % 2, :], ACT.Silu).then_inc(silu_out, 1)
                        s = i - 1
                        if s >= 0:
                            act.wait_ge(hid_turned, s + 1)
                            if s >= 2:
                                act.wait_ge(down_ready, s - 1)
                            nc.scalar.copy(hidT[:, s % 2, :, :].rearrange("p f t -> p (f t)"), ps[:, 4 + s % 2, :]).then_inc(hidT_ready, 1)

                @block.tensor
                def _(pe):
                    norm.tensor(pe)
                    for t in range(NT):
                        pe.wait_ge(norm.out, t // TPC + 1)
                        ins = nc.tensor.matmul(ps[:, 2, t * E:(t + 1) * E], xT[:, t * P:(t + 1) * P], w["gate"][:], start=True, stop=True)
                    ins.then_inc(logits, 1)
                    pe.wait_ge(chosen, 1)
                    sel = both.rearrange("p t e -> p (t e)")
                    nc.tensor.matmul(ps[:, 3, 0:NT * E], before, sel, start=True, stop=True)
                    nc.tensor.matmul(ps[:, 3, NT * E:2 * NT * E], ones, sel, start=True, stop=True).then_inc(counted, 1)
                    pe.wait_ge(moe_loaded, 48)
                    pe.wait_ge(slots_known, 2)
                    expert = {}

                    def turn_x(s):
                        if s in LOAD_AT:
                            pe.wait_ge(slots_loaded[LOAD_AT.index(s)], 16)
                        if s >= 1:
                            pe.wait_ge(xsT_ready, s)
                        nc.tensor.transpose(ps[:, 6, 0:P], xs[:, s, 0:D], ident).then_inc(x_turned, 1)

                    turn_x(0)
                    for i in range(ST + 2):
                        if i < ST:
                            expert[i] = nc.tensor.value_load(expert_of[0:1, i:i + 1], min_val=0, max_val=E - 1)
                            pe.wait_ge(xsT_ready, i + 1)
                            if i >= 2:
                                pe.wait_ge(hid_ready, i - 1)
                            nc.tensor.matmul(ps[:, i % 2, :], xsT[:, i % 2, :], w1[:, expert[i], :], start=True, stop=True)
                            nc.tensor.matmul(ps[:, 2 + i % 2, :], xsT[:, i % 2, :], w3[:, expert[i], :],
                                             start=True, stop=True).then_inc(up_ready, 1)
                        s = i - 1
                        if 0 <= s < ST:
                            pe.wait_ge(hid_ready, s + 1)
                            if s >= 2:
                                pe.wait_ge(hidT_ready, s - 1)
                            for f in range(NF):
                                ins = nc.tensor.transpose(ps[:, 4 + s % 2, f * P:(f + 1) * P], hid[:, s % 2, f * P:(f + 1) * P], ident)
                            ins.then_inc(hid_turned, 1)
                        if i + 1 < ST:
                            turn_x(i + 1)
                        s = i - 2
                        if s >= 0:
                            pe.wait_ge(hidT_ready, s + 1)
                            if s >= 1:
                                pe.wait_ge(y_ready, s)
                            for f in range(NF):
                                ins = nc.tensor.matmul(ps[:, 7, 0:D], hidT[:, s % 2, f, :], w2[:, expert[s], f, :],
                                                       start=f == 0, stop=f == NF - 1)
                            ins.then_inc(down_ready, 1)

        softmax_attention()
        load_experts()
        end_stage()
        channel_mix("f0")
        end_stage()
        linear_attention("g", "gated")
        end_stage()
        channel_mix("f1")
        end_stage()
        linear_attention("r", "retention")
        end_stage()
        experts("m0", slots[0], results[0])
        end_stage()
        linear_attention("l", "lightning")
        end_stage()
        experts("m1", slots[1], results[1])
        x_stored = sem("x_stored")
        with nc.Block() as block:
            @block.sync
            def _(sp):
                sp.dma_start(io["out"].rearrange("a (t p) d -> p (a t) d", p=P), x[:]).then_inc(x_stored, 16)
                sp.wait_ge(x_stored, 16)


def constants():
    import numpy as np
    c = np.zeros((P, C_F32), np.float32)
    c[:, C_IDENT:C_IDENT + P] = np.eye(P)
    ch = np.arange(P)
    for e in range(HD):
        c[ch, C_PICK + e * P + ch // HD * HD + e] = 1.0
    c[:, C_HEAD:C_HEAD + P] = (ch[:, None] // HD == ch[None, :] // HD) / HD
    h = ch // HD
    c[:, C_RET] = 1.0 - 2.0 ** (-5.0 - h * (8.0 / H))
    start = 2.0 ** (-2.0 ** (-(np.log2(H) - 3)))
    slope = np.array([start * start ** i for i in range(H)], np.float32) * np.float32(1.0 + 1e-05)
    c[:, C_LT] = np.exp(-slope.astype(np.float64))[h]
    c[:, C_RANK:C_RANK + E] = E - np.arange(E)
    c[:, C_QMASK:C_QMASK + P] = np.where(ch[None, :] > ch[:, None], NEG, 0.0)
    c[:, C_KMASK:C_KMASK + P] = np.where(ch[:, None] > ch[None, :], NEG, 0.0)
    c[:, C_COUNT:C_PART] = np.arange(C_PART - C_COUNT)
    c[:, C_PART] = ch
    return c


def kernel(**inputs):
    import numpy as np
    import concourse.bacc as bacc
    from concourse.bass_utils import run_bass_kernel_spmd

    a = {k: np.asarray(v) for k, v in inputs.items()}
    vq = a["L0_attn_b_vq_w"]
    given = {
        "x": a["L0_attn_a_x"], "cst": constants(),
        "qkv": a["L0_attn_a_W_qkv"], "wout": a["L0_attn_a_W_out"],
        "wr": a["L0_ffn_W_r"].T, "wk": a["L0_ffn_W_k"].T, "wv": a["L0_ffn_W_v"].T,
        "hk": a["L0_attn_b_key_w"].T, "hv": vq[:D].T, "hq": vq[D:].T, "ho": a["L0_attn_b_out_w"].T,
        "rq": a["L1_attn_a_Wq"].T, "rk": a["L1_attn_a_Wk"].T, "rv": a["L1_attn_a_Wv"].T, "ro": a["L1_attn_a_Wo"].T,
        "lq": a["L1_attn_b_Wq"], "lk": a["L1_attn_b_Wk"], "lv": a["L1_attn_b_Wv"], "lo": a["L1_attn_b_Wo"],
        "lg1": a["L1_attn_b_Wg1"], "lg2": a["L1_attn_b_Wg2"], "gate": a["L1_ffn_gate_w"],
        "out_b": a["L0_attn_b_out_b"], "w1": a["L1_ffn_w1"], "w2": a["L1_ffn_w2"], "w3": a["L1_ffn_w3"],
        "q_scale": a["L0_attn_a_q_scale"], "k_scale": a["L0_attn_a_k_scale"], "key_b": a["L0_attn_b_key_b"],
        "mu_r": a["L0_ffn_mu_r"], "mu_k": a["L0_ffn_mu_k"], "gn_w": a["L1_attn_a_gn_w"], "gn_b": a["L1_attn_a_gn_b"],
        "gamma": a["L1_attn_b_gamma"], "beta": a["L1_attn_b_beta"],
    }
    nc = bacc.Bacc("TRN2", target_bir_lowering=False, num_devices=1)
    arrays, io = {}, {}
    for name, v in given.items():
        v = np.ascontiguousarray(v)
        arrays["in_" + name] = v
        io[name] = nc.dram_tensor("in_" + name, v.shape, mybir.dt.from_np(v.dtype), kind="ExternalInput").ap()
    io["out"] = nc.dram_tensor("out_x", (1, T, D), FP32, kind="ExternalOutput").ap()
    build(nc, io)
    r = run_bass_kernel_spmd(nc, [arrays], core_ids=[0])
    return r.results[0]["out_x"]
```

```python
import concourse.bass as bass
from concourse import mybir
from contextlib import ExitStack

FP32 = mybir.dt.float32
BF16 = mybir.dt.bfloat16
U32 = mybir.dt.uint32
ACT = mybir.ActivationFunctionType
ALU = mybir.AluOpType
AX = mybir.AxisListType

T = 2048
D = 128
H = 16
HD = D // H
P = 128
NT = T // P
CH = 512
NC = T // CH
TPC = CH // P
E = 8
F = 512
NF = F // P
TOP = 2
ST = TOP * NT + E - 1
EARLY = 5
ROW = D + 1
PARTS = 3
KROWS = PARTS * PARTS * HD
MROW = 96
GH = 4
NG = H // GH
NEG = -1.0e30

C_IDENT = 0
C_PICK = C_IDENT + P
C_HEAD = C_PICK + HD * P
C_RET = C_HEAD + P
C_LT = C_RET + 1
C_RANK = C_LT + 1
C_QMASK = C_RANK + E
C_KMASK = C_QMASK + P
C_COUNT = C_KMASK + P
C_PART = C_COUNT + P
C_F32 = C_PART + 1

WEIGHTS = [("qkv", 3 * D), ("wout", D), ("wr", D), ("wk", D), ("wv", D), ("hk", D), ("hv", D), ("hq", D), ("ho", D),
           ("rq", D), ("rk", D), ("rv", D), ("ro", D), ("lq", D), ("lk", D), ("lv", D), ("lo", D), ("lg1", HD),
           ("gate", E)]
VECTORS = ["q_scale", "k_scale", "key_b", "mu_r", "mu_k", "gn_w", "gn_b", "gamma", "beta"]
LOADS = 1 + len(WEIGHTS) + len(VECTORS)


def build(nc, io):
    ctx = ExitStack()
    with ctx:
        def sb(name, shape, dt=FP32):
            return ctx.enter_context(nc.sbuf_tensor(name, shape, dt))

        stage_sems = []

        def sem(name):
            stage_sems.append(nc.alloc_semaphore(name=name))
            return stage_sems[-1]

        def end_stage():
            with nc.Block() as block:
                @block.gpsimd
                def _(pool):
                    nc.clear_and_free_semaphores(stage_sems)
            stage_sems.clear()

        x = sb("x", [P, NT, D])
        xn = sb("xn", [P, NT, D])
        xt = sb("xt", [P, 1 + T])
        xT = xt[:, 1:1 + T]
        cst = sb("cst", [P, C_F32])
        cstb = sb("cstb", [P, 3 * P], BF16)
        w = {}
        for name, width in WEIGHTS:
            w[name] = sb("w_" + name, [P, width])
        w["lg2"] = sb("w_lg2", [HD, D])
        vec = sb("vec", [P, len(VECTORS)])
        col = {name: vec[:, i:i + 1] for i, name in enumerate(VECTORS)}
        out_bias = sb("out_bias", [P, D])
        w1 = sb("w1", [P, E, F])
        w3 = sb("w3", [P, E, F])
        w2 = sb("w2", [P, E, NF, D])
        stats = sb("stats", [P, 2 * NT, 6])
        small = sb("small", [P, 10, 2 * NT])
        neghalf = sb("neghalf", [P, NT])
        arena = sb("arena", [P, 24 * 1024 + 8])
        ps = ctx.enter_context(nc.psum_tensor("ps", [P, 8, CH], FP32))

        ident = cst[:, C_IDENT:C_IDENT + P]
        pick = cst[:, C_PICK:C_PICK + HD * P].rearrange("p (e m) -> p e m", e=HD)
        head_mean = cst[:, C_HEAD:C_HEAD + P]
        rank = cst[:, C_RANK:C_RANK + E]
        count = cst[:, C_COUNT:C_PART]
        row_number = cst[:, C_PART:C_PART + 1]
        identb, qmask, kmask = (cstb[:, i * P:(i + 1) * P] for i in range(3))

        q_parts = nc.dram_tensor("q_parts", [H, PARTS, HD, T], BF16, kind="Internal").ap()
        k_parts = nc.dram_tensor("k_parts", [H, PARTS, HD, T], BF16, kind="Internal").ap()

        slots = [nc.dram_tensor(f"slots{i}", [ST * P, ROW], FP32, kind="Internal").ap() for i in range(2)]
        results = [nc.dram_tensor(f"results{i}", [(TOP * NT + ST) * P, D], FP32, kind="Internal").ap() for i in range(2)]
        slots_cleared = ctx.enter_context(nc.semaphore("slots_cleared"))
        EMPTY1 = E * F // ROW
        empty = [(0, EMPTY1, w2[:].rearrange("p e f d -> p (e f d)")[:, 0:EMPTY1 * ROW].rearrange("p (s c) -> p s c", c=ROW)),
                 (EMPTY1, ST, arena[:, 11 * NT * D:11 * NT * D + (ST - EMPTY1) * ROW].rearrange("p (s c) -> p s c", c=ROW))]

        loaded = ctx.enter_context(nc.semaphore("loaded"))
        moe_loaded = ctx.enter_context(nc.semaphore("moe_loaded"))

        class Chain:

            def __init__(self, eng, s):
                self.eng, self.s, self.n = eng, s, 0

            def __call__(self, ins):
                self.n += 1
                ins.then_inc(self.s, 1)
                self.eng.wait_ge(self.s, self.n)

        class Norm:

            def __init__(self, name, src, dst, n, eps, banks=(0, 1)):
                self.src, self.dst, self.n, self.eps, self.banks = src, dst, n, eps, banks
                self.chain = sem(name + "_chain")
                self.var_ready = sem(name + "_var_ready")
                self.rstd_ready = sem(name + "_rstd_ready")
                self.normed = sem(name + "_normed")
                self.turned = sem(name + "_turned")
                self.out = sem(name + "_out")

            def vector(self, dve, after=lambda g: None):
                n = self.n
                link = Chain(dve, self.chain)
                st = stats[:, 0:n, :]
                me, se, mo, so = st[:, :, 1], st[:, :, 2], st[:, :, 4], st[:, :, 5]
                mean, diff, m2, sq, var = (small[:, i, 0:n] for i in range(5))
                nc.vector.tensor_tensor(mean, me, mo, ALU.add)
                nc.vector.tensor_tensor(diff, me, mo, ALU.subtract)
                link(nc.vector.tensor_tensor(m2, se, so, ALU.add))
                nc.vector.tensor_tensor(sq, diff, diff, ALU.mult)
                nc.vector.tensor_scalar(mean, mean, 0.5, None, ALU.mult)
                link(nc.vector.tensor_scalar(m2, m2, 1.0 / D, self.eps, ALU.mult, ALU.add))
                nc.vector.scalar_tensor_tensor(out=var, in0=sq, scalar=0.25, in1=m2, op0=ALU.mult,
                                               op1=ALU.add).then_inc(self.var_ready, 1)
                for g in range(n // 4):
                    dve.wait_ge(self.rstd_ready, g + 1)
                    for t in range(4 * g, 4 * g + 4):
                        ins = nc.vector.tensor_scalar(self.dst[:, t, :], self.src[:, t, :], small[:, 0, t:t + 1],
                                                      small[:, 5, t:t + 1], ALU.subtract, ALU.mult)
                    ins.then_inc(self.normed, 1)
                    after(g)

            def gpsimd(self, pool):
                pool.wait_ge(self.var_ready, 1)
                for g in range(self.n // 4):
                    nc.gpsimd.tensor_tensor(small[:, 5, 4 * g:4 * g + 4], small[:, 4, 4 * g:4 * g + 4],
                                            neghalf[:, 0:4], ALU.pow).then_inc(self.rstd_ready, 1)

            def tensor(self, pe, groups=None):
                for g in groups or range(self.n // 4):
                    pe.wait_ge(self.normed, g + 1)
                    if g >= 2:
                        pe.wait_ge(self.out, g - 1)
                    for i in range(4):
                        ins = nc.tensor.transpose(ps[:, self.banks[g % 2], i * P:(i + 1) * P],
                                                  self.dst[:, 4 * g + i, :], ident)
                    ins.then_inc(self.turned, 1)

            def scalar(self, act, groups=None):
                for g in groups or range(self.n // 4):
                    act.wait_ge(self.turned, g + 1)
                    nc.scalar.copy(xT[:, g * CH:(g + 1) * CH], ps[:, self.banks[g % 2], :]).then_inc(self.out, 1)

        def statistics(tiles, src):
            for t in tiles:
                ins = nc.vector.bn_stats(stats[:, t, :], src[:, t, :])
            return ins

        def x_statistics(dve, added, c):
            if c >= 0:
                dve.wait_ge(added, c + 1)
                statistics(range(c * TPC, (c + 1) * TPC), x)

        x_loaded = sem("x_loaded")
        tables_loaded = sem("tables_loaded")
        empty_zeroed = sem("empty_zeroed")
        empty_ready = sem("empty_ready")
        with nc.Block() as block:
            @block.sync
            def _(sp):
                sp.dma_start(x[:], io["x"].rearrange("a (t p) d -> p (a t) d", p=P)).then_inc(x_loaded, 16)
                sp.dma_start(cst[:], io["cst"]).then_inc(tables_loaded, 16)
                sp.dma_start(w["qkv"][:], io["qkv"]).then_inc(tables_loaded, 16)

            @block.gpsimd
            def _(pool):
                for _, _, dst in empty:
                    ins = nc.gpsimd.memset(dst, 0.0).then_inc(empty_zeroed, 1)

            @block.vector
            def _(dve):
                nc.vector.memset(xt[:, 0:1], 0.0)
                nc.vector.memset(neghalf[:], -0.5)
                dve.wait_ge(x_loaded, 16)
                statistics(range(NT), x)

        def attention_order(units, u0, m0, steps):
            FIRST, LEAD, RATE, SLOTS = 40, 2, 3.0, GH + 2
            plan, given, turned = [], 0, 0

            def give():
                nonlocal given, turned
                plan.append(("max", given))
                given += 1
                if turned < steps and given >= min(m0[turned + 1] + 3, m0[-1]):
                    plan.append(("turn max", turned))
                    turned += 1

            for _ in range(FIRST):
                give()
            owed = 0.0

            def slot(place):
                nonlocal owed
                need = [(m0[k + 1] + 4 - given) / (u0[k] - LEAD - place) for k in range(steps) if u0[k] - LEAD > place]
                owed += max([RATE] + need) / SLOTS
                while owed >= 1.0 and given < m0[-1]:
                    give()
                    owed -= 1.0

            for u, (k, kt, _) in enumerate(units):
                for j in range(GH):
                    plan.append(("scores", u, j))
                    slot(u + j / SLOTS)
                if u >= 1:
                    plan.append(("values", u - 1))
                slot(u + GH / SLOTS)
                if k >= 1 and kt == 1:
                    plan.append(("turn values", k - 1))
                slot(u + (GH + 1) / SLOTS)
            plan.append(("values", len(units) - 1))
            plan.append(("turn values", steps - 1))
            return plan

        def softmax_attention():
            QK = GH * T // 2
            Qs = [arena[:, 2 * b * QK:(2 * b + 1) * QK].bitcast(BF16).rearrange("p (j t) -> p j t", j=GH) for b in (0, 1)]
            Ks = [arena[:, (2 * b + 1) * QK:(2 * b + 2) * QK].bitcast(BF16).rearrange("p (j t) -> p j t", j=GH) for b in (0, 1)]
            at = 4 * QK
            probs = arena[:, at:at + 2 * GH * CH].rearrange("p (b j q) -> p b j q", b=2, j=GH)
            at += 2 * GH * CH
            qk = arena[:, 0:2 * NT * D].rearrange("p (n d) -> p n d", d=D)
            qkn = arena[:, 2 * NT * D:4 * NT * D].rearrange("p (n d) -> p n d", d=D)
            rest = arena[:, 4 * NT * D:6 * NT * D].rearrange("p (s t) -> p s t", s=2)
            feat = arena[:, 6 * NT * D:8 * NT * D].rearrange("p (s t) -> p s t", s=2)
            parts = arena[:, 8 * NT * D:11 * NT * D].bitcast(BF16).rearrange("p (s r t) -> p s r t", s=2, r=PARTS)
            ctxt = xn
            with ExitStack() as mem:
                def own(name, shape, dt=FP32):
                    return mem.enter_context(nc.sbuf_tensor(name, shape, dt))

                spare = w1[:].rearrange("p e f -> p (e f)")
                nv = NT * H * (HD + 1)
                vaug = spare[:, 0:nv].rearrange("p (t h d) -> p t h d", t=NT, h=H)
                osb = spare[:, nv:nv + 2 * CH].rearrange("p (b q) -> p b q", b=2)
                vg = w3[:].rearrange("p e f -> p (e f)").rearrange("p (b t j m) -> p b t j m", b=2, t=NT, j=GH)
                qscaled = own("qscaled", [P, 1])
                rec = own("rec", [P, 2, TPC, GH])
                mpart = own("mpart", [P, GH, TPC, NC])
                negmax = own("negmax", [P, 2, GH, TPC])
                mwide = own("mwide", [P, GH, P // GH], BF16)
                mparts = mwide[:, :, 0:PARTS * TPC].rearrange("p j (r t) -> p j r t", r=PARTS)
                ones = own("ones", [PARTS, T], BF16)
                mrow = own("mrow", [P, P], BF16)

                norm = Norm("a0", x, xn, NT, 1e-5)
                qkn_norm = Norm("a1", qk, qkn, 2 * NT, 1e-6, banks=(6, 7))
                projected = sem("a_projected")
                split_out = sem("a_split_out")
                v_out = sem("a_v_out")
                scaled = sem("a_scaled")
                with nc.Block() as block:
                    @block.vector
                    def _(dve):
                        norm.vector(dve)
                        dve.wait_ge(tables_loaded, 32)
                        nc.vector.tensor_copy(identb, ident)
                        nc.vector.tensor_copy(cstb[:, P:3 * P], cst[:, C_QMASK:C_QMASK + 2 * P])
                        dve.wait_ge(empty_zeroed, len(empty))
                        for a, b, dst in empty:
                            nc.vector.tensor_scalar(dst[:, :, D].bitcast(U32), count[:, TOP * NT + a:TOP * NT + b], float(P), row_number,
                                                    ALU.mult, ALU.add).then_inc(empty_ready, 1)
                        for t in range(NT):
                            dve.wait_ge(projected, t + 1)
                            dve.wait_ge(split_out, t + 1)
                            nc.vector.tensor_copy(vaug[:, t, :, 0:HD],
                                                  ps[:, 2 + t % 4, 2 * D:3 * D].rearrange("p (h d) -> p h d", h=H)).then_inc(v_out, 1)
                            statistics((t, NT + t), qk)
                        dve.wait_ge(loaded, 16 * LOADS)
                        nc.vector.tensor_scalar(qscaled[:], col["q_scale"], float(HD) ** -0.5, None, ALU.mult).then_inc(scaled, 1)

                    @block.sync
                    def _(sp):
                        for name, _ in WEIGHTS[1:]:
                            sp.dma_start(w[name][:], io[name]).then_inc(loaded, 16)
                        sp.dma_start(w["lg2"][:], io["lg2"]).then_inc(loaded, 16)
                        sp.dma_start(out_bias[:], io["out_b"].rearrange("(a n) -> a n", a=1).to_broadcast([P, D])).then_inc(loaded, 16)
                        for i, name in enumerate(VECTORS):
                            sp.dma_start(vec[:, i:i + 1], io[name].rearrange("(n a) -> n a", a=1)).then_inc(loaded, 16)
                        sp.wait_ge(empty_ready, len(empty))
                        for rows in slots:
                            for a, b, src in empty:
                                sp.dma_start(rows[a * P:b * P, :].rearrange("(s p) c -> p s c", p=P), src).then_inc(slots_cleared, 16)
                        sp.wait_ge(loaded, 16 * LOADS)

                    @block.gpsimd
                    def _(pool):
                        norm.gpsimd(pool)
                        nc.gpsimd.memset(vaug[:, :, :, HD:HD + 1], 1.0)
                        nc.gpsimd.memset(ones[:], 1.0)
                        nc.gpsimd.memset(mwide[:], 0.0)
                        nc.gpsimd.memset(vg, 0.0)

                    @block.tensor
                    def _(pe):
                        pe.wait_ge(tables_loaded, 32)
                        norm.tensor(pe)
                        for t in range(NT):
                            pe.wait_ge(norm.out, t // TPC + 1)
                            if t >= 4:
                                pe.wait_ge(v_out, t - 3)
                            nc.tensor.matmul(ps[:, 2 + t % 4, 0:3 * D], xT[:, t * P:(t + 1) * P], w["qkv"][:],
                                             start=True, stop=True).then_inc(projected, 1)

                    @block.scalar
                    def _(act):
                        norm.scalar(act)
                        for t in range(NT):
                            act.wait_ge(projected, t + 1)
                            nc.scalar.copy(qk.rearrange("p (s t) d -> p s t d", s=2)[:, :, t, :],
                                           ps[:, 2 + t % 4, 0:2 * D].rearrange("p (s d) -> p s d", s=2)).then_inc(split_out, 1)

                high = sem("a_high")
                mid = sem("a_mid")
                rest_ready = sem("a_rest_ready")
                low = sem("a_low")
                stored = sem("a_stored")
                cleared = sem("a_cleared")
                ones_loaded = [sem(f"a_ones_loaded{b}") for b in (0, 1)]
                first_loaded = sem("a_first_loaded")
                first_rest_loaded = sem("a_first_rest_loaded")

                def load(sp, g, b, loaded_sem, a=0, z=T):
                    def rows(dst, row, src, part, n):
                        sp.dma_start(dst[row * HD:(row + n) * HD, :, a:z], bass.AP(
                            tensor=src.tensor, offset=g * (GH * PARTS * HD * T) + (part * HD * T + a),
                            ap=[[T, n * HD], [PARTS * HD * T, GH], [1, z - a]])).then_inc(loaded_sem, 16)

                    for r in range(PARTS):
                        rows(Qs[b], r * PARTS, q_parts, 0, PARTS)
                        rows(Ks[b], r * PARTS, k_parts, r, PARTS - r)
                        if r >= 1:
                            rows(Ks[b], r * PARTS + PARTS - r, k_parts, 0, r)

                LOADS_OF_GROUP = 3 * PARTS - 1

                with nc.Block() as block:
                    @block.vector
                    def _(dve):
                        def take_rest(g):
                            s, o = g // NC, slice(g % NC * CH, (g % NC + 1) * CH)
                            dve.wait_ge(high, g + 1)
                            nc.vector.tensor_tensor(rest[:, s, o], feat[:, s, o], parts[:, s, 0, o], ALU.subtract).then_inc(rest_ready, 1)

                        def take_low(g):
                            s, o = g // NC, slice(g % NC * CH, (g % NC + 1) * CH)
                            dve.wait_ge(mid, g + 1)
                            nc.vector.tensor_tensor(parts[:, s, 2, o], rest[:, s, o], parts[:, s, 1, o], ALU.subtract).then_inc(low, 1)

                        def split_behind(g):
                            if 2 <= g < 2 * NC + 2:
                                take_rest(g - 2)
                            if g >= 3:
                                take_low(g - 3)

                        qkn_norm.vector(dve, after=split_behind)
                        for g in range(2 * NC, 2 * NC + 3):
                            split_behind(g)
                        dve.wait_ge(low, 2 * NC)
                        nc.vector.memset(Qs[1][64:P].bitcast(FP32), 0.0)

                    @block.gpsimd
                    def _(pool):
                        qkn_norm.gpsimd(pool)
                        pool.wait_ge(qkn_norm.normed, 2 * NC)
                        nc.gpsimd.memset(Qs[0][64:P].bitcast(FP32), 0.0).then_inc(cleared, 1)
                        pool.wait_ge(qkn_norm.turned, 2 * NC)
                        nc.gpsimd.memset(Ks[0][64:P].bitcast(FP32), 0.0).then_inc(cleared, 1)
                        pool.wait_ge(low, 2 * NC)
                        nc.gpsimd.memset(Ks[1][64:P].bitcast(FP32), 0.0).then_inc(cleared, 1)

                    @block.tensor
                    def _(pe):
                        qkn_norm.tensor(pe)

                    @block.scalar
                    def _(act):
                        act.wait_ge(scaled, 1)
                        def take_mid(g):
                            s, o = g // NC, slice(g % NC * CH, (g % NC + 1) * CH)
                            act.wait_ge(rest_ready, g + 1)
                            nc.scalar.copy(parts[:, s, 1, o], rest[:, s, o]).then_inc(mid, 1)

                        for g in range(2 * NC):
                            s, o = g // NC, slice(g % NC * CH, (g % NC + 1) * CH)
                            act.wait_ge(qkn_norm.turned, g + 1)
                            nc.scalar.mul(feat[:, s, o], ps[:, 6 + g % 2, :],
                                          qscaled[:, 0:1] if s == 0 else col["k_scale"]).then_inc(qkn_norm.out, 1)
                            act.wait_ge(qkn_norm.out, g + 1)
                            nc.scalar.copy(parts[:, s, 0, o], feat[:, s, o]).then_inc(high, 1)
                            if g >= 1:
                                take_mid(g - 1)
                        take_mid(2 * NC - 1)

                    @block.sync
                    def _(sp):
                        for s, dst in ((0, q_parts), (1, k_parts)):
                            for half in (1, 2):
                                o = slice((half - 1) * T // 2, half * T // 2)
                                sp.wait_ge(low, NC * s + half * NC // 2)
                                for r in range(PARTS):
                                    sp.dma_start(dst[:, r, :, o], parts[:, s, r, o]).then_inc(stored, 16)
                        sp.wait_ge(stored, 16 * 2 * 2 * PARTS)
                        sp.wait_ge(cleared, 2)
                        load(sp, 0, 0, first_loaded, 0, CH)
                        for b in (0, 1):
                            if b == 1:
                                load(sp, 0, 0, first_rest_loaded, CH, T)
                                sp.wait_ge(cleared, 3)
                            sp.dma_start(Ks[b][MROW:MROW + PARTS], ones[:].rearrange("p (a t) -> p a t", a=1).to_broadcast([PARTS, GH, T])
                                         ).then_inc(ones_loaded[b], 16)
                        sp.wait_ge(slots_cleared, 16 * len(empty) * len(slots))
                        sp.wait_ge(ones_loaded[0], 16)
                        sp.wait_ge(first_loaded, 16 * LOADS_OF_GROUP)

                STEPS = [(0, 0), (0, 1), (0, 2), (0, 3), (1, 3), (1, 2), (1, 1), (1, 0)]
                UNITS = [TPC * (c + 1) for _, c in STEPS]
                CHUNKS = [GH * TPC * (c + 1) for _, c in STEPS]
                NU, NM, NS = sum(UNITS), sum(CHUNKS), len(STEPS)
                u0 = [sum(UNITS[:k]) for k in range(NS + 1)]
                m0 = [sum(CHUNKS[:k]) for k in range(NS + 1)]
                MAXIMA = [(k, t, j, kc, CH if kc < c else (t + 1) * P) for k, (_, c) in enumerate(STEPS)
                          for t in range(TPC) for j in range(GH) for kc in range(c + 1)]
                UNIT = [(k, kt, max(0, (kt - c * TPC) * P)) for k, (_, c) in enumerate(STEPS) for kt in range(UNITS[k])]
                PLAN = attention_order(UNIT, u0, m0, NS)
                RING = {(p[0], p[1]): m for m, p in enumerate(p for p in PLAN if p[0] in ("max", "turn max", "turn values"))}

                mark = len(stage_sems)
                stack_loaded = sem("a_stack_loaded")
                next_loaded = sem("a_next_loaded")
                vg_ready = sem("a_vg_ready")
                ring_ready = sem("a_ring_ready")
                ring_read = sem("a_ring_read")
                max_split = sem("a_max_split")
                max_set = sem("a_max_set")
                st_ready = sem("a_st_ready")
                exp_done = sem("a_exp_done")
                pv_done = sem("a_pv_done")
                o_out = sem("a_o_out")
                split_link = sem("a_split_link")
                keep_link = sem("a_keep_link")
                rows_cleared = sem("a_rows_cleared")
                body_sems = stage_sems[mark:]
                ST, S, O = 0, 4, 7
                DEPTH = 3

                with nc.Fori(0, 2) as i:
                    with nc.Block() as block:
                        @block.sync
                        def _(sp):
                            def set_maxima(k):
                                b, c = STEPS[k]
                                n = k + 1
                                if k == 4:
                                    sp.wait_ge(rows_cleared, 1)
                                sp.wait_ge(ring_read, RING["turn max", k] + 1)
                                for j in range(GH):
                                    sp.dma_start(Qs[b][MROW:MROW + PARTS, j, c * CH:(c + 1) * CH],
                                                 mrow[j * P // GH:j * P // GH + PARTS * TPC, :]).then_inc(max_set, 16)
                                sp.wait_ge(max_set, 16 * GH * n)

                            load(sp, i * 2 + 1, 1, stack_loaded)
                            for k in range(NS):
                                set_maxima(k)
                            sp.wait_ge(pv_done, u0[4])
                            load(sp, 2 - i * 2, 0, next_loaded)
                            sp.wait_ge(next_loaded, 16 * LOADS_OF_GROUP)

                        @block.gpsimd
                        def _(pool):
                            nc.gpsimd.memset(Qs[1][MROW:P].bitcast(FP32), 0.0).then_inc(rows_cleared, 1)
                            pool.wait_ge(rows_cleared, 1)
                            for b in (0, 1):
                                nc.gpsimd.tensor_copy(vg[:, b, :, :, 0:HD + 1],
                                                      vaug[:, :, bass.ds(i * (2 * GH) + b * GH, GH), :]).then_inc(vg_ready, 1)
                            pool.wait_ge(pv_done, u0[4])
                            pool.wait_ge(vg_ready, 2)
                            nc.gpsimd.memset(Qs[0][MROW:P].bitcast(FP32), 0.0).then_inc(rows_cleared, 1)

                        def keep_values(dve, k):
                            b, c = STEPS[k]
                            m = RING["turn values", k]
                            dve.wait_ge(ring_ready, m + 1)
                            o = ps[:, S + m % DEPTH, :].rearrange("p (t j m) -> p t j m", t=TPC, j=GH)
                            nc.vector.reciprocal(rec[:, k % 2], o[:, :, :, HD]).then_inc(keep_link, 1)
                            dve.wait_ge(keep_link, k + 1)
                            for t in range(TPC):
                                ins = nc.vector.tensor_tensor(
                                    ctxt[:, c * TPC + t, bass.ds(i * (2 * GH * HD) + b * GH * HD, GH * HD)].rearrange("p (j d) -> p j d", j=GH),
                                    o[:, t, :, 0:HD],
                                    rec[:, k % 2, t].rearrange("p (j a) -> p j a", a=1).to_broadcast([P, GH, HD]), ALU.mult)
                            ins.then_inc(ring_read, 1)

                        def split_maxima(dve, k):
                            c = STEPS[k][1]
                            m, r1 = negmax[:, 0], negmax[:, 1]
                            dve.wait_ge(ring_read, RING["max", m0[k + 1] - 1] + 1)
                            nc.vector.tensor_reduce(out=m, in_=mpart[:, :, :, 0:c + 1],
                                                    axis=AX.X, op=ALU.max, negate=True).then_inc(split_link, 1)
                            dve.wait_ge(split_link, 4 * k + 1)
                            if k >= 1:
                                dve.wait_ge(ring_ready, RING["turn max", k - 1] + 1)
                            nc.vector.tensor_copy(mparts[:, :, 0, :], m).then_inc(split_link, 1)
                            dve.wait_ge(split_link, 4 * k + 2)
                            nc.vector.tensor_tensor(r1, m, mparts[:, :, 0, :], ALU.subtract).then_inc(split_link, 1)
                            dve.wait_ge(split_link, 4 * k + 3)
                            nc.vector.tensor_copy(mparts[:, :, 1, :], r1).then_inc(split_link, 1)
                            dve.wait_ge(split_link, 4 * k + 4)
                            nc.vector.tensor_tensor(mparts[:, :, 2, :], r1, mparts[:, :, 1, :], ALU.subtract).then_inc(max_split, 1)

                        @block.vector
                        def _(dve):
                            for what, n, *_ in PLAN:
                                if what == "max":
                                    k, t, j, kc, width = MAXIMA[n]
                                    m = RING[what, n]
                                    dve.wait_ge(ring_ready, m + 1)
                                    nc.vector.tensor_reduce(out=mpart[:, j, t, kc:kc + 1], in_=ps[:, S + m % DEPTH, 0:width],
                                                            axis=AX.X, op=ALU.max).then_inc(ring_read, 1)
                                    if n + 1 == m0[k + 1]:
                                        split_maxima(dve, k)
                                if what == "turn max":
                                    m = RING[what, n]
                                    dve.wait_ge(ring_ready, m + 1)
                                    if n >= 1:
                                        dve.wait_ge(max_set, 16 * GH * n)
                                    nc.vector.tensor_copy(mrow[:], ps[:, S + m % DEPTH, 0:P // 2].bitcast(BF16)).then_inc(ring_read, 1)
                                if what == "turn values":
                                    keep_values(dve, n)

                        @block.tensor
                        def _(pe):
                            def free_bank(what, n):
                                m = RING[what, n]
                                if m >= DEPTH:
                                    pe.wait_ge(ring_read, m - DEPTH + 1)
                                return m

                            def scores_for_max(n):
                                k, t, j, kc, width = MAXIMA[n]
                                b, c = STEPS[k]
                                if n == m0[1]:
                                    pe.wait_ge(first_rest_loaded, 16 * LOADS_OF_GROUP)
                                if n == m0[4]:
                                    pe.wait_ge(ones_loaded[1], 16)
                                    pe.wait_ge(stack_loaded, 16 * LOADS_OF_GROUP)
                                    pe.wait_ge(rows_cleared, 1)
                                m = free_bank("max", n)
                                out = ps[:, S + m % DEPTH, 0:width]
                                ins = nc.tensor.matmul(out, Qs[b][:, j, (c * TPC + t) * P:(c * TPC + t + 1) * P],
                                                       Ks[b][:, j, kc * CH:kc * CH + width], start=True, stop=kc < c)
                                if kc == c:
                                    ins = nc.tensor.matmul(out[:, width - P:width], identb, qmask, start=False, stop=True)
                                ins.then_inc(ring_ready, 1)

                            def scores(u, j):
                                k, kt, off = UNIT[u]
                                b, c = STEPS[k]
                                if kt == 0 and j == 0:
                                    pe.wait_ge(max_set, 16 * GH * (k + 1))
                                if u >= 1:
                                    pe.wait_ge(exp_done, GH * (u - 1) + j + 1)
                                diagonal = kt >= c * TPC
                                ins = nc.tensor.matmul(ps[:, ST + j, off:CH], Ks[b][:, j, kt * P:(kt + 1) * P],
                                                       Qs[b][:, j, c * CH + off:(c + 1) * CH], start=True, stop=not diagonal)
                                if diagonal:
                                    ins = nc.tensor.matmul(ps[:, ST + j, off:off + P], identb, kmask, start=False, stop=True)
                                ins.then_inc(st_ready, 1)

                            def values(u):
                                k, kt, off = UNIT[u]
                                b = STEPS[k][0]
                                pe.wait_ge(exp_done, GH * (u + 1))
                                pe.wait_ge(vg_ready, b + 1)
                                if kt == 0 and k >= 1:
                                    pe.wait_ge(o_out, k)
                                for j in range(GH):
                                    ins = nc.tensor.matmul(ps[32 * j:32 * j + 32, O, off:CH], vg[:, b, kt, j, :],
                                                           probs[:, u % 2, j, off:CH], start=kt == 0, stop=kt == UNITS[k] - 1)
                                ins.then_inc(pv_done, 1)

                            for what, n, *j in PLAN:
                                if what == "max":
                                    scores_for_max(n)
                                if what == "scores":
                                    scores(n, j[0])
                                if what == "values":
                                    values(n)
                                if what == "turn max":
                                    pe.wait_ge(max_split, n + 1)
                                    m = free_bank(what, n)
                                    nc.tensor.transpose(ps[:, S + m % DEPTH, 0:P // 2].bitcast(BF16),
                                                        mwide[:].rearrange("p j m -> p (j m)"), identb).then_inc(ring_ready, 1)
                                if what == "turn values":
                                    pe.wait_ge(o_out, n + 1)
                                    m = free_bank(what, n)
                                    for t in range(TPC):
                                        ins = nc.tensor.transpose(ps[:, S + m % DEPTH, t * P:(t + 1) * P],
                                                                  osb[:, n % 2, t * P:(t + 1) * P], ident)
                                    ins.then_inc(ring_ready, 1)

                        @block.scalar
                        def _(act):
                            for what, n, *j in PLAN:
                                if what == "scores":
                                    k, kt, off = UNIT[n]
                                    if n >= 2 and j[0] == 0:
                                        act.wait_ge(pv_done, n - 1)
                                    act.wait_ge(st_ready, GH * n + j[0] + 1)
                                    nc.scalar.activation(probs[:, n % 2, j[0], off:CH], ps[:, ST + j[0], off:CH],
                                                         ACT.Exp).then_inc(exp_done, 1)
                                if what == "values":
                                    k = UNIT[n][0]
                                    if n + 1 == u0[k + 1]:
                                        act.wait_ge(pv_done, n + 1)
                                        if k >= 2:
                                            act.wait_ge(ring_ready, RING["turn values", k - 2] + 1)
                                        nc.scalar.copy(osb[:, k % 2, :], ps[:, O, :]).then_inc(o_out, 1)

                    with nc.Block() as block:
                        @block.gpsimd
                        def _(pool):
                            for s in body_sems:
                                pool.sem_clear(s)

                project_out("a_out", ctxt, w["wout"], None)

        def project_out(name, src, weight, source_norm):
            turned = sem(name + "_turned")
            copied = sem(name + "_copied")
            product = sem(name + "_product")
            added = sem(name + "_added")
            with nc.Block() as block:
                @block.sync
                def _(sp):
                    sp.dma_start(w1[:], io["w1"].rearrange("e h f -> h e f")).then_inc(moe_loaded, 16)
                    sp.dma_start(w3[:], io["w3"].rearrange("e h f -> h e f")).then_inc(moe_loaded, 16)
                    sp.dma_start(w2[:], io["w2"].rearrange("e (t f) h -> f e t h", f=P)).then_inc(moe_loaded, 16)

                @block.tensor
                def _(pe):
                    def turn(g):
                        if g >= 2:
                            pe.wait_ge(copied, g - 1)
                        for t in range(TPC):
                            ins = nc.tensor.transpose(ps[:, g % 2, t * P:(t + 1) * P], src[:, g * TPC + t, :], ident)
                        ins.then_inc(turned, 1)

                    turn(0)
                    turn(1)
                    for g in range(NC):
                        pe.wait_ge(copied, g + 1)
                        if g >= 2:
                            pe.wait_ge(added, g - 1)
                        for t in range(TPC):
                            ins = nc.tensor.matmul(ps[:, 2 + g % 2, t * P:(t + 1) * P],
                                                   xT[:, (g * TPC + t) * P:(g * TPC + t + 1) * P], weight[:], start=True, stop=True)
                        ins.then_inc(product, 1)
                        if g + 2 < NC:
                            turn(g + 2)

                @block.scalar
                def _(act):
                    for g in range(NC):
                        act.wait_ge(turned, g + 1)
                        nc.scalar.copy(xT[:, g * CH:(g + 1) * CH], ps[:, g % 2, :]).then_inc(copied, 1)

                @block.vector
                def _(dve):
                    for g in range(NC):
                        x_statistics(dve, added, g - 1)
                        dve.wait_ge(product, g + 1)
                        xs = x[:, g * TPC:(g + 1) * TPC, :].rearrange("p t d -> p (t d)")
                        nc.vector.tensor_tensor(xs, ps[:, 2 + g % 2, :], xs, ALU.add).then_inc(added, 1)
                    x_statistics(dve, added, NC - 1)

        def channel_mix(name):
            xr = arena[:, 0:T]
            xk = arena[:, T:2 * T]
            diff = arena[:, 2 * T:3 * T]
            rk = arena[:, 3 * T:4 * T]
            ka = arena[:, 4 * T:5 * T]
            r = arena[:, 5 * T:6 * T]
            rv = arena[:, 6 * T:7 * T]
            added = sem(name + "_added")
            norm = Norm(name, x, xn, NT, 1e-5)
            differed = sem(name + "_differed")
            mixed_r = sem(name + "_mixed_r")
            k_ready = sem(name + "_k_ready")
            k_relu = sem(name + "_k_relu")
            k_squared = sem(name + "_k_squared")
            r_ready = sem(name + "_r_ready")
            r_out = sem(name + "_r_out")
            v_ready = sem(name + "_v_ready")
            gated = sem(name + "_gated")
            with nc.Block() as block:
                @block.vector
                def _(dve):
                    norm.vector(dve)
                    for c in range(NC):
                        o = slice(c * CH, (c + 1) * CH)
                        dve.wait_ge(differed, c + 1)
                        nc.vector.scalar_tensor_tensor(out=xk[:, o], in0=diff[:, o], scalar=col["mu_k"], in1=xt[:, o],
                                                       op0=ALU.mult, op1=ALU.add)
                        nc.vector.scalar_tensor_tensor(out=xr[:, o], in0=diff[:, o], scalar=col["mu_r"], in1=xt[:, o],
                                                       op0=ALU.mult, op1=ALU.add).then_inc(mixed_r, 1)
                    for c in range(NC):
                        o = slice(c * CH, (c + 1) * CH)
                        x_statistics(dve, added, c - 1)
                        dve.wait_ge(v_ready, c + 1)
                        dve.wait_ge(r_out, c + 1)
                        nc.vector.tensor_tensor(rv[:, o], ps[:, 6 + c % 2, :], r[:, o], ALU.mult).then_inc(gated, 1)
                        dve.wait_ge(gated, c + 1)
                        xs = x[:, c * TPC:(c + 1) * TPC, :].rearrange("p t d -> p (t d)")
                        nc.vector.tensor_tensor(xs, rv[:, o], xs, ALU.add).then_inc(added, 1)
                    x_statistics(dve, added, NC - 1)

                @block.gpsimd
                def _(pool):
                    norm.gpsimd(pool)
                    for c in range(NC):
                        pool.wait_ge(norm.out, c + 1)
                        nc.gpsimd.tensor_tensor(diff[:, c * CH:(c + 1) * CH], xT[:, c * CH:(c + 1) * CH],
                                                xt[:, c * CH:(c + 1) * CH], ALU.subtract).then_inc(differed, 1)

                @block.scalar
                def _(act):
                    norm.scalar(act)
                    for c in range(NC):
                        o = slice(c * CH, (c + 1) * CH)
                        act.wait_ge(k_ready, c + 1)
                        nc.scalar.activation(rk[:, o], ps[:, 2 + c % 2, :], ACT.Relu).then_inc(k_relu, 1)
                        act.wait_ge(k_relu, c + 1)
                        nc.scalar.activation(ka[:, o], rk[:, o], ACT.Square).then_inc(k_squared, 1)
                        act.wait_ge(r_ready, c + 1)
                        nc.scalar.activation(r[:, o], ps[:, 4 + c % 2, :], ACT.Sigmoid).then_inc(r_out, 1)

                @block.tensor
                def _(pe):
                    norm.tensor(pe)

                    def value(c):
                        pe.wait_ge(k_squared, c + 1)
                        if c >= 2:
                            pe.wait_ge(gated, c - 1)
                        for t in range(TPC):
                            ins = nc.tensor.matmul(ps[:, 6 + c % 2, t * P:(t + 1) * P],
                                                   ka[:, c * CH + t * P:c * CH + (t + 1) * P], w["wv"][:], start=True, stop=True)
                        ins.then_inc(v_ready, 1)

                    for c in range(NC):
                        pe.wait_ge(mixed_r, c + 1)
                        if c >= 2:
                            pe.wait_ge(k_relu, c - 1)
                        nc.tensor.matmul(ps[:, 2 + c % 2, :], w["wk"][:], xk[:, c * CH:(c + 1) * CH],
                                         start=True, stop=True).then_inc(k_ready, 1)
                        if c >= 2:
                            pe.wait_ge(r_out, c - 1)
                        for t in range(TPC):
                            ins = nc.tensor.matmul(ps[:, 4 + c % 2, t * P:(t + 1) * P],
                                                   xr[:, c * CH + t * P:c * CH + (t + 1) * P], w["wr"][:], start=True, stop=True)
                        ins.then_inc(r_ready, 1)
                        if c >= 1:
                            value(c - 1)
                    value(NC - 1)

        def linear_attention(name, kind):
            wq, wk, wv = {"gated": ("hq", "hk", "hv"), "retention": ("rq", "rk", "rv"), "lightning": ("lq", "lk", "lv")}[kind]
            at = [0]

            def take(words):
                at[0] += words
                return arena[:, at[0] - words:at[0]]

            q = take(2 * CH).rearrange("p (b t) -> p b t", b=2)
            k = take(2 * CH).rearrange("p (b t) -> p b t", b=2)
            dec = take(2 * CH).rearrange("p (b t) -> p b t", b=2)
            vs = take(2 * CH).rearrange("p (b t) -> p b t", b=2)
            upd = take(2 * CH).rearrange("p (b t) -> p b t", b=2)
            SB, ZB = HD + 4, HD
            LAG = 4
            state = take(SB * CH).rearrange("p (b t) -> p b t", b=SB)
            z = take(ZB * CH).rearrange("p (b t) -> p b t", b=ZB)
            vrep = take(HD * P).rearrange("p (e h d) -> p e h d", e=HD, h=H)
            orep = take(HD * P).rearrange("p (e m) -> p e m", e=HD)
            y = take(T)
            gate = take(T)
            g1 = take(2 * CH)[0:HD, :].rearrange("p (b t) -> p b t", b=2)
            negb = take(1)
            VB = 4
            vd = take(VB * CH).rearrange("p (b t) -> p b t", b=VB)
            v_full = xn[:, 0:2 * TPC, :].rearrange("p (b t) d -> p b (t d)", b=2)
            v_dram = nc.dram_tensor(name + "_v", [NC, P, CH], FP32, kind="Internal").ap()
            by_dma = [n for n in range(NC * HD) if n >= HD and n % HD in (1, 3, 5, 6, 7)]
            by_pe = [n for n in range(NC * HD) if n not in by_dma]
            v_full_ready = sem(name + "_v_full_ready")
            v_full_out = sem(name + "_v_full_out")
            v_stored = sem(name + "_v_stored")
            v_loaded = [sem(f"{name}_v_loaded{b}") for b in range(VB)]
            norm = Norm(name, x, xn, NT, 1e-5)
            rep_ready = sem(name + "_rep_ready")
            negb_ready = sem(name + "_negb_ready")
            kq_ready = sem(name + "_kq_ready")
            kq_out = sem(name + "_kq_out")
            v_ready = sem(name + "_v_ready")
            v_out = sem(name + "_v_out")
            upd_ready = sem(name + "_upd_ready")
            scanned = sem(name + "_scanned")
            z_ready = sem(name + "_z_ready")
            z_used = sem(name + "_z_used")
            sum_out = sem(name + "_sum_out")
            x_added = sem(name + "_x_added")
            g_ready = sem(name + "_g_ready")
            g_out = sem(name + "_g_out")
            gate_ready = sem(name + "_gate_ready")
            gate_out = sem(name + "_gate_out")
            orep_loaded = sem(name + "_orep_loaded")
            if kind == "gated":
                reduce_w = orep
            else:
                reduce_w = pick
            with nc.Block() as block:
                @block.gpsimd
                def _(pool):
                    norm.gpsimd(pool)
                    wvT = w[wv][:].rearrange("p (h e) -> p h e", e=HD)
                    if kind == "gated":
                        nc.gpsimd.tensor_scalar(negb, col["key_b"], -1.0, None, ALU.mult).then_inc(negb_ready, 1)
                    for e in range(HD):
                        nc.gpsimd.tensor_copy(vrep[:, e], wvT[:, :, e:e + 1].to_broadcast([P, H, HD])).then_inc(rep_ready, 1)
                    for n in range(NC * HD):
                        c = n // HD
                        pool.wait_ge(scanned, n + 1)
                        pool.wait_ge(kq_out, 2 * c + 2)
                        if n >= ZB:
                            pool.wait_ge(z_used, n - ZB + 1)
                        nc.gpsimd.tensor_tensor(z[:, n % ZB, :], state[:, n % SB, :], q[:, c % 2, :], ALU.mult).then_inc(z_ready, 1)

                def add(dve, c):
                    x_statistics(dve, x_added, c - 1)
                    dve.wait_ge(z_used, (c + 1) * HD)
                    xs = x[:, c * TPC:(c + 1) * TPC, :]
                    nc.vector.tensor_tensor(xs, ps[:, 6 + c % 2, :].rearrange("p (t d) -> p t d", d=D), xs, ALU.add).then_inc(sum_out, 1)
                    dve.wait_ge(sum_out, c + 1)
                    nc.vector.tensor_tensor(xs, xs, out_bias[:].rearrange("p (a d) -> p a d", a=1).to_broadcast([P, TPC, D]),
                                            ALU.add).then_inc(x_added, 1)

                def y_statistics(dve, c):
                    dve.wait_ge(sum_out, c + 1)
                    if kind == "lightning":
                        statistics(range(c * TPC, (c + 1) * TPC), y.rearrange("p (t d) -> p t d", d=D))
                    else:
                        nc.vector.bn_stats(stats[:, c, :], y[:, c * CH:(c + 1) * CH])

                @block.vector
                def _(dve):
                    norm.vector(dve)

                    def update(n):
                        if n in by_dma:
                            m = by_dma.index(n)
                            dve.wait_ge(v_loaded[m % VB], 16 * (m // VB + 1))
                            v_in = vd[:, m % VB, :]
                        elif kind == "lightning":
                            m = by_pe.index(n)
                            dve.wait_ge(v_out, m + 1)
                            v_in = vs[:, m % 2, :]
                        else:
                            m = by_pe.index(n)
                            dve.wait_ge(v_ready, m + 1)
                            v_in = ps[:, 4 + m % 2, :]
                        dve.wait_ge(kq_out, 2 * (n // HD) + 1)
                        if n >= 2:
                            dve.wait_ge(scanned, n - 1)
                        nc.vector.tensor_tensor(upd[:, n % 2, :], v_in, k[:, n // HD % 2, :], ALU.mult).then_inc(upd_ready, 1)

                    update(0)
                    for n in range(NC * HD):
                        c = n // HD
                        if n + 1 < NC * HD:
                            update(n + 1)
                        dve.wait_ge(upd_ready, n + 1)
                        if n >= SB:
                            dve.wait_ge(z_ready, n - SB + 1)
                        if c >= 1:
                            dve.wait_ge(scanned, n - HD + 1)
                        a = dec[:, c % 2, :] if kind == "gated" else \
                            cst[:, C_RET if kind == "retention" else C_LT:][:, 0:1].to_broadcast([P, CH])
                        nc.vector.tensor_tensor_scan(
                            out=state[:, n % SB, :], data0=a, data1=upd[:, n % 2, :],
                            initial=0.0 if c == 0 else state[:, (n - HD) % SB, CH - 1:CH],
                            op0=ALU.mult, op1=ALU.add).then_inc(scanned, 1)
                        if kind == "gated" and c >= 1 and n % HD == LAG + 1:
                            add(dve, c - 1)
                        if kind != "gated" and c >= 1 and n % HD == LAG + 2:
                            y_statistics(dve, c - 1)
                    if kind == "gated":
                        add(dve, NC - 1)
                        x_statistics(dve, x_added, NC - 1)
                    if kind != "gated":
                        y_statistics(dve, NC - 1)

                def copy_out(act, c):
                    act.wait_ge(z_used, (c + 1) * HD)
                    nc.scalar.copy(y[:, c * CH:(c + 1) * CH], ps[:, 6 + c % 2, :]).then_inc(sum_out, 1)

                @block.scalar
                def _(act):
                    def take_kq(c):
                        act.wait_ge(kq_ready, 2 * c + 1)
                        if c >= 2:
                            act.wait_ge(z_ready, (c - 1) * HD)
                        pk = ps[:, 2, :]
                        if kind == "gated":
                            nc.scalar.activation(dec[:, c % 2, :], pk, ACT.Sigmoid, bias=col["key_b"])
                            if c == 0:
                                act.wait_ge(negb_ready, 1)
                            nc.scalar.activation(k[:, c % 2, :], pk, ACT.Sigmoid, bias=negb, scale=-1.0).then_inc(kq_out, 1)
                        elif kind == "retention":
                            nc.scalar.copy(k[:, c % 2, :], pk).then_inc(kq_out, 1)
                        else:
                            nc.scalar.activation(k[:, c % 2, :], pk, ACT.Silu).then_inc(kq_out, 1)
                        act.wait_ge(kq_ready, 2 * c + 2)
                        pq = ps[:, 3, :]
                        if kind == "gated":
                            nc.scalar.copy(q[:, c % 2, :], pq).then_inc(kq_out, 1)
                        elif kind == "retention":
                            nc.scalar.mul(q[:, c % 2, :], pq, float(HD) ** -0.5).then_inc(kq_out, 1)
                        else:
                            nc.scalar.activation(q[:, c % 2, :], pq, ACT.Silu).then_inc(kq_out, 1)

                    norm.scalar(act, (0, 1))
                    take_kq(0)
                    norm.scalar(act, (2, 3))
                    for n in range(NC * HD):
                        c, e = n // HD, n % HD
                        if kind == "lightning" and n in by_pe:
                            m = by_pe.index(n)
                            act.wait_ge(v_ready, m + 1)
                            if m >= 2:
                                act.wait_ge(upd_ready, by_pe[m - 2] + 1)
                            nc.scalar.activation(vs[:, m % 2, :], ps[:, 4 + m % 2, :], ACT.Silu).then_inc(v_out, 1)
                        if e == 1 and c + 1 < NC:
                            act.wait_ge(v_full_ready, c + 1)
                            if c >= 2:
                                act.wait_ge(v_stored, 16 * (c - 1))
                            nc.scalar.activation(v_full[:, c % 2, :], ps[:, 0, :],
                                                 ACT.Silu if kind == "lightning" else ACT.Copy).then_inc(v_full_out, 1)
                        if e == 2 and kind == "lightning":
                            act.wait_ge(g_ready, c + 1)
                            nc.scalar.copy(g1[:, c % 2, :], ps[0:HD, 1, :]).then_inc(g_out, 1)
                        if e == 3 and kind == "lightning":
                            act.wait_ge(gate_ready, c + 1)
                            nc.scalar.copy(gate[:, c * CH:(c + 1) * CH], ps[:, 1, :]).then_inc(gate_out, 1)
                        if e == LAG and c >= 1 and kind != "gated":
                            copy_out(act, c - 1)
                        if e == LAG + 1 and c + 1 < NC:
                            take_kq(c + 1)
                    if kind != "gated":
                        copy_out(act, NC - 1)

                @block.tensor
                def _(pe):
                    def project_kq(c):
                        o = slice(c * CH, (c + 1) * CH)
                        pe.wait_ge(norm.out, c + 1)
                        for j, weight in enumerate((wk, wq)):
                            if c >= 1:
                                pe.wait_ge(kq_out, 2 * c - 1 + j)
                            nc.tensor.matmul(ps[:, 2 + j, :], w[weight][:], xT[:, o], start=True, stop=True).then_inc(kq_ready, 1)

                    def add_product(n):
                        c, e = n // HD, n % HD
                        pe.wait_ge(z_ready, n + 1)
                        if kind == "gated" and n == 0:
                            pe.wait_ge(orep_loaded, 16 * HD)
                        if e == 0 and c >= 2:
                            pe.wait_ge(sum_out, c - 1)
                        if kind == "retention":
                            ins = nc.tensor.matmul(ps[:, 6 + c % 2, :], reduce_w[:, e, :], z[:, n % ZB, :],
                                                   start=e == 0, stop=e == HD - 1)
                        else:
                            for t in range(TPC):
                                ins = nc.tensor.matmul(ps[:, 6 + c % 2, t * P:(t + 1) * P], z[:, n % ZB, t * P:(t + 1) * P],
                                                       reduce_w[:, e, :], start=(e, t) == (0, 0), stop=(e, t) == (HD - 1, TPC - 1))
                        ins.then_inc(z_used, 1)

                    norm.tensor(pe, (0, 1))
                    project_kq(0)
                    norm.tensor(pe, (2, 3))
                    for n in range(NC * HD):
                        c, e = n // HD, n % HD
                        if n in by_pe:
                            m = by_pe.index(n)
                            if c == 0:
                                pe.wait_ge(rep_ready, e + 1)
                            if m >= 2 and kind == "lightning":
                                pe.wait_ge(v_out, m - 1)
                            if m >= 2 and kind != "lightning":
                                pe.wait_ge(upd_ready, by_pe[m - 2] + 1)
                            nc.tensor.matmul(ps[:, 4 + m % 2, :], vrep[:, e].rearrange("p h d -> p (h d)"),
                                             xT[:, c * CH:(c + 1) * CH], start=True, stop=True).then_inc(v_ready, 1)
                        if e == 1 and c + 1 < NC:
                            pe.wait_ge(norm.out, NC if c == 0 else c + 2)
                            if c >= 1:
                                pe.wait_ge(v_full_out, c)
                            nc.tensor.matmul(ps[:, 0, :], w[wv][:], xT[:, (c + 1) * CH:(c + 2) * CH],
                                             start=True, stop=True).then_inc(v_full_ready, 1)
                        if e == 2 and kind == "lightning":
                            pe.wait_ge(norm.out, NC)
                            if c >= 1:
                                pe.wait_ge(gate_out, c)
                            nc.tensor.matmul(ps[0:HD, 1, :], w["lg1"][:], xT[:, c * CH:(c + 1) * CH], start=True, stop=True).then_inc(g_ready, 1)
                        if e == 3 and kind == "lightning":
                            pe.wait_ge(g_out, c + 1)
                            nc.tensor.matmul(ps[:, 1, :], w["lg2"][:], g1[:, c % 2, :], start=True, stop=True).then_inc(gate_ready, 1)
                        if n >= LAG:
                            add_product(n - LAG)
                        if e == LAG + 1 and c + 1 < NC:
                            project_kq(c + 1)
                    for n in range(NC * HD - LAG, NC * HD):
                        add_product(n)

                @block.sync
                def _(sp):
                    if kind == "gated":
                        for e in range(HD):
                            sp.dma_start(orep[:, e, :], bass.AP(tensor=io["ho"].tensor, offset=e * D,
                                                                ap=[[HD * D, H], [0, HD], [1, D]])).then_inc(orep_loaded, 16)
                    for c in range(1, NC):
                        sp.wait_ge(v_full_out, c)
                        sp.dma_start(v_dram[c], v_full[:, (c - 1) % 2, :]).then_inc(v_stored, 16)
                        sp.wait_ge(v_stored, 16 * c)
                        for n in (n for n in by_dma if n // HD == c):
                            m = by_dma.index(n)
                            if m >= VB:
                                sp.wait_ge(upd_ready, by_dma[m - VB] + 1)
                            sp.dma_start(vd[:, m % VB, :], bass.AP(tensor=v_dram.tensor, offset=c * P * CH + n % HD * CH,
                                                                   ap=[[HD * CH, H], [0, HD], [1, CH]])).then_inc(v_loaded[m % VB], 16)

            if kind == "retention":
                retention_out(name, y, z)
            if kind == "lightning":
                lightning_out(name, y, gate)

        def retention_out(name, y, z):
            yn = z.rearrange("p b t -> p (b t)")[:, 0:T]
            st = stats[:, 0:NC, :]
            mv, dev, sc = small[:, 0, 0:2], small[:, 1, 0:3], small[:, 2, 0:8]
            link_sem = sem(name + "_gn_link")
            stat_ready = sem(name + "_gn_stat")
            scaled = sem(name + "_gn_scaled")
            head_mean_ready = sem(name + "_gn_mean")
            dev_ready = sem(name + "_gn_dev")
            head_var_ready = sem(name + "_gn_var")
            var_ready = sem(name + "_gn_vareps")
            rstd_ready = sem(name + "_gn_rstd")
            normed = sem(name + "_gn_normed")
            product = sem(name + "_gn_product")
            added = sem(name + "_gn_added")
            with nc.Block() as block:
                @block.vector
                def _(dve):
                    link = Chain(dve, link_sem)
                    nc.vector.bn_aggr(mv, st.rearrange("p c s -> p (c s)")).then_inc(stat_ready, 1)
                    dve.wait_ge(head_mean_ready, 1)
                    link(nc.vector.tensor_copy(sc[:, 0:1], ps[:, 0, 0:1]))
                    link(nc.vector.tensor_tensor(dev[:, 0:1], mv[:, 0:1], sc[:, 0:1], ALU.subtract))
                    link(nc.vector.tensor_tensor(dev[:, 1:2], dev[:, 0:1], dev[:, 0:1], ALU.mult))
                    nc.vector.tensor_tensor(dev[:, 2:3], dev[:, 1:2], mv[:, 1:2], ALU.add).then_inc(dev_ready, 1)
                    dve.wait_ge(head_var_ready, 1)
                    nc.vector.tensor_scalar(sc[:, 1:2], ps[:, 1, 0:1], 1e-5, None, ALU.add).then_inc(var_ready, 1)
                    dve.wait_ge(rstd_ready, 1)
                    link(nc.vector.tensor_tensor(sc[:, 3:4], sc[:, 2:3], col["gn_w"], ALU.mult))
                    for c in range(NC):
                        o = slice(c * CH, (c + 1) * CH)
                        nc.vector.tensor_scalar(yn[:, o], y[:, o], sc[:, 0:1], sc[:, 3:4], ALU.subtract, ALU.mult).then_inc(scaled, 1)
                    for c in range(NC):
                        x_statistics(dve, added, c - 1)
                        dve.wait_ge(product, c + 1)
                        xs = x[:, c * TPC:(c + 1) * TPC, :].rearrange("p t d -> p (t d)")
                        nc.vector.tensor_tensor(xs, ps[:, 2 + c % 2, :], xs, ALU.add).then_inc(added, 1)
                    x_statistics(dve, added, NC - 1)

                @block.scalar
                def _(act):
                    for c in range(NC):
                        o = slice(c * CH, (c + 1) * CH)
                        act.wait_ge(scaled, c + 1)
                        nc.scalar.activation(yn[:, o], yn[:, o], ACT.Identity, bias=col["gn_b"]).then_inc(normed, 1)

                @block.gpsimd
                def _(pool):
                    pool.wait_ge(var_ready, 1)
                    nc.gpsimd.tensor_tensor(sc[:, 2:3], sc[:, 1:2], neghalf[:, 0:1], ALU.pow).then_inc(rstd_ready, 1)

                @block.tensor
                def _(pe):
                    pe.wait_ge(stat_ready, 1)
                    nc.tensor.matmul(ps[:, 0, 0:1], head_mean, mv[:, 0:1], start=True, stop=True).then_inc(head_mean_ready, 1)
                    pe.wait_ge(dev_ready, 1)
                    nc.tensor.matmul(ps[:, 1, 0:1], head_mean, dev[:, 2:3], start=True, stop=True).then_inc(head_var_ready, 1)
                    for c in range(NC):
                        pe.wait_ge(normed, c + 1)
                        if c >= 2:
                            pe.wait_ge(added, c - 1)
                        for t in range(TPC):
                            ins = nc.tensor.matmul(ps[:, 2 + c % 2, t * P:(t + 1) * P],
                                                   yn[:, c * CH + t * P:c * CH + (t + 1) * P], w["ro"][:], start=True, stop=True)
                        ins.then_inc(product, 1)

        def lightning_out(name, y, gate):
            gate_ready = sem(name + "_gate_sigmoid")
            norm = Norm(name + "_o", y.rearrange("p (t d) -> p t d", d=D), xn, NT, 1e-5)
            gated = sem(name + "_gated")
            product = sem(name + "_product")
            added = sem(name + "_added")
            with nc.Block() as block:
                @block.vector
                def _(dve):
                    norm.vector(dve)
                    for c in range(NC):
                        o = slice(c * CH, (c + 1) * CH)
                        dve.wait_ge(norm.turned, c + 1)
                        nc.vector.tensor_scalar(xT[:, o], ps[:, c % 2, :], col["gamma"], col["beta"], ALU.mult, ALU.add).then_inc(norm.out, 1)
                    for c in range(NC):
                        x_statistics(dve, added, c - 1)
                        dve.wait_ge(product, c + 1)
                        xs = x[:, c * TPC:(c + 1) * TPC, :].rearrange("p t d -> p (t d)")
                        nc.vector.tensor_tensor(xs, ps[:, 2 + c % 2, :], xs, ALU.add).then_inc(added, 1)
                    x_statistics(dve, added, NC - 1)

                @block.scalar
                def _(act):
                    for c in range(NC):
                        o = slice(c * CH, (c + 1) * CH)
                        nc.scalar.activation(gate[:, o], gate[:, o], ACT.Sigmoid).then_inc(gate_ready, 1)

                @block.gpsimd
                def _(pool):
                    norm.gpsimd(pool)
                    for c in range(NC):
                        o = slice(c * CH, (c + 1) * CH)
                        pool.wait_ge(norm.out, c + 1)
                        pool.wait_ge(gate_ready, c + 1)
                        nc.gpsimd.tensor_tensor(xT[:, o], xT[:, o], gate[:, o], ALU.mult).then_inc(gated, 1)

                @block.tensor
                def _(pe):
                    norm.tensor(pe)
                    for c in range(NC):
                        pe.wait_ge(gated, c + 1)
                        if c >= 2:
                            pe.wait_ge(added, c - 1)
                        for t in range(TPC):
                            ins = nc.tensor.matmul(ps[:, 2 + c % 2, t * P:(t + 1) * P],
                                                   xT[:, c * CH + t * P:c * CH + (t + 1) * P], w["lo"][:], start=True, stop=True)
                        ins.then_inc(product, 1)

        def experts(name, slot_rows, result_rows, last):
            at = [0]

            def take(words):
                at[0] += words
                return arena[:, at[0] - words:at[0]]

            lg, l2, eq, oh1, oh2, ex, msk, t0, place = (take(NT * E).rearrange("p (t e) -> p t e", e=E) for _ in range(9))
            both = take(NT * E).rearrange("p (t e) -> p t e", e=E)
            m1, m2, mx, s1, s2 = (take(NT).rearrange("p (t a) -> p t a", a=1) for _ in range(5))
            carry, tot, upto = (take(NT * E).rearrange("p (e t) -> p e t", e=E) for _ in range(3))
            over = take(E * NT).rearrange("p (e t) -> p e t", e=E)
            tiles, tiles_upto, first_slot, ones8 = (take(E) for _ in range(4))
            before = take(P)
            ones = take(P)
            passed = take(ST * E).rearrange("p (s e) -> p s e", e=E)
            expert_f = take(ST)
            expert_of = take(ST).bitcast(U32)
            spot = take(TOP * NT).rearrange("p (k t) -> p k t", k=TOP)
            slot_of = take(TOP * NT).bitcast(U32).rearrange("p (k t) -> p k t", k=TOP)
            sent = take(TOP * NT * ROW).rearrange("p (k t c) -> p k t c", k=TOP, t=NT)
            xs = take(ST * ROW).rearrange("p (s c) -> p s c", c=ROW)
            xsT = take(2 * P).rearrange("p (b t) -> p b t", b=2)
            act_a = take(2 * F).rearrange("p (b f) -> p b f", b=2)
            hid = take(2 * F).rearrange("p (b f) -> p b f", b=2)
            hidT = take(2 * F).rearrange("p (b f t) -> p b f t", b=2, f=NF)
            YB = EARLY + 2
            y = take(YB * D).rearrange("p (b d) -> p b d", b=YB)
            back = take(TOP * NT * D).rearrange("p (k t d) -> p k t d", k=TOP, t=NT)
            takes = back.rearrange("p b t s -> p (b t s)").rearrange("p (b t s) -> p b t s", b=2, t=NT)
            near, apart, seat = take(NT), take(NT), take(NT)
            norm = Norm(name, x, sent[:, 0, :, 0:D], NT, 1e-5)
            LOADS_OF_SLOTS = [(EARLY, 7), (7, 11), (0, EARLY), (11, 15), (15, 27), (27, ST)]
            logits, link_sem, exp_in, exp_out, chosen, counted, sent_ready, slots_known = (sem(f"{name}_{n}") for n in (
                "logits", "link", "exp_in", "exp_out", "chosen", "counted", "sent_ready", "slots_known"))
            dispatched, x_turned, xsT_ready, up_ready, silu_out, hid_ready, hid_turned, hidT_ready, down_ready, y_ready = (
                sem(f"{name}_{n}") for n in ("dispatched", "x_turned", "xsT_ready", "up_ready", "silu_out", "hid_ready",
                                             "hid_turned", "hidT_ready", "down_ready", "y_ready"))
            slots_loaded = [sem(f"{name}_slots_loaded{i}") for i in range(len(LOADS_OF_SLOTS))]
            seat_link, takes_ready = sem(name + "_seat_link"), sem(name + "_takes_ready")
            y_stored = [sem(f"{name}_y_stored{i}") for i in range(YB)]
            y_back = [sem(f"{name}_y_back{g}") for g in range(NC)]
            x_stored = sem(name + "_x_stored")
            gate32 = take(P // NC)
            logitsT = take(CH)
            weights_ready, second_weighted = sem(name + "_weights_ready"), sem(name + "_second_weighted")
            gate_ready, logits_out = sem(name + "_gate_ready"), sem(name + "_logits_out")
            x_added = sem(name + "_x_added")

            with nc.Block() as block:
                @block.vector
                def _(dve):
                    nc.vector.memset(ones, 1.0)
                    nc.vector.memset(ones8, 1.0)
                    nc.vector.tensor_scalar(before, cst[:, C_QMASK:C_QMASK + P], 0.0, None, ALU.is_lt)
                    nc.vector.tensor_scalar(sent[:, :, :, D].bitcast(U32), count[:, 0:TOP * NT].rearrange("p (k t) -> p k t", k=TOP),
                                            float(P), row_number, ALU.mult, ALU.add)
                    nc.vector.tensor_scalar(carry, count[:, 0:NT].rearrange("p (a t) -> p a t", a=1).to_broadcast([P, E, NT]),
                                            0.0, None, ALU.is_gt)
                    norm.vector(dve)
                    link = Chain(dve, link_sem)

                    def wide(a):
                        return a.to_broadcast([P, NT, E])

                    def per_expert(a):
                        return a.rearrange("p (a e) -> p a e", a=1).to_broadcast([P, NT, E])

                    def first_max(src, m, onehot):
                        link(nc.vector.tensor_reduce(out=m[:, :, 0], in_=src, axis=AX.X, op=ALU.max))
                        link(nc.vector.tensor_tensor(eq, src, wide(m), ALU.is_equal))
                        link(nc.vector.tensor_tensor(eq, eq, per_expert(rank), ALU.mult))
                        link(nc.vector.tensor_reduce(out=mx[:, :, 0], in_=eq, axis=AX.X, op=ALU.max))
                        link(nc.vector.tensor_tensor(onehot, eq, wide(mx), ALU.is_equal))

                    def multiplier(k, src, m, s):
                        link(nc.vector.scalar_tensor_tensor(out=msk, in0=lg, scalar=-1.0, in1=lg, op0=ALU.mult, op1=ALU.max))
                        link(nc.vector.tensor_tensor(msk, msk, wide(m), ALU.max))
                        link(nc.vector.tensor_tensor(t0, wide(m), lg, ALU.subtract))
                        link(nc.vector.scalar_tensor_tensor(out=msk, in0=msk, scalar=0.02, in1=t0, op0=ALU.mult, op1=ALU.is_ge))
                        nc.vector.tensor_tensor(t0, src, wide(m), ALU.subtract).then_inc(exp_in, 1)
                        dve.wait_ge(exp_out, k)
                        link(nc.vector.tensor_tensor(ex, ex, msk, ALU.mult))
                        link(nc.vector.tensor_reduce(out=s[:, :, 0], in_=ex, axis=AX.X, op=ALU.add))
                        nc.vector.reciprocal(s, s).then_inc(weights_ready, 1)
                        dve.wait_ge(weights_ready, k)

                    dve.wait_ge(logits, 1)
                    nc.vector.tensor_copy(logitsT, ps[:, 2, :]).then_inc(logits_out, 1)
                    dve.wait_ge(logits, 2)
                    link(nc.vector.tensor_copy(lg.rearrange("p (c t) e -> p c t e", c=NC),
                                               ps[:, 3, :].rearrange("p (t c m) -> p c t m", t=TPC, c=NC)[:, :, :, 0:E]))
                    first_max(lg, m1, oh1)
                    link(nc.vector.scalar_tensor_tensor(out=l2, in0=oh1, scalar=NEG, in1=lg, op0=ALU.mult, op1=ALU.add))
                    first_max(l2, m2, oh2)
                    nc.vector.tensor_tensor(both, oh1, oh2, ALU.add).then_inc(chosen, 1)
                    dve.wait_ge(counted, 1)
                    link(nc.vector.tensor_copy(tot, ps[:, 3, NT * E:2 * NT * E].rearrange("p (t e) -> p e t", e=E)))
                    link(nc.vector.tensor_tensor_scan(upto.rearrange("p e t -> p (e t)"), carry.rearrange("p e t -> p (e t)"),
                                                      tot.rearrange("p e t -> p (e t)"), 0.0, ALU.mult, ALU.add))
                    link(nc.vector.scalar_tensor_tensor(
                        out=over, in0=count[:, 0:NT].rearrange("p (a t) -> p a t", a=1).to_broadcast([P, E, NT]), scalar=float(P),
                        in1=upto[:, :, NT - 1:NT].to_broadcast([P, E, NT]), op0=ALU.mult, op1=ALU.is_lt))
                    link(nc.vector.tensor_reduce(out=tiles, in_=over, axis=AX.X, op=ALU.add))
                    link(nc.vector.tensor_tensor_scan(tiles_upto, ones8, tiles, 0.0, ALU.mult, ALU.add))
                    link(nc.vector.tensor_tensor(first_slot, tiles_upto, tiles, ALU.subtract))
                    link(nc.vector.tensor_tensor(place, upto.rearrange("p e t -> p t e"), tot.rearrange("p e t -> p t e"), ALU.subtract))
                    link(nc.vector.scalar_tensor_tensor(out=place, in0=per_expert(first_slot), scalar=float(P), in1=place,
                                                        op0=ALU.mult, op1=ALU.add))
                    link(nc.vector.tensor_tensor(place, place, ps[:, 3, 0:NT * E].rearrange("p (t e) -> p t e", e=E), ALU.add))
                    link(nc.vector.tensor_tensor(t0, oh1, place, ALU.mult))
                    link(nc.vector.tensor_reduce(out=spot[:, 0, :], in_=t0, axis=AX.X, op=ALU.add))
                    link(nc.vector.tensor_tensor(t0, oh2, place, ALU.mult))
                    link(nc.vector.tensor_reduce(out=spot[:, 1, :], in_=t0, axis=AX.X, op=ALU.add))
                    nc.vector.tensor_copy(slot_of, spot).then_inc(slots_known, 1)

                    nc.vector.tensor_tensor(apart, spot[:, 0, :], spot[:, 1, :], ALU.subtract).then_inc(seat_link, 1)

                    def find_takers(s):
                        dve.wait_ge(seat_link, 3 * s + 1)
                        if s >= 1:
                            dve.wait_ge(takes_ready, 2 * s)
                        nc.vector.scalar_tensor_tensor(out=near, in0=spot[:, 0, :], scalar=float(s * P), in1=apart, op0=ALU.is_ge,
                                                       op1=ALU.mult).then_inc(seat_link, 1)
                        dve.wait_ge(seat_link, 3 * s + 2)
                        nc.vector.scalar_tensor_tensor(out=near, in0=spot[:, 0, :], scalar=float((s + 1) * P), in1=near, op0=ALU.is_lt,
                                                       op1=ALU.mult).then_inc(seat_link, 1)
                        dve.wait_ge(seat_link, 3 * s + 3)
                        nc.vector.scalar_tensor_tensor(out=seat, in0=spot[:, 1, :], scalar=-float(s * P), in1=near, op0=ALU.add,
                                                       op1=ALU.add).then_inc(seat_link, 1)
                        dve.wait_ge(seat_link, 3 * s + 4)
                        if s >= 2:
                            dve.wait_ge(x_turned, s - 1)
                        for half in (0, 1):
                            t = slice(half * NT // 2, (half + 1) * NT // 2)
                            nc.vector.tensor_tensor(takes[:, s % 2, t], count.rearrange("p (a s) -> p a s", a=1).to_broadcast([P, NT // 2, P]),
                                                    seat[:, t].rearrange("p (t a) -> p t a", a=1).to_broadcast([P, NT // 2, P]),
                                                    ALU.is_equal).then_inc(takes_ready, 1)

                    find_takers(0)
                    link(nc.vector.tensor_tensor(passed, count[:, 0:ST].rearrange("p (s a) -> p s a", a=1).to_broadcast([P, ST, E]),
                                                 tiles_upto.rearrange("p (a e) -> p a e", a=1).to_broadcast([P, ST, E]), ALU.is_ge))
                    link(nc.vector.tensor_reduce(out=expert_f, in_=passed, axis=AX.X, op=ALU.add))
                    nc.vector.tensor_scalar(expert_of, expert_f, float(E - 1), None, ALU.min).then_inc(slots_known, 1)
                    find_takers(1)

                    def take_turned(s):
                        dve.wait_ge(x_turned, s + 1)
                        if s >= 2:
                            dve.wait_ge(up_ready, s - 1)
                        nc.vector.tensor_copy(xsT[:, s % 2, :], ps[:, 6, 0:P]).then_inc(xsT_ready, 1)

                    take_turned(0)
                    for i in range(ST + 2):
                        if i + 2 < EARLY:
                            find_takers(i + 2)
                        if i + 1 < ST:
                            take_turned(i + 1)
                        if i < ST:
                            dve.wait_ge(silu_out, i + 1)
                            if i >= 2:
                                dve.wait_ge(hid_turned, i - 1)
                            nc.vector.tensor_tensor(hid[:, i % 2, :], ps[:, 2 + i % 2, :], act_a[:, i % 2, :],
                                                    ALU.mult).then_inc(hid_ready, 1)
                        s = i - 2
                        if s >= 0:
                            dve.wait_ge(down_ready, s + 1)
                            if s >= YB:
                                dve.wait_ge(y_stored[s % YB], 16 * (s // YB))
                            nc.vector.tensor_copy(y[:, s % YB, :], ps[:, 7, 0:D]).then_inc(y_ready, 1)
                    multiplier(1, lg, m1, s1)
                    multiplier(2, l2, m2, s2)
                    for g in range(NC):
                        dve.wait_ge(y_back[g], 16 * TOP)
                        chunk = slice(g * TPC, (g + 1) * TPC)
                        for t in range(g * TPC, (g + 1) * TPC):
                            ins = nc.vector.scalar_tensor_tensor(out=x[:, t, :], in0=back[:, 0, t, :], scalar=s1[:, t, :],
                                                                 in1=x[:, t, :], op0=ALU.mult, op1=ALU.add)
                        ins.then_inc(x_added, 1)
                        dve.wait_ge(x_added, 2 * g + 1)
                        dve.wait_ge(second_weighted, g + 1)
                        nc.vector.tensor_tensor(x[:, chunk, :], x[:, chunk, :], back[:, 1, chunk, :], ALU.add).then_inc(x_added, 1)
                        dve.wait_ge(x_added, 2 * g + 2)
                        if not last:
                            statistics(range(g * TPC, (g + 1) * TPC), x)

                @block.gpsimd
                def _(pool):
                    norm.gpsimd(pool)
                    nc.gpsimd.memset(gate32, 0.0).then_inc(gate_ready, 1)
                    pool.wait_ge(gate_ready, 1)
                    nc.gpsimd.tensor_copy(gate32[:, 0:E], w["gate"][:]).then_inc(gate_ready, 1)
                    pool.wait_ge(sent_ready, NC)
                    pool.wait_ge(slots_known, 1)
                    for t in range(NT):
                        for k in range(TOP):
                            nc.gpsimd.indirect_dma_start(
                                out=slot_rows, out_offset=bass.IndirectOffsetOnAxis(ap=slot_of[:, k, t:t + 1], axis=0),
                                in_=sent[:, k, t, :], in_offset=None).then_inc(dispatched, 16)
                    for s in range(ST):
                        for i, (a, b) in enumerate(LOADS_OF_SLOTS):
                            if s == a:
                                pool.wait_ge(slots_loaded[i], 16)
                        pool.wait_ge(y_ready, s + 1)
                        nc.gpsimd.indirect_dma_start(
                            out=result_rows, out_offset=bass.IndirectOffsetOnAxis(ap=xs[:, s, D:ROW].bitcast(U32), axis=0),
                            in_=y[:, s % YB, :], in_offset=None).then_inc(y_stored[s % YB], 16)

                @block.sync
                def _(sp):
                    sp.wait_ge(dispatched, 16 * TOP * NT)
                    for i, done in enumerate(slots_loaded):
                        a, b = LOADS_OF_SLOTS[i]
                        sp.dma_start(xs[:, a:b, :], slot_rows[a * P:b * P, :].rearrange("(s p) c -> p s c", p=P)).then_inc(done, 16)
                    for b in range(YB):
                        sp.wait_ge(y_stored[b], 16 * len(range(b, ST, YB)))
                    for g in range(NC):
                        for k in range(TOP):
                            r = k * T + g * CH
                            sp.dma_start(back[:, k, g * TPC:(g + 1) * TPC, :],
                                         result_rows[r:r + CH, :].rearrange("(t p) d -> p t d", p=P)).then_inc(y_back[g], 16)
                    if last:
                        for g in range(NC):
                            sp.wait_ge(x_added, 2 * (g + 1))
                            t = slice(g * TPC, (g + 1) * TPC)
                            sp.dma_start(io["out"].rearrange("a (t p) d -> p (a t) d", p=P)[:, t, :], x[:, t, :]).then_inc(x_stored, 16)
                        sp.wait_ge(x_stored, 16 * NC)

                @block.scalar
                def _(act):
                    norm.scalar(act)
                    for g in range(NC):
                        t = slice(g * TPC, (g + 1) * TPC)
                        nc.scalar.copy(sent[:, 1, t, 0:D], sent[:, 0, t, 0:D]).then_inc(sent_ready, 1)
                    for i in range(ST + 1):
                        if i < ST:
                            act.wait_ge(up_ready, i + 1)
                            if i >= 2:
                                act.wait_ge(hid_ready, i - 1)
                            nc.scalar.activation(act_a[:, i % 2, :], ps[:, i % 2, :], ACT.Silu).then_inc(silu_out, 1)
                        s = i - 1
                        if s >= 0:
                            act.wait_ge(hid_turned, s + 1)
                            if s >= 2:
                                act.wait_ge(down_ready, s - 1)
                            nc.scalar.copy(hidT[:, s % 2, :, :].rearrange("p f t -> p (f t)"), ps[:, 4 + s % 2, :]).then_inc(hidT_ready, 1)
                    for k in (1, 2):
                        act.wait_ge(exp_in, k)
                        nc.scalar.activation(ex, t0, ACT.Exp).then_inc(exp_out, 1)
                    act.wait_ge(weights_ready, 2)
                    for g in range(NC):
                        act.wait_ge(y_back[g], 16 * TOP)
                        for t in range(g * TPC, (g + 1) * TPC):
                            ins = nc.scalar.mul(back[:, 1, t, :], back[:, 1, t, :], s2[:, t, :])
                        ins.then_inc(second_weighted, 1)

                @block.tensor
                def _(pe):
                    norm.tensor(pe)
                    pe.wait_ge(gate_ready, 2)
                    for c in range(NC):
                        pe.wait_ge(norm.out, c + 1)
                        ins = nc.tensor.matmul(ps[c * 32:c * 32 + 32, 2, :], gate32, xT[:, c * CH:(c + 1) * CH], start=True, stop=True)
                    ins.then_inc(logits, 1)
                    pe.wait_ge(logits_out, 1)
                    for t in range(TPC):
                        ins = nc.tensor.transpose(ps[:, 3, t * P:(t + 1) * P], logitsT[:, t * P:(t + 1) * P], ident)
                    ins.then_inc(logits, 1)
                    pe.wait_ge(chosen, 1)
                    sel = both.rearrange("p t e -> p (t e)")
                    nc.tensor.matmul(ps[:, 3, 0:NT * E], before, sel, start=True, stop=True)
                    nc.tensor.matmul(ps[:, 3, NT * E:2 * NT * E], ones, sel, start=True, stop=True).then_inc(counted, 1)
                    pe.wait_ge(moe_loaded, 48)
                    pe.wait_ge(slots_known, 2)
                    expert = {}

                    def turn_x(s):
                        if s >= 1:
                            pe.wait_ge(xsT_ready, s)
                        if s < EARLY:
                            for t in range(NT):
                                if t % (NT // 2) == 0:
                                    pe.wait_ge(takes_ready, 2 * s + 1 + t // (NT // 2))
                                ins = nc.tensor.matmul(ps[:, 6, 0:P], sent[:, 0, t, 0:D], takes[:, s % 2, t, :],
                                                       start=t == 0, stop=t == NT - 1)
                            ins.then_inc(x_turned, 1)
                            return
                        for i, (a, b) in enumerate(LOADS_OF_SLOTS):
                            if s == a:
                                pe.wait_ge(slots_loaded[i], 16)
                        nc.tensor.transpose(ps[:, 6, 0:P], xs[:, s, 0:D], ident).then_inc(x_turned, 1)

                    turn_x(0)
                    for i in range(ST + 2):
                        if i < ST:
                            expert[i] = nc.tensor.value_load(expert_of[0:1, i:i + 1], min_val=0, max_val=E - 1)
                            pe.wait_ge(xsT_ready, i + 1)
                            if i >= 2:
                                pe.wait_ge(hid_ready, i - 1)
                            nc.tensor.matmul(ps[:, i % 2, :], xsT[:, i % 2, :], w1[:, expert[i], :], start=True, stop=True)
                            nc.tensor.matmul(ps[:, 2 + i % 2, :], xsT[:, i % 2, :], w3[:, expert[i], :],
                                             start=True, stop=True).then_inc(up_ready, 1)
                        s = i - 1
                        if 0 <= s < ST:
                            pe.wait_ge(hid_ready, s + 1)
                            if s >= 2:
                                pe.wait_ge(hidT_ready, s - 1)
                            for f in range(NF):
                                ins = nc.tensor.transpose(ps[:, 4 + s % 2, f * P:(f + 1) * P], hid[:, s % 2, f * P:(f + 1) * P], ident)
                            ins.then_inc(hid_turned, 1)
                        if i + 1 < ST:
                            turn_x(i + 1)
                        s = i - 2
                        if s >= 0:
                            pe.wait_ge(hidT_ready, s + 1)
                            if s >= 1:
                                pe.wait_ge(y_ready, s)
                            for f in range(NF):
                                ins = nc.tensor.matmul(ps[:, 7, 0:D], hidT[:, s % 2, f, :], w2[:, expert[s], f, :],
                                                       start=f == 0, stop=f == NF - 1)
                            ins.then_inc(down_ready, 1)

        softmax_attention()
        channel_mix("f0")
        linear_attention("g", "gated")
        channel_mix("f1")
        end_stage()
        linear_attention("r", "retention")
        experts("m0", slots[0], results[0], last=False)
        linear_attention("l", "lightning")
        end_stage()
        experts("m1", slots[1], results[1], last=True)


def constants():
    import numpy as np
    c = np.zeros((P, C_F32), np.float32)
    c[:, C_IDENT:C_IDENT + P] = np.eye(P)
    ch = np.arange(P)
    for e in range(HD):
        c[ch, C_PICK + e * P + ch // HD * HD + e] = 1.0
    c[:, C_HEAD:C_HEAD + P] = (ch[:, None] // HD == ch[None, :] // HD) / HD
    h = ch // HD
    c[:, C_RET] = 1.0 - 2.0 ** (-5.0 - h * (8.0 / H))
    start = 2.0 ** (-2.0 ** (-(np.log2(H) - 3)))
    slope = np.array([start * start ** i for i in range(H)], np.float32) * np.float32(1.0 + 1e-05)
    c[:, C_LT] = np.exp(-slope.astype(np.float64))[h]
    c[:, C_RANK:C_RANK + E] = E - np.arange(E)
    c[:, C_QMASK:C_QMASK + P] = np.where(ch[None, :] > ch[:, None], NEG, 0.0)
    c[:, C_KMASK:C_KMASK + P] = np.where(ch[:, None] > ch[None, :], NEG, 0.0)
    c[:, C_COUNT:C_PART] = np.arange(C_PART - C_COUNT)
    c[:, C_PART] = ch
    return c


def kernel(**inputs):
    import numpy as np
    import concourse.bacc as bacc
    from concourse.bass_utils import run_bass_kernel_spmd

    a = {k: np.asarray(v) for k, v in inputs.items()}
    vq = a["L0_attn_b_vq_w"]
    given = {
        "x": a["L0_attn_a_x"], "cst": constants(),
        "qkv": a["L0_attn_a_W_qkv"], "wout": a["L0_attn_a_W_out"],
        "wr": a["L0_ffn_W_r"].T, "wk": a["L0_ffn_W_k"].T, "wv": a["L0_ffn_W_v"].T,
        "hk": a["L0_attn_b_key_w"].T, "hv": vq[:D].T, "hq": vq[D:].T, "ho": a["L0_attn_b_out_w"].T,
        "rq": a["L1_attn_a_Wq"].T, "rk": a["L1_attn_a_Wk"].T, "rv": a["L1_attn_a_Wv"].T, "ro": a["L1_attn_a_Wo"].T,
        "lq": a["L1_attn_b_Wq"], "lk": a["L1_attn_b_Wk"], "lv": a["L1_attn_b_Wv"], "lo": a["L1_attn_b_Wo"],
        "lg1": a["L1_attn_b_Wg1"], "lg2": a["L1_attn_b_Wg2"], "gate": a["L1_ffn_gate_w"],
        "out_b": a["L0_attn_b_out_b"], "w1": a["L1_ffn_w1"], "w2": a["L1_ffn_w2"], "w3": a["L1_ffn_w3"],
        "q_scale": a["L0_attn_a_q_scale"], "k_scale": a["L0_attn_a_k_scale"], "key_b": a["L0_attn_b_key_b"],
        "mu_r": a["L0_ffn_mu_r"], "mu_k": a["L0_ffn_mu_k"], "gn_w": a["L1_attn_a_gn_w"], "gn_b": a["L1_attn_a_gn_b"],
        "gamma": a["L1_attn_b_gamma"], "beta": a["L1_attn_b_beta"],
    }
    nc = bacc.Bacc("TRN2", target_bir_lowering=False, num_devices=1)
    arrays, io = {}, {}
    for name, v in given.items():
        v = np.ascontiguousarray(v)
        arrays["in_" + name] = v
        io[name] = nc.dram_tensor("in_" + name, v.shape, mybir.dt.from_np(v.dtype), kind="ExternalInput").ap()
    io["out"] = nc.dram_tensor("out_x", (1, T, D), FP32, kind="ExternalOutput").ap()
    build(nc, io)
    r = run_bass_kernel_spmd(nc, [arrays], core_ids=[0])
    return r.results[0]["out_x"]
```
